# Optimizing a Trainium2 kernel written in Bass

```python
import numpy as np
import jax
import jax.numpy as jnp

def _softmax(x, axis=-1):
    return jax.nn.softmax(x, axis=axis)

def _gelu(x):
    return jax.nn.gelu(x, approximate=True)

def _silu(x):
    return jax.nn.silu(x)

def _sigmoid(x):
    return jax.nn.sigmoid(x)

def _layernorm(x, axis=-1, eps=1e-05):
    m = jnp.mean(x, axis=axis, keepdims=True)
    v = jnp.var(x, axis=axis, keepdims=True)
    return (x - m) / jnp.sqrt(v + eps)

def _scatter_add(tgt, idx, src, axis=0):
    return tgt.at[idx].add(src)

def _segment_sum(src, seg, n):
    return jax.ops.segment_sum(src, seg, n)
kernel_name = 'mk_xattn_ffn_d2_seqx_r4_bee8a3'

def setup_inputs(seed: int=0):
    np.random.seed(seed)
    _w = jnp.asarray

    def _rec_inputs():
        import jax
        import jax.numpy as jnp
        _rk = jax.random.key(seed)
        x = 6.313e-05 + 0.9998 * jax.random.normal(jax.random.fold_in(_rk, 1), (16, 256, 256), jnp.float32)
        _lenS = 256 - jax.random.randint(jax.random.fold_in(_rk, 7), (16,), 0, max(1, 256 // 4) + 1, jnp.int32)
        _lenS2 = 77 - jax.random.randint(jax.random.fold_in(_rk, 8), (16,), 0, max(1, 77 // 4) + 1, jnp.int32)
        _ctx_1024P = jax.random.normal(jax.random.fold_in(_rk, 11), (16, 16, 256), jnp.float32)
        _ctx_1024c = jax.random.dirichlet(jax.random.fold_in(_rk, 511), 0.3 * jnp.ones((16,), jnp.float32), (16, 77))
        _ctx_1024t = jnp.einsum('bsk,bkd->bsd', _ctx_1024c, _ctx_1024P)
        _ctx_1024t = _ctx_1024t * jax.lax.rsqrt(jnp.mean(jnp.square(_ctx_1024t)) + 1e-12) * 0.953939
        ctx_1024 = -0.000214406 + 1.00034 * (_ctx_1024t + 0.3 * jax.random.normal(jax.random.fold_in(_rk, 611), (16, 77, 256), jnp.float32))
        return (x, ctx_1024)
    x, ctx_1024 = _rec_inputs()

    def _L0_xattn_setup():
        import jax, jax.numpy as jnp
        import numpy as np
        from jax import lax
        BIG = jnp.float32(1e+30)

        def _pairwise_euclidean(a, b):
            aa = jnp.sum(a * a, axis=-1)[:, None]
            bb = jnp.sum(b * b, axis=-1)[None, :]
            ab = a @ b.T
            return jnp.sqrt(jnp.maximum(aa + bb - 2.0 * ab, 0.0))

        def _dtw_cost(D):
            row0 = jnp.cumsum(D[0])

            def row_step(prev_row, d_row):
                first = d_row[0] + prev_row[0]

                def col_step(left, inp):
                    d_ij, up, diag = inp
                    r = d_ij + jnp.minimum(jnp.minimum(up, left), diag)
                    return (r, r)
                _, rest = lax.scan(col_step, first, (d_row[1:], prev_row[1:], prev_row[:-1]))
                row = jnp.concatenate([first[None], rest])
                return (row, row)
            _, rows = lax.scan(row_step, row0, D[1:])
            return jnp.concatenate([row0[None], rows], axis=0)

        def _backtrack(R, T1, T2):
            L = T1 + T2 - 1

            def step(carry, _):
                i, j, done = carry
                valid = jnp.logical_not(done)
                cd = jnp.where((i > 0) & (j > 0), R[jnp.maximum(i - 1, 0), jnp.maximum(j - 1, 0)], BIG)
                cu = jnp.where(i > 0, R[jnp.maximum(i - 1, 0), j], BIG)
                cl = jnp.where(j > 0, R[i, jnp.maximum(j - 1, 0)], BIG)
                choice = jnp.argmin(jnp.stack([cd, cu, cl]))
                ni = jnp.where(choice <= 1, i - 1, i)
                nj = jnp.where((choice == 0) | (choice == 2), j - 1, j)
                at_origin = (i == 0) & (j == 0)
                ni = jnp.where(at_origin, 0, ni)
                nj = jnp.where(at_origin, 0, nj)
                return ((ni, nj, done | at_origin), (i, j, valid))
            init = (jnp.int32(T1 - 1), jnp.int32(T2 - 1), jnp.bool_(False))
            _, (i_idx, j_idx, valid) = lax.scan(step, init, None, length=L)
            return (i_idx, j_idx, valid)

        def _align_one(small, large):
            T_small, d = small.shape
            T_large = large.shape[0]
            D = _pairwise_euclidean(small, large)
            R = _dtw_cost(D)
            i_idx, j_idx, valid = _backtrack(R, T_small, T_large)
            contrib = small[i_idx] * valid[:, None].astype(small.dtype)
            expanded = jnp.zeros((T_large, d), dtype=small.dtype).at[j_idx].add(contrib)
            return expanded
        key = jax.random.key(seed)
        k1, k2 = jax.random.split(key)
        teacher = jax.random.normal(k1, (16, 100, 256), dtype=jnp.float32)
        student = jax.random.normal(k2, (16, 150, 256), dtype=jnp.float32)
        return {'teacher_features': teacher, 'student_features': student}
    _L0_xattn_all = _L0_xattn_setup()
    _L0_xattn_in = {k: v for k, v in _L0_xattn_all.items() if k in ()}
    del _L0_xattn_all

    def _L0_ffn_setup():
        import jax, jax.numpy as jnp
        import numpy as np
        DIM = 256
        E = 16
        TOPK = 2
        G = 4
        TOPK_G = 2
        INTER = 128
        N_SHARED = 2
        ROUTE_SCALE = 1.0

        def _gate(xf, gate_w, gate_b):
            scores = xf @ gate_w.T
            scores = jax.nn.softmax(scores.astype(jnp.float32), axis=-1)
            orig = scores
            scores = scores + gate_b
            T = xf.shape[0]
            sg = scores.reshape(T, G, E // G)
            group_scores = jax.lax.top_k(sg, 2)[0].sum(-1)
            _, gidx = jax.lax.top_k(group_scores, TOPK_G)
            keep = jax.nn.one_hot(gidx, G).sum(axis=1) > 0
            sg = jnp.where(keep[:, :, None], sg, -jnp.inf)
            scores = sg.reshape(T, E)
            _, idx = jax.lax.top_k(scores, TOPK)
            weights = jnp.take_along_axis(orig, idx, axis=1)
            weights = (weights * ROUTE_SCALE).astype(xf.dtype)
            return (weights, idx)
        key = jax.random.key(seed)
        ks = jax.random.split(key, 16)
        s = lambda fan_in: 1.0 / np.sqrt(fan_in)
        inp = {'x': jax.random.normal(ks[0], (4, 256, DIM), dtype=jnp.float32), 'gate_w': jax.random.normal(ks[1], (E, DIM), dtype=jnp.float32) * s(DIM), 'gate_b': jnp.zeros((E,), dtype=jnp.float32), 'We1': jax.random.normal(ks[2], (E, DIM, INTER), dtype=jnp.float32) * s(DIM), 'be1': jnp.zeros((E, INTER), dtype=jnp.float32), 'We2': jax.random.normal(ks[3], (E, INTER, DIM), dtype=jnp.float32) * s(INTER), 'be2': jnp.zeros((E, DIM), dtype=jnp.float32), 'We3': jax.random.normal(ks[4], (E, DIM, INTER), dtype=jnp.float32) * s(DIM), 'be3': jnp.zeros((E, INTER), dtype=jnp.float32), 'ws1': jax.random.normal(ks[5], (DIM, N_SHARED * INTER), dtype=jnp.float32) * s(DIM), 'bs1': jnp.zeros((N_SHARED * INTER,), dtype=jnp.float32), 'ws2': jax.random.normal(ks[6], (N_SHARED * INTER, DIM), dtype=jnp.float32) * s(N_SHARED * INTER), 'bs2': jnp.zeros((DIM,), dtype=jnp.float32), 'ws3': jax.random.normal(ks[7], (DIM, N_SHARED * INTER), dtype=jnp.float32) * s(DIM), 'bs3': jnp.zeros((N_SHARED * INTER,), dtype=jnp.float32)}
        return inp
    _L0_ffn_all = _L0_ffn_setup()
    _L0_ffn_in = {k: v for k, v in _L0_ffn_all.items() if k in ('gate_w', 'gate_b', 'We1', 'be1', 'We2', 'be2', 'We3', 'be3', 'ws1', 'bs1', 'ws2', 'bs2', 'ws3', 'bs3')}
    del _L0_ffn_all

    def _L1_xattn_setup():
        import jax, jax.numpy as jnp
        import numpy as np
        B, L_ENC, L_DEC, D = (16, 128, 128, 256)
        key = jax.random.key(seed)
        k1, k2, k3, k4, k5, k6 = jax.random.split(key, 6)
        encoder_hc = jax.random.normal(k1, (B, L_ENC, D), dtype=jnp.float32)
        decoder_hq = jax.random.normal(k2, (B, L_DEC, D), dtype=jnp.float32)
        w_sim = jax.random.normal(k3, (3 * D,), dtype=jnp.float32) * 0.02
        b_sim = jax.random.normal(k4, (1,), dtype=jnp.float32) * 0.02
        W_qv = jax.random.normal(k5, (4 * D, D), dtype=jnp.float32) * 0.02
        b_qv = jax.random.normal(k6, (D,), dtype=jnp.float32) * 0.02
        return {'encoder_hc': encoder_hc, 'decoder_hq': decoder_hq, 'w_sim': w_sim, 'b_sim': b_sim, 'W_qv': W_qv, 'b_qv': b_qv}
    _L1_xattn_all = _L1_xattn_setup()
    _L1_xattn_in = {k: v for k, v in _L1_xattn_all.items() if k in ('w_sim', 'b_sim', 'W_qv', 'b_qv')}
    del _L1_xattn_all

    def _L1_ffn_setup():
        import jax, jax.numpy as jnp
        import numpy as np
        E, D, F = (8, 256, 1024)
        B, S = (4, 512)

        def _layernorm(x, g, b, eps=1e-05):
            mu = jnp.mean(x, axis=-1, keepdims=True)
            var = jnp.var(x, axis=-1, keepdims=True)
            return (x - mu) * jax.lax.rsqrt(var + eps) * g + b
        key = jax.random.key(seed)
        ks = jax.random.split(key, 5)
        return {'input_features': jax.random.normal(ks[0], (B, S, D), jnp.float32), 'centroids': jax.random.normal(ks[1], (E, D), jnp.float32) * 0.1, 'ln_g': jnp.ones((E, D), jnp.float32), 'ln_b': jnp.zeros((E, D), jnp.float32), 'w1': jax.random.normal(ks[2], (E, F, D), jnp.float32) * (1.0 / np.sqrt(D).astype(np.float32)), 'b1': jnp.zeros((E, F), jnp.float32), 'w2': jax.random.normal(ks[3], (E, D, F), jnp.float32) * (1.0 / np.sqrt(F).astype(np.float32)), 'b2': jnp.zeros((E, D), jnp.float32)}
    _L1_ffn_all = _L1_ffn_setup()
    _L1_ffn_in = {k: v for k, v in _L1_ffn_all.items() if k in ('centroids', 'ln_g', 'ln_b', 'w1', 'b1', 'w2', 'b2')}
    del _L1_ffn_all
    return {'x': x, 'ctx_1024': ctx_1024, 'L0_ffn_gate_w': _L0_ffn_in['gate_w'], 'L0_ffn_gate_b': _L0_ffn_in['gate_b'], 'L0_ffn_We1': _L0_ffn_in['We1'], 'L0_ffn_be1': _L0_ffn_in['be1'], 'L0_ffn_We2': _L0_ffn_in['We2'], 'L0_ffn_be2': _L0_ffn_in['be2'], 'L0_ffn_We3': _L0_ffn_in['We3'], 'L0_ffn_be3': _L0_ffn_in['be3'], 'L0_ffn_ws1': _L0_ffn_in['ws1'], 'L0_ffn_bs1': _L0_ffn_in['bs1'], 'L0_ffn_ws2': _L0_ffn_in['ws2'], 'L0_ffn_bs2': _L0_ffn_in['bs2'], 'L0_ffn_ws3': _L0_ffn_in['ws3'], 'L0_ffn_bs3': _L0_ffn_in['bs3'], 'L1_xattn_w_sim': _L1_xattn_in['w_sim'], 'L1_xattn_b_sim': _L1_xattn_in['b_sim'], 'L1_xattn_W_qv': _L1_xattn_in['W_qv'], 'L1_xattn_b_qv': _L1_xattn_in['b_qv'], 'L1_ffn_centroids': _L1_ffn_in['centroids'], 'L1_ffn_ln_g': _L1_ffn_in['ln_g'], 'L1_ffn_ln_b': _L1_ffn_in['ln_b'], 'L1_ffn_w1': _L1_ffn_in['w1'], 'L1_ffn_b1': _L1_ffn_in['b1'], 'L1_ffn_w2': _L1_ffn_in['w2'], 'L1_ffn_b2': _L1_ffn_in['b2']}

def reference(x, ctx_1024, L0_ffn_gate_w, L0_ffn_gate_b, L0_ffn_We1, L0_ffn_be1, L0_ffn_We2, L0_ffn_be2, L0_ffn_We3, L0_ffn_be3, L0_ffn_ws1, L0_ffn_bs1, L0_ffn_ws2, L0_ffn_bs2, L0_ffn_ws3, L0_ffn_bs3, L1_xattn_w_sim, L1_xattn_b_sim, L1_xattn_W_qv, L1_xattn_b_qv, L1_ffn_centroids, L1_ffn_ln_g, L1_ffn_ln_b, L1_ffn_w1, L1_ffn_b1, L1_ffn_w2, L1_ffn_b2):
    import jax
    import jax.numpy as jnp

    def _L0_xattn_ref(teacher_features, student_features):
        import jax, jax.numpy as jnp
        import numpy as np
        from jax import lax
        BIG = jnp.float32(1e+30)

        def _pairwise_euclidean(a, b):
            aa = jnp.sum(a * a, axis=-1)[:, None]
            bb = jnp.sum(b * b, axis=-1)[None, :]
            ab = a @ b.T
            return jnp.sqrt(jnp.maximum(aa + bb - 2.0 * ab, 0.0))

        def _dtw_cost(D):
            row0 = jnp.cumsum(D[0])

            def row_step(prev_row, d_row):
                first = d_row[0] + prev_row[0]

                def col_step(left, inp):
                    d_ij, up, diag = inp
                    r = d_ij + jnp.minimum(jnp.minimum(up, left), diag)
                    return (r, r)
                _, rest = lax.scan(col_step, first, (d_row[1:], prev_row[1:], prev_row[:-1]))
                row = jnp.concatenate([first[None], rest])
                return (row, row)
            _, rows = lax.scan(row_step, row0, D[1:])
            return jnp.concatenate([row0[None], rows], axis=0)

        def _backtrack(R, T1, T2):
            L = T1 + T2 - 1

            def step(carry, _):
                i, j, done = carry
                valid = jnp.logical_not(done)
                cd = jnp.where((i > 0) & (j > 0), R[jnp.maximum(i - 1, 0), jnp.maximum(j - 1, 0)], BIG)
                cu = jnp.where(i > 0, R[jnp.maximum(i - 1, 0), j], BIG)
                cl = jnp.where(j > 0, R[i, jnp.maximum(j - 1, 0)], BIG)
                choice = jnp.argmin(jnp.stack([cd, cu, cl]))
                ni = jnp.where(choice <= 1, i - 1, i)
                nj = jnp.where((choice == 0) | (choice == 2), j - 1, j)
                at_origin = (i == 0) & (j == 0)
                ni = jnp.where(at_origin, 0, ni)
                nj = jnp.where(at_origin, 0, nj)
                return ((ni, nj, done | at_origin), (i, j, valid))
            init = (jnp.int32(T1 - 1), jnp.int32(T2 - 1), jnp.bool_(False))
            _, (i_idx, j_idx, valid) = lax.scan(step, init, None, length=L)
            return (i_idx, j_idx, valid)

        def _align_one(small, large):
            T_small, d = small.shape
            T_large = large.shape[0]
            D = _pairwise_euclidean(small, large)
            R = _dtw_cost(D)
            i_idx, j_idx, valid = _backtrack(R, T_small, T_large)
            contrib = small[i_idx] * valid[:, None].astype(small.dtype)
            expanded = jnp.zeros((T_large, d), dtype=small.dtype).at[j_idx].add(contrib)
            return expanded
        return jax.vmap(_align_one)(teacher_features, student_features)

    def _L0_ffn_ref(x, gate_w, gate_b, We1, be1, We2, be2, We3, be3, ws1, bs1, ws2, bs2, ws3, bs3):
        import jax, jax.numpy as jnp
        import numpy as np
        DIM = 256
        E = 16
        TOPK = 2
        G = 4
        TOPK_G = 2
        INTER = 128
        N_SHARED = 2
        ROUTE_SCALE = 1.0

        def _gate(xf, gate_w, gate_b):
            scores = xf @ gate_w.T
            scores = jax.nn.softmax(scores.astype(jnp.float32), axis=-1)
            orig = scores
            scores = scores + gate_b
            T = xf.shape[0]
            sg = scores.reshape(T, G, E // G)
            group_scores = jax.lax.top_k(sg, 2)[0].sum(-1)
            _, gidx = jax.lax.top_k(group_scores, TOPK_G)
            keep = jax.nn.one_hot(gidx, G).sum(axis=1) > 0
            sg = jnp.where(keep[:, :, None], sg, -jnp.inf)
            scores = sg.reshape(T, E)
            _, idx = jax.lax.top_k(scores, TOPK)
            weights = jnp.take_along_axis(orig, idx, axis=1)
            weights = (weights * ROUTE_SCALE).astype(xf.dtype)
            return (weights, idx)
        shape = x.shape
        xf = x.reshape(-1, DIM)
        weights, idx = _gate(xf, gate_w, gate_b)
        combine = (jax.nn.one_hot(idx, E, dtype=xf.dtype) * weights[..., None]).sum(1)
        h1 = jnp.einsum('td,edi->tei', xf, We1) + be1
        h3 = jnp.einsum('td,edi->tei', xf, We3) + be3
        h = jax.nn.silu(h1) * h3
        yo = jnp.einsum('tei,eid->ted', h, We2) + be2
        y = jnp.einsum('te,ted->td', combine, yo)
        z = jax.nn.silu(xf @ ws1 + bs1) * (xf @ ws3 + bs3) @ ws2 + bs2
        return (y + z).reshape(shape)

    def _L1_xattn_ref(encoder_hc, decoder_hq, w_sim, b_sim, W_qv, b_qv):
        import jax, jax.numpy as jnp
        import numpy as np
        B, L_ENC, L_DEC, D = (16, 128, 128, 256)
        d = encoder_hc.shape[-1]
        w1, w2, w3 = (w_sim[:d], w_sim[d:2 * d], w_sim[2 * d:])
        Sim = (encoder_hc @ w1)[:, :, None] + (decoder_hq @ w2)[:, None, :] + jnp.einsum('bid,bjd->bij', encoder_hc * w3, decoder_hq) + b_sim[0]
        A = jax.nn.softmax(Sim, axis=2)
        hq_hat = jnp.einsum('bij,bjd->bid', A, decoder_hq)
        Batt = jax.nn.softmax(jnp.max(Sim, axis=2), axis=1)
        hc_bar = jnp.einsum('bi,bid->bd', Batt, encoder_hc)[:, None, :]
        hc_hat = jnp.broadcast_to(hc_bar, encoder_hc.shape)
        feats = jnp.concatenate([encoder_hc, hq_hat, encoder_hc * hq_hat, encoder_hc * hc_hat], axis=-1)
        hcq = feats @ W_qv + b_qv
        return hcq

    def _L1_ffn_ref(input_features, centroids, ln_g, ln_b, w1, b1, w2, b2):
        import jax, jax.numpy as jnp
        import numpy as np
        E, D, F = (8, 256, 1024)
        B, S = (4, 512)

        def _layernorm(x, g, b, eps=1e-05):
            mu = jnp.mean(x, axis=-1, keepdims=True)
            var = jnp.var(x, axis=-1, keepdims=True)
            return (x - mu) * jax.lax.rsqrt(var + eps) * g + b
        Bf, Sf, Df = input_features.shape
        x = input_features.reshape(-1, Df)
        aff = x @ centroids.T
        assign = jnp.argmax(aff, axis=1)
        order = jnp.argsort(assign)
        xs = x[order]
        es = assign[order]
        alpha = jax.nn.sigmoid(jnp.take_along_axis(aff[order], es[:, None], axis=1))
        nE = centroids.shape[0]
        y = jnp.zeros_like(xs)
        for e in range(nE):
            h = _layernorm(xs, ln_g[e], ln_b[e])
            h = jax.nn.relu(h @ w1[e].T + b1[e])
            ye = xs + h @ w2[e].T + b2[e]
            y = y + jnp.where((es == e)[:, None], ye, 0.0)
        out_sorted = alpha * y + (1.0 - alpha) * xs
        inv = jnp.argsort(order)
        return out_sorted[inv].reshape(Bf, Sf, Df)
    x = x + _L0_xattn_ref(ctx_1024, _layernorm(x, axis=-1))
    x = x + _L0_ffn_ref(_layernorm(x, axis=-1), L0_ffn_gate_w, L0_ffn_gate_b, L0_ffn_We1, L0_ffn_be1, L0_ffn_We2, L0_ffn_be2, L0_ffn_We3, L0_ffn_be3, L0_ffn_ws1, L0_ffn_bs1, L0_ffn_ws2, L0_ffn_bs2, L0_ffn_ws3, L0_ffn_bs3)
    x = x + _L1_xattn_ref(_layernorm(x, axis=-1), ctx_1024, L1_xattn_w_sim, L1_xattn_b_sim, L1_xattn_W_qv, L1_xattn_b_qv)
    x = x + _L1_ffn_ref(_layernorm(x, axis=-1), L1_ffn_centroids, L1_ffn_ln_g, L1_ffn_ln_b, L1_ffn_w1, L1_ffn_b1, L1_ffn_w2, L1_ffn_b2)
    return x

_drawn_inputs = setup_inputs


def setup_inputs(seed=0):
    import zlib

    import numpy as np

    out = dict(_drawn_inputs(seed))
    spreads = {'L0_ffn_gate_b': (0.0, 0.1),
     'L0_ffn_be1': (0.0, 0.1),
     'L0_ffn_be2': (0.0, 0.1),
     'L0_ffn_be3': (0.0, 0.301),
     'L0_ffn_bs1': (0.0, 0.1),
     'L0_ffn_bs2': (0.0, 0.1),
     'L0_ffn_bs3': (0.0, 0.1),
     'L1_ffn_ln_g': (1.0, 0.2),
     'L1_ffn_ln_b': (0.0, 0.335),
     'L1_ffn_b1': (0.0, 0.327),
     'L1_ffn_b2': (0.0, 0.1)}
    factors = {}
    for name, (base, spread) in spreads.items():
        noise = np.random.default_rng([zlib.crc32(name.encode()), seed]).standard_normal(out[name].shape)
        drawn = base * np.exp(spread * noise) if base else spread * noise
        out[name] = jnp.asarray(drawn.astype(out[name].dtype))
    for name, factor in factors.items():
        out[name] = (out[name] * factor).astype(out[name].dtype)
    return out
```

```python
from contextlib import ExitStack

import numpy as np
import concourse.bass as bass
from concourse import mybir

ALU = mybir.AluOpType
ACT = mybir.ActivationFunctionType
AX = mybir.AxisListType
F32 = mybir.dt.float32
I32 = mybir.dt.int32
U32 = mybir.dt.uint32

P = 128
B, S, D = 16, 256, 256
C = 77
TOK = B * S
NT = TOK // P
TPB = S // P
KD = D // P
EPS = 1e-5
BIG = 1e30

LANES = 8
RPL = C // (LANES - 1)
WCOL = 64
NCOL = S // WCOL
STEPS = NCOL + LANES - 2
PADL = WCOL + 1
SKEW = PADL + STEPS * WCOL
assert RPL * (LANES - 1) == C

C_ID, C_TRI, C_ONE, C_IOTA = 0, 128, 256, 384
C_WIDE = C_IOTA + 256


def constants():
    c = np.zeros((P, C_WIDE), np.float32)
    c[:, C_ID:C_ID + P] = np.eye(P)
    c[:, C_TRI:C_TRI + P] = np.triu(np.ones((P, P)), 1)
    c[:, C_ONE:C_ONE + P] = 1.0
    c[:, C_IOTA:C_IOTA + 256] = np.arange(256)
    return c


def flat2b(ap):
    return ap.rearrange("p a b n -> p (a b) n")


def flat3(ap):
    return ap.rearrange("p a k n -> p (a k) n")


def flat2(ap):
    return ap.rearrange("p a n -> p (a n)")


E0, K0, I0 = 16, 2, 128
GRP = 4
U0 = 4
NTL0 = -(-((TOK * K0 + E0 * (P - 1)) // P) // U0) * U0


E1, F1 = 8, 1024
FB = F1 // P
U1 = 2
NTL1 = -(-((TOK + E1 * (P - 1)) // P) // 4) * 4


def pick_first_max(dve, chain, oh, top, v, rev, t3, t1, ne):
    def wide(ap):
        return ap.unsqueeze(2).to_broadcast([P, NT, ne])
    chain(dve.tensor_reduce(top, v, AX.X, ALU.max))
    chain(dve.tensor_tensor(t3, v, wide(top), ALU.is_ge))
    chain(dve.tensor_tensor(t3, t3, rev.unsqueeze(1).to_broadcast([P, NT, ne]), ALU.mult))
    chain(dve.tensor_reduce(t1, t3, AX.X, ALU.min))
    chain(dve.tensor_tensor(oh, rev.unsqueeze(1).to_broadcast([P, NT, ne]), wide(t1), ALU.is_equal))


def assign_slots(dve, chain, r, ohs, slots, etile, ne, ntl, rank_ps, tot_ps, cst, s_mask, s_rank):
    totE, cum, sst, cnt, ti, tl, tend, delta, red, cmp = (r[n] for n in (
        "totE", "cum", "sst", "cnt", "ti", "tl", "tend", "delta", "red", "cmp"))
    t3 = r["t3"]
    if len(ohs) == 2:
        chain(dve.tensor_tensor(r["mask"], ohs[0], ohs[1], ALU.add))
    dve.engine_nop().then_inc(s_mask, 1)
    dve.wait_ge(s_rank, 1)
    chain(dve.tensor_copy(totE.rearrange("p e t -> p t e"), tot_ps))
    flat, cumf = totE.rearrange("p e t -> p (e t)"), cum.rearrange("p e t -> p (e t)")
    chain(dve.tensor_tensor_scan(cumf, flat, flat, 0.0, ALU.add, ALU.max))
    chain(dve.memset(sst[:, 0:1], 0.0))
    chain(dve.tensor_copy(sst[:, 1:ne + 1], cum[:, :, NT - 1]))
    chain(dve.tensor_tensor(cnt, sst[:, 1:ne + 1], sst[:, 0:ne], ALU.subtract))
    chain(dve.tensor_scalar(ti, cnt, float(P - 1), None, ALU.add))
    chain(dve.tensor_scalar(ti, ti, 7, None, ALU.arith_shift_right))
    chain(dve.tensor_copy(tl, ti))
    chain(dve.tensor_tensor_scan(tend, tl, tl, 0.0, ALU.add, ALU.max))
    chain(dve.tensor_tensor(delta, tend, tl, ALU.subtract))
    chain(dve.scalar_tensor_tensor(delta, delta, float(P), sst[:, 0:ne], ALU.mult, ALU.subtract))
    chain(dve.tensor_tensor(cumf, cumf, flat, ALU.subtract))
    chain(dve.tensor_tensor(cum, cum, delta.unsqueeze(2).to_broadcast([P, ne, NT]), ALU.add))
    chain(dve.tensor_tensor(t3, rank_ps, cum.rearrange("p e t -> p t e"), ALU.add))
    for oh, slot in zip(ohs, slots):
        chain(dve.tensor_tensor(totE.rearrange("p e t -> p (e t)").rearrange("p (t e) -> p t e", e=ne), oh, t3, ALU.mult))
        chain(dve.tensor_reduce(red, totE.rearrange("p e t -> p (e t)").rearrange("p (t e) -> p t e", e=ne), AX.X, ALU.add))
        chain(dve.tensor_copy(slot, red))
    chain(dve.tensor_tensor(cmp, tend[0:1, :].unsqueeze(1).to_broadcast([1, ntl, ne]),
                            cst[0:1, C_IOTA:C_IOTA + ntl].unsqueeze(2).to_broadcast([1, ntl, ne]), ALU.is_le))
    chain(dve.tensor_reduce(r["tsum"], cmp, AX.X, ALU.add))
    chain(dve.tensor_scalar(etile, r["tsum"], float(ne - 1), None, ALU.min))


class Chain:

    def __init__(self, eng, sem, base=0):
        self.eng, self.sem, self.base, self.n = eng, sem, base, 0

    def __call__(self, ins):
        self.n += 1
        ins.then_inc(self.sem, 1)
        self.eng.wait_ge(self.sem, self.base + self.n)


def program(nc, a, out, dbg=None):
    with ExitStack() as top:
        build(nc, top, a, out)


def build(nc, top, a, out):
    def sb(ctx, name, shape, dt=F32):
        return ctx.enter_context(nc.sbuf_tensor(name, shape, dt))

    def pb(ctx, name, shape, dt=F32):
        return ctx.enter_context(nc.psum_tensor(name, shape, dt))

    def sem(name):
        return top.enter_context(nc.semaphore(name))

    cst = sb(top, "cst", [P, C_WIDE])
    ident = cst[:, C_ID:C_ID + P]
    xres = sb(top, "xres", [P, NT, D])
    mv = sb(top, "mv", [P, NT, 2])
    rstd = sb(top, "rstd", [P, NT])
    nmr = sb(top, "nmr", [P, NT])
    st6 = sb(top, "st6", [P, NT, 6])
    lnt = sb(top, "lnt", [P, 3, NT])
    s_cst = sem("s_cst")

    x_tok = a["x"].rearrange("b s d -> (b s) d").rearrange("(t p) d -> p t d", p=P)
    out_tok = out.rearrange("b s d -> (b s) d").rearrange("(t p) d -> p t d", p=P)

    def stats_loop(dve, load_sems, s_st):
        per = 8
        if load_sems is None:
            with dve.Fori(0, NT // per) as c:
                for u in range(per):
                    t = c * per + u
                    dve.bn_stats(st6[:, bass.ds(t, 1), :].rearrange("p a s -> p (a s)"),
                                 xres[:, bass.ds(t, 1), :].rearrange("p a d -> p (a d)")).then_inc(s_st, 1)
        else:
            for c in range(NT // per):
                dve.wait_ge(load_sems[c], 16)
                for u in range(per):
                    dve.bn_stats(st6[:, c * per + u, :], xres[:, c * per + u, :]).then_inc(s_st, 1)
        dve.wait_ge(s_st, NT)
        for t in range(NT):
            dve.bn_aggr(mv[:, t, :], st6[:, t, :]).then_inc(s_st, 1)
        dve.wait_ge(s_st, 2 * NT)

    def norm_tile(dve, dst, t):
        return dve.tensor_scalar(dst, flat2(xres[:, bass.ds(t, 1), :]), rstd[:, bass.ds(t, 1)], nmr[:, bass.ds(t, 1)],
                                 ALU.mult, ALU.add)

    def rstd_steps(dve, chain, s_var, s_root):
        ve, t0, t1 = lnt[:, 0, :], lnt[:, 1, :], lnt[:, 2, :]
        dve.tensor_scalar(ve, mv[:, :, 1], EPS, None, ALU.add).then_inc(s_var, 1)
        dve.wait_ge(s_root, 1)
        chain(dve.reciprocal(t1, t0))
        chain(dve.tensor_tensor(t1, ve, t1, ALU.mult))
        chain(dve.tensor_tensor(t1, t1, t0, ALU.add))
        chain(dve.tensor_scalar(t1, t1, 0.5, None, ALU.mult))
        chain(dve.reciprocal(rstd[:, :], t1))
        chain(dve.scalar_tensor_tensor(nmr[:, :], mv[:, :, 0], -1.0, rstd[:, :], ALU.mult, ALU.mult))

    xs0 = nc.dram_tensor("xs0", [NTL0 * P, D], F32).ap()
    ys0 = nc.dram_tensor("ys0", [NTL0 * P, D], F32).ap()
    xs1 = nc.dram_tensor("xs1", [NTL1 * P, D], F32).ap()
    ys1 = nc.dram_tensor("ys1", [NTL1 * P, D], F32).ap()
    s_zero = sem("s_zero")
    zbuf = sb(top, "zbuf", [P, 1024])
    s_zb = sem("s_zb")
    n_zero = (NTL0 + NTL1) * D // 1024

    def zero_fill(sp):
        sp.wait_ge(s_zb, 1)
        for rows in (xs0, xs1):
            v = rows.rearrange("(p r) d -> p (r d)", p=P)
            for c in range(v.shape[1] // 1024):
                sp.dma_start(v[:, c * 1024:(c + 1) * 1024], zbuf[:, :]).then_inc(s_zero, 16)

    with ExitStack() as warp_sems:
        old_sems = []

        def warp_sem(name):
            old_sems.append(warp_sems.enter_context(nc.semaphore(name)))
            return old_sems[-1]

        phase_warp(nc, a, out_tok, locals())
        phase_moe0(nc, a, out_tok, locals())
    with ExitStack() as late:
        l1_w1 = sb(late, "l1_w1", [P, KD, E1, F1])
        s_w1 = sem("s_w1")
        phase_xattn(nc, a, out_tok, locals())
        phase_moe1(nc, a, out_tok, locals())


def phase_warp(nc, a, out_tok, k):
    sb, pb, sem = k["sb"], k["pb"], k["warp_sem"]
    cst, ident, xres, rstd, nmr, lnt = (k[n] for n in ("cst", "ident", "xres", "rstd", "nmr", "lnt"))
    x_tok, s_cst = k["x_tok"], k["s_cst"]
    with ExitStack() as ctx:
        ctx_sb = sb(ctx, "ctx_sb", [C, B, D])
        DSK = RPL * STEPS * WCOL
        RSK = (RPL + 1) * SKEW
        CH = (LANES - 1) * RPL * S
        arena = sb(ctx, "w_arena", [P, max(DSK + RSK, CH)])
        dskew = arena[:, 0:DSK].rearrange("p (r w) -> p r w", r=RPL)
        rskew = arena[:, DSK:DSK + RSK].rearrange("p (r w) -> p r w", r=RPL + 1)
        chain_tab = arena[0:B, 0:CH].rearrange("p (r w) -> p r w", w=S)
        rrow = sb(ctx, "w_rrow", [P, RPL + 1, S + 1])
        up = sb(ctx, "w_up", [P, RPL, S])
        gv = sb(ctx, "w_gv", [P, RPL, S])
        jr = sb(ctx, "w_jr", [P, RPL, S])
        junk = sb(ctx, "w_junk", [B, S])
        c2 = sb(ctx, "w_c2", [B, C + 1])
        cs = sb(ctx, "w_cs", [C, 2, B])
        minw = sb(ctx, "w_min", [P, WCOL])
        aa = sb(ctx, "w_aa", [C, B])
        iota15 = sb(ctx, "w_iota15", [C, S])
        iota2 = sb(ctx, "w_iota2", [C, S])
        halfneg = sb(ctx, "w_halfneg", [P, C])
        xn = [sb(ctx, f"w_xn{u}", [P, TPB, D]) for u in range(2)]
        xT = [sb(ctx, f"w_xT{u}", [P, KD, S]) for u in range(2)]
        xsq = [sb(ctx, f"w_xsq{u}", [P, KD, S]) for u in range(2)]
        cT = [sb(ctx, f"w_cT{u}", [P, KD, C]) for u in range(2)]
        d2 = [sb(ctx, f"w_d2{u}", [C, S]) for u in range(2)]
        y0 = [sb(ctx, f"w_y0{u}", [C, S]) for u in range(2)]
        ysq = [sb(ctx, f"w_ysq{u}", [C, S]) for u in range(2)]
        ri = [sb(ctx, f"w_ri{u}", [C, S]) for u in range(2)]
        path = [sb(ctx, f"w_path{u}", [C, S]) for u in range(2)]
        pm = [sb(ctx, f"w_pm{u}", [C, S]) for u in range(2)]
        tpx = [pb(ctx, f"w_tpx{u}", [P, KD, S]) for u in range(2)]
        tpc = [pb(ctx, f"w_tpc{u}", [P, KD, S]) for u in range(2)]
        dps = [pb(ctx, f"w_dps{u}", [P, 2 * S]) for u in range(2)]
        xps = tpx
        dscr = nc.dram_tensor("dscr", [B, C, S], F32).ap()

        x_in = [sem(f"w_x_in{c}") for c in range(4)]
        c_in = sem("w_c_in")
        s_st, s_var, s_root, s_dve = sem("w_st"), sem("w_var"), sem("w_root"), sem("w_dve")
        s_init = sem("w_init")
        s_ln, s_xnp, s_tp, s_xT, s_sq, s_dd, s_d2 = (sem("w_" + n) for n in ("ln", "xn", "tp", "xT", "sq", "dd", "d2"))
        s_y0, s_ysq, s_res, s_ri, s_cor, s_y = (sem("w_" + n) for n in ("y0", "ysq", "res", "ri", "cor", "y"))
        s_aa, s_cT, s_ctp, s_cTs = sem("w_aa_s"), sem("w_cT_s"), sem("w_ctp"), sem("w_cTs")
        d_out = [sem(f"w_d_out{u}") for u in range(2)]
        d_in, s_dp, s_dpm, r_un, s_g, t_in, s_c2, s_c2t, s_cs = (
            sem("w_" + n) for n in ("d_in", "dp", "dpm", "r_un", "g", "t_in", "c2_s", "c2t", "cs_s"))
        s_pm, s_path, s_ex, s_add, s_dmp, s_gch, s_bt = (sem("w_" + n) for n in ("pm_s", "path_s", "ex", "add", "dmp", "gch", "bt"))
        s_corner = k["sem"]("w_corner")

        block = ctx.enter_context(nc.Block())

        @block.sync
        def _(sp):
            for u in range(2):
                sp.sem_inc(d_out[u], 16)
            sp.dma_start(cst[:, :], a["cst"]).then_inc(s_cst, 16)
            for c in range(4):
                sp.dma_start(xres[:, 8 * c:8 * c + 8, :], x_tok[:, 8 * c:8 * c + 8, :]).then_inc(x_in[c], 16)
            k["zero_fill"](sp)
            sp.dma_start(ctx_sb[:, :, :], a["ctx_1024"].rearrange("b i d -> i b d")).then_inc(c_in, 16)
            with sp.Fori(0, B // 2) as h:
                for u in range(2):
                    sp.wait_ge(s_y, h * 2 + u + 1)
                    sp.dma_start(dscr[bass.ds(h * 2 + u, 1), :, :].rearrange("a i j -> (a i) j"),
                                 ysq[u][:, :]).then_inc(d_out[u], 16)
            for u in range(2):
                sp.wait_ge(d_out[u], 16 * (B // 2 + 1))
            sp.wait_ge(s_init, 2)
            for lane in range(1, LANES):
                sp.dma_start(dskew[lane::LANES, :, WCOL * (lane - 1):WCOL * (lane - 1) + S],
                             dscr[:, RPL * (lane - 1):RPL * lane, :]).then_inc(d_in, 16)
            sp.wait_ge(s_dp, STEPS * (2 * RPL + 1))
            for lane in range(LANES):
                o = PADL - 1 + WCOL * max(lane - 1, 0)
                sp.dma_start(rrow[lane::LANES, :, :], rskew[lane::LANES, :, o:o + S + 1]).then_inc(r_un, 16)
            sp.wait_ge(s_gch, 8)
            for lane in range(LANES - 1, 0, -1):
                sp.dma_start(chain_tab[:, RPL * (lane - 1):RPL * lane, :], gv[lane::LANES, :, :]).then_inc(t_in, 16)

        @block.gpsimd
        def _(pool):
            pool.memset(k["zbuf"][:, :], 0.0).then_inc(k["s_zb"], 1)
            pool.memset(dskew, BIG).then_inc(s_init, 1)
            pool.memset(rskew, BIG).then_inc(s_init, 1)
            pool.iota(jr[:, :, :], pattern=[[512, RPL], [1, S]], base=1, channel_multiplier=0,
                      allow_small_or_imprecise_dtypes=True).then_inc(s_dmp, 1)
            pool.wait_ge(s_init, 2)
            pool.dma_start(rskew[1::LANES, 0, PADL - 1:PADL], a["zeros"][0:B, :]).then_inc(s_corner, 16)
            with pool.Fori(0, B // 2) as h:
                for u in range(2):
                    pool.wait_ge(s_xT, h * 2 + u + 1)
                    pool.tensor_tensor(xsq[u][:, :, :], xT[u][:, :, :], xT[u][:, :, :], ALU.mult).then_inc(s_sq, 1)
                for u in range(2):
                    pool.wait_ge(s_ysq, h * 2 + u + 1)
                    pool.tensor_tensor(d2[u][:, :], d2[u][:, :], ysq[u][:, :], ALU.subtract).then_inc(s_res, 1)
                for u in range(2):
                    pool.wait_ge(s_cor, h * 2 + u + 1)
                    pool.tensor_tensor(ysq[u][:, :], y0[u][:, :], d2[u][:, :], ALU.add).then_inc(s_y, 1)

        @block.scalar
        def _(act):
            act.wait_ge(c_in, 16)
            for b in range(B):
                if b >= 2:
                    act.wait_ge(s_aa, b - 1)
                act.activation(ysq[b % 2][:, :], ctx_sb[:, b, :], ACT.Square, accum_out=aa[:, b:b + 1]).then_inc(s_aa, 1)
            act.wait_ge(s_var, 1)
            act.activation(lnt[:, 1, :], lnt[:, 0, :], ACT.Sqrt).then_inc(s_root, 1)
            act.wait_ge(s_aa, B)
            with act.Fori(0, B // 2) as h:
                for u in range(2):
                    b = h * 2 + u
                    act.wait_ge(s_dd, b + 1)
                    act.activation(d2[u][:, :], dps[u][0:C, 0:S], ACT.Relu, bias=aa[:, bass.ds(b, 1)],
                                   scale=-2.0).then_inc(s_d2, 1)
                for u in range(2):
                    b = h * 2 + u
                    act.wait_ge(s_d2, b + 1)
                    act.activation(y0[u][:, :], d2[u][:, :], ACT.Sqrt).then_inc(s_y0, 1)
                for u in range(2):
                    b = h * 2 + u
                    act.wait_ge(s_y0, b + 1)
                    act.wait_ge(d_out[u], h * 16 + 16)
                    act.activation(ysq[u][:, :], y0[u][:, :], ACT.Square).then_inc(s_ysq, 1)

        @block.tensor
        def _(pe):
            pe.wait_ge(s_cst, 16)
            pe.wait_ge(c_in, 16)

            def transposes(b, u):
                for i in range(TPB):
                    for kb in range(KD):
                        ins = pe.transpose(tpx[u][:, kb, i * P:(i + 1) * P], xn[u][:, i, kb * P:(kb + 1) * P], ident)
                ins.then_inc(s_tp, 1)
            pe.wait_ge(s_bt, 1)
            with pe.Fori(0, B // 2) as h:
                for u in range(2):
                    b = h * 2 + u
                    pe.wait_ge(s_xnp, b + 1)
                    transposes(b, u)
                    pe.wait_ge(s_ctp, b + 1)
                    for kb in range(KD):
                        ins = pe.transpose(tpc[u][:, kb, 0:C], path[u][:, kb * P:(kb + 1) * P], ident[0:C, 0:C])
                    ins.then_inc(s_cT, 1)
                for u in range(2):
                    b = h * 2 + u
                    pe.wait_ge(s_cTs, b + 1)
                    for kb in range(KD):
                        pe.matmul(dps[u][0:C, 0:S], cT[u][:, kb, :], xT[u][:, kb, :], start=(kb == 0), stop=False)
                    pe.wait_ge(s_sq, b + 1)
                    for kb in range(KD):
                        ins = pe.matmul(dps[u][0:C, 0:S], halfneg[:, :], xsq[u][:, kb, :], start=False, stop=(kb == KD - 1))
                    ins.then_inc(s_dd, 1)
            pe.wait_ge(s_c2, 1)
            pe.transpose(tpx[0][0:C, 0, 0:B], c2[:, 0:C], ident[0:B, 0:B])
            pe.transpose(tpx[0][0:C, 0, B:2 * B], c2[:, 1:C + 1], ident[0:B, 0:B]).then_inc(s_c2t, 1)
            with pe.Fori(0, B // 2) as h:
                for u in range(2):
                    b = h * 2 + u
                    pe.wait_ge(s_path, b + 1)
                    for i in range(TPB):
                        ins = pe.matmul(xps[u][:, i, :], path[u][:, i * P:(i + 1) * P],
                                        ctx_sb[:, bass.ds(b, 1), :].rearrange("p a d -> p (a d)"), start=True, stop=True)
                    ins.then_inc(s_ex, 1)

        @block.vector
        def _(dve):
            dve.memset(halfneg[:, :], -0.5).then_inc(s_bt, 1)
            chain = Chain(dve, s_dve)
            dve.wait_ge(s_cst, 16)
            dve.tensor_scalar(iota15[:, :], cst[0:C, C_IOTA:C_IOTA + S], 1.5, None, ALU.add).then_inc(s_bt, 1)
            dve.tensor_scalar(iota2[:, :], cst[0:C, C_IOTA:C_IOTA + S], 2.0, None, ALU.add).then_inc(s_bt, 1)
            k["stats_loop"](dve, x_in, s_st)
            k["rstd_steps"](dve, chain, s_var, s_root)
            dve.wait_ge(c_in, 16)
            with dve.Fori(0, B // 2) as h:
                for u in range(2):
                    b = h * 2 + u
                    for i in range(TPB):
                        ins = k["norm_tile"](dve, xn[u][:, i, :], b * TPB + i)
                    ins.then_inc(s_xnp, 1)
                    dve.tensor_copy(path[u][:, :], flat2(ctx_sb[:, bass.ds(b, 1), :])).then_inc(s_ctp, 1)
                for u in range(2):
                    b = h * 2 + u
                    dve.wait_ge(s_tp, b + 1)
                    dve.tensor_copy(xT[u][:, :, :], tpx[u][:, :, :]).then_inc(s_xT, 1)
                    dve.wait_ge(s_cT, b + 1)
                    dve.tensor_copy(cT[u][:, :, :], tpc[u][:, :, 0:C]).then_inc(s_cTs, 1)
                for u in range(2):
                    b = h * 2 + u
                    dve.wait_ge(s_y0, b + 1)
                    dve.tensor_scalar(ri[u][:, :].bitcast(I32), y0[u][:, :].bitcast(I32), -1.0, float(0x7EF311C7),
                                      ALU.mult, ALU.add).then_inc(s_ri, 1)
                for u in range(2):
                    b = h * 2 + u
                    dve.wait_ge(s_ri, b + 1)
                    dve.wait_ge(s_res, b + 1)
                    dve.scalar_tensor_tensor(d2[u][:, :], d2[u][:, :], 0.5, ri[u][:, :], ALU.mult, ALU.mult).then_inc(s_cor, 1)
            dve.wait_ge(d_in, 16 * (LANES - 1))
            dve.wait_ge(s_corner, 16)
            dp = Chain(dve, s_dp)
            mask = [max(q - 1, 0) for q in range(32)]
            for s in range(STEPS):
                o = s * WCOL + PADL
                dp(dve.stream_shuffle(rskew[:, 0, o:o + WCOL], rskew[:, RPL, o - WCOL:o], mask))
                for r in range(RPL):
                    dp(dve.tensor_tensor(minw[:, :], rskew[:, r, o:o + WCOL], rskew[:, r, o - 1:o + WCOL - 1], ALU.min))
                    dp(dve.tensor_tensor_scan(rskew[:, r + 1, o:o + WCOL], minw[:, :], dskew[:, r, s * WCOL:(s + 1) * WCOL],
                                              rskew[:, r + 1, o - 1:o], ALU.min, ALU.add))
            g = Chain(dve, s_gch)
            dve.wait_ge(r_un, 16 * LANES)
            dve.wait_ge(s_dmp, 1)
            over, diag, left = rrow[:, 0:RPL, 1:S + 1], rrow[:, 0:RPL, 0:S], rrow[:, 1:RPL + 1, 0:S]
            g(dve.tensor_tensor(up[:, :, :], over, diag, ALU.is_lt))
            g(dve.scalar_tensor_tensor(up[:, :, :], up[:, :, :], 0.75, jr[:, :, :], ALU.mult, ALU.add))
            g(dve.tensor_tensor(gv[:, :, :], over, diag, ALU.min))
            g(dve.tensor_tensor(gv[:, :, :], gv[:, :, :], left, ALU.is_le))
            g(dve.tensor_tensor(up[:, :, :], up[:, :, :], gv[:, :, :], ALU.mult))
            flat = up[:, :, :].rearrange("p r w -> p (r w)")
            runs = rrow[:, :, :].rearrange("p r w -> p (r w)")[:, 0:RPL * S]
            g(dve.tensor_tensor_scan(runs, flat, flat, 0.0, ALU.max, ALU.max))
            run3 = runs.rearrange("p (r w) -> p r w", w=S)
            g(dve.tensor_tensor(gv[:, :, 1:S], run3[:, :, 1:S], run3[:, :, 0:S - 1], ALU.subtract))
            g(dve.scalar_tensor_tensor(gv[:, :, 0:1], run3[:, :, 0:1], 1.0, jr[:, :, 0:1], ALU.add, ALU.subtract))
            dve.memset(c2[:, :], float(S + 1)).then_inc(s_bt, 1)
            for lane in range(LANES - 1, 0, -1):
                dve.wait_ge(t_in, 16 * (LANES - 1))
                for r in range(RPL - 1, -1, -1):
                    i = RPL * (lane - 1) + r
                    dve.wait_ge(s_bt, 4 + C - 1 - i)
                    dve.scalar_tensor_tensor(junk[:, :], iota15[0:B, :], c2[:, i + 1:i + 2], chain_tab[:, i, :],
                                             ALU.is_le, ALU.mult, accum_out=c2[:, i:i + 1]).then_inc(s_bt, 1)
            dve.wait_ge(s_bt, 4 + C)
            dve.engine_nop().then_inc(s_c2, 1)
            dve.wait_ge(s_c2t, 1)
            dve.tensor_copy(cs[:, :, :], tpx[0][0:C, 0, 0:2 * B].rearrange("p (a b) -> p a b", a=2)).then_inc(s_cs, 1)
            dve.wait_ge(s_cs, 1)
            with dve.Fori(0, B // 2) as h:
                for u in range(2):
                    b = h * 2 + u
                    dve.tensor_scalar(pm[u][:, :], iota2[:, :], cs[:, 0, bass.ds(b, 1)], None, ALU.is_gt).then_inc(s_pm, 1)
                    dve.wait_ge(s_pm, b + 1)
                    dve.scalar_tensor_tensor(path[u][:, :], iota15[:, :], cs[:, 1, bass.ds(b, 1)], pm[u][:, :],
                                             ALU.is_le, ALU.mult).then_inc(s_path, 1)
                for u in range(2):
                    b = h * 2 + u
                    dve.wait_ge(s_ex, b + 1)
                    xb = xres[:, bass.ds(b * TPB, TPB), :]
                    dve.tensor_tensor(xb, xps[u][:, :, :], xb, ALU.add).then_inc(s_add, 1)


def phase_moe0(nc, a, out_tok, k):
    sb, pb, sem = k["sb"], k["pb"], k["sem"]
    cst, ident, xres, rstd, nmr, lnt = (k[n] for n in ("cst", "ident", "xres", "rstd", "nmr", "lnt"))
    xs, ys = k["xs0"], k["ys0"]
    NE, G4 = E0, E0 // GRP
    NG = TOK // 512
    with ExitStack() as ctx:
        w13 = sb(ctx, "e_w13", [P, KD, NE, 2 * I0])
        w2 = sb(ctx, "e_w2", [P, NE, D])
        b13 = sb(ctx, "e_b13", [P, NE, 2 * I0])
        b2 = sb(ctx, "e_b2", [P, NE, D])
        ws1 = sb(ctx, "e_ws1", [P, KD, 2 * I0])
        ws3 = sb(ctx, "e_ws3", [P, KD, 2 * I0])
        ws2 = sb(ctx, "e_ws2", [P, KD, D])
        bs13 = sb(ctx, "e_bs13", [P, 2, KD])
        bs2 = sb(ctx, "e_bs2", [P, D])
        gw = sb(ctx, "e_gw", [P, KD, NE])
        gb = sb(ctx, "e_gb", [P, NE])
        xT = sb(ctx, "e_xT", [P, NG, KD * 512])
        xT4 = xT[:, :, :].rearrange("p g (k n) -> p g k n", k=KD)
        z4 = xT[:, :, :].rearrange("p g (q d) -> p g q d", q=4)
        xn = [sb(ctx, f"e_xn{u}", [P, D]) for u in range(4)]
        xin = [sb(ctx, f"e_xin{u}", [P, D]) for u in range(U0)]
        xinT = [sb(ctx, f"e_xinT{u}", [P, KD, P]) for u in range(U0)]
        arena = sb(ctx, "e_arena", [P, 4096])
        hb = [arena[:, 256 * u:256 * u + 256] for u in range(U0)]
        yo = [arena[:, 1024 + 256 * u:1280 + 256 * u] for u in range(U0)]
        sg = [arena[:, 2048 + 128 * u:2176 + 128 * u] for u in range(U0)]
        gg = [arena[:, 2560 + 128 * u:2688 + 128 * u] for u in range(U0)]
        gT = [arena[:, 3072 + 128 * u:3200 + 128 * u] for u in range(U0)]
        gsh = [sb(ctx, f"e_gsh{i}", [P, 512]) for i in range(KD)]
        ssh = [sb(ctx, f"e_ssh{i}", [P, 512]) for i in range(KD)]
        big = [arena[:, 512 * i:512 * i + 512].rearrange("p (t e) -> p t e", e=NE) for i in range(7)]
        sr, scb, oh1, oh2, t3, mask = big[0], big[1], big[2], big[3], big[4], big[5]
        small = sb(ctx, "e_small", [P, 12, NT * G4])
        em = sb(ctx, "e_em", [P, NE])
        mx, t1 = small[:, 0, 0:NT], small[:, 1, 0:NT]
        wk = sb(ctx, "e_wk", [P, K0, NT])
        slots = [sb(ctx, f"e_slot{i}", [P, NT], U32) for i in range(K0)]
        etile = sb(ctx, "e_etile", [1, NTL0], I32)
        r = {"totE": big[6].rearrange("p t e -> p (t e)").rearrange("p (e t) -> p e t", e=NE), "t3": t3, "mask": mask,
             "cum": arena[:, 3584:4096].rearrange("p (e t) -> p e t", e=NE), "sst": sb(ctx, "e_sst", [P, NE + 1])[:, :],
             "ti": sb(ctx, "e_ti", [P, NE], I32)[:, :], "red": small[:, 2, 0:NT],
             "cmp": sb(ctx, "e_cmp", [1, NTL0, NE])[:, :, :], "tsum": sb(ctx, "e_tsum", [1, NTL0])[:, :]}
        for i, n in enumerate(("cnt", "tl", "tend", "delta")):
            r[n] = small[:, 3 + i, 0:NE]
        bank = [pb(ctx, f"e_bank{u}", [P, 512]) for u in range(8)]

        w_in = [sem(f"e_w_in{i}") for i in range(5)]
        (s_st, s_var, s_root, s_dve, s_xn, s_tp, s_xT, s_xTall, s_gs, s_gate, s_exp, s_max, s_mask, s_rank, s_slot) = (
            sem("e_" + n) for n in ("st", "var", "root", "dve", "xn_s", "tp", "xT_s", "xTall", "gs", "gate", "exp", "max",
                                    "mask", "rank", "slot"))
        s_h1, s_si, s_h3, s_gsh, s_zp, s_z, s_row = (sem("e_" + n) for n in ("h1", "si", "h3", "gsh_s", "zp", "z", "row"))
        sct = [sem(f"e_sct{u}") for u in range(4)]
        x_in = [sem(f"e_x_in{u}") for u in range(U0)]
        y_out = [sem(f"e_y_out{u}") for u in range(U0)]
        s_xt, s_xe, s_hh, s_hb, s_sg, s_g, s_gt, s_ge, s_yp, s_yo = (
            sem("e_" + n) for n in ("xt", "xe", "hh", "hb_s", "sg_s", "g", "gt", "ge", "yp", "yo_s"))
        gat = [sem(f"e_gat{u}") for u in range(4)]
        s_cb, s_c0 = sem("e_cb"), sem("e_c0")

        block = ctx.enter_context(nc.Block())

        @block.sync
        def _(sp):
            for old in k["old_sems"]:
                sp.sem_clear(old)
            sp.dma_start(gw[:, :, :], a["gate_w"]).then_inc(w_in[0], 16)
            sp.dma_start(gb[:, :], a["L0_ffn_gate_b"].partition_broadcast(P)).then_inc(w_in[0], 16)
            for dst, name in ((ws1, "ws1"), (ws3, "ws3"), (ws2, "ws2")):
                sp.dma_start(dst[:, :, :], a[name]).then_inc(w_in[1], 16)
            sp.dma_start(bs13[:, :, :], a["bs13"]).then_inc(w_in[1], 16)
            sp.dma_start(bs2[:, :], a["L0_ffn_bs2"].partition_broadcast(P)).then_inc(w_in[2], 16)
            sp.dma_start(w13[:, :, :, :], a["w13"]).then_inc(w_in[3], 16)
            sp.dma_start(w2[:, :, :], a["w2"]).then_inc(w_in[3], 16)
            sp.dma_start(b13[:, :, :].rearrange("p e n -> p (e n)"),
                         a["b13"].rearrange("e n -> (e n)").partition_broadcast(P)).then_inc(w_in[3], 16)
            sp.dma_start(b2[:, :, :].rearrange("p e n -> p (e n)"),
                         a["L0_ffn_be2"].rearrange("e n -> (e n)").partition_broadcast(P)).then_inc(w_in[4], 16)
            for u in range(U0):
                sp.sem_inc(y_out[u], 16)
            for u in range(4):
                sp.wait_ge(sct[u], 16 * K0 * NT // 4)
            with sp.Fori(0, NTL0 // U0) as h:
                for u in range(U0):
                    n = h * U0 + u
                    sp.wait_ge(s_xt, n + 1)
                    sp.dma_start(xin[u][:, :], xs[bass.ds(n * P, P), :]).then_inc(x_in[u], 16)
                for u in range(U0):
                    n = h * U0 + u
                    sp.wait_ge(s_yo, n + 1 + U0)
                    sp.dma_start(ys[bass.ds(n * P, P), :], yo[u]).then_inc(y_out[u], 16)

        @block.gpsimd
        def _(pool):
            pool.wait_ge(s_slot, 1)
            pool.wait_ge(k["s_zero"], 16 * k["n_zero"])
            for t in range(NT):
                pool.wait_ge(s_row, t + 1)
                for i in range(K0):
                    pool.indirect_dma_start(out=xs, out_offset=bass.IndirectOffsetOnAxis(ap=slots[i][:, t:t + 1], axis=0),
                                            in_=xn[t % 4][:, :], in_offset=None).then_inc(sct[t % 4], 16)
            for u in range(U0):
                pool.wait_ge(y_out[u], 16 * (NTL0 // U0 + 1))
            for t in range(NT):
                if t >= 4:
                    pool.wait_ge(s_cb, t - 3)
                for i in range(K0):
                    dst = (xn, xin)[i][t % 4]
                    pool.indirect_dma_start(out=dst[:, :], out_offset=None, in_=ys,
                                            in_offset=bass.IndirectOffsetOnAxis(ap=slots[i][:, t:t + 1], axis=0)
                                            ).then_inc(gat[t % 4], 16)

        @block.scalar
        def _(act):
            act.wait_ge(s_var, 1)
            act.activation(lnt[:, 1, :], lnt[:, 0, :], ACT.Sqrt).then_inc(s_root, 1)
            with act.Fori(0, NG) as g:
                for q in range(4):
                    act.wait_ge(s_tp, g * 4 + q + 1)
                    act.copy(flat3(xT4[:, bass.ds(g, 1), :, q * P:(q + 1) * P]),
                             bank[q][:, 0:D].rearrange("p (k n) -> p k n", k=KD)).then_inc(s_xTall, 1)
            act.wait_ge(s_max, 1)
            act.activation(scb, sr, ACT.Exp).then_inc(s_exp, 1)
            act.wait_ge(w_in[1], 64)
            with act.Fori(0, NG) as g:
                for i in range(KD):
                    act.wait_ge(s_h1, g * 4 + 2 * i + 1)
                    act.activation(ssh[i][:, :], bank[2 * i][:, :], ACT.Silu, bias=bs13[:, 0, i:i + 1]).then_inc(s_si, 1)
                    act.wait_ge(s_h1, g * 4 + 2 * i + 2)
                    act.activation(gsh[i][:, :], bank[2 * i + 1][:, :], ACT.Identity, bias=bs13[:, 1, i:i + 1]).then_inc(s_si, 1)
                for q in range(4):
                    act.wait_ge(s_zp, g * 4 + q + 1)
                    act.copy(flat2(flat2b(z4[:, bass.ds(g, 1), q:q + 1, :])), bank[4 + q][:, 0:D]).then_inc(s_z, 1)
            with act.Fori(0, NTL0 // U0) as h:
                for u in range(U0):
                    act.wait_ge(s_xt, h * U0 + u + 1 + U0)
                    act.copy(xinT[u][:, :, :], bank[u][:, 0:D].rearrange("p (k n) -> p k n", k=KD)).then_inc(s_xe, 1)
                for u in range(U0):
                    act.wait_ge(s_hb, h * U0 + u + 1)
                    act.activation(sg[u], hb[u][:, 0:I0], ACT.Silu).then_inc(s_sg, 1)
                for u in range(U0):
                    act.wait_ge(s_gt, h * U0 + u + 1)
                    act.copy(gT[u], bank[u][:, 0:P]).then_inc(s_ge, 1)

        @block.tensor
        def _(pe):
            pe.wait_ge(w_in[0], 32)
            with pe.Fori(0, NT // 4) as h:
                for q in range(4):
                    pe.wait_ge(s_xn, h * 4 + q + 1)
                    for kb in range(KD):
                        ins = pe.transpose(bank[q][:, kb * P:(kb + 1) * P], xn[q][:, kb * P:(kb + 1) * P], ident)
                    ins.then_inc(s_tp, 1)
                for q in range(4):
                    pe.wait_ge(s_xT, h * 4 + q + 1)
                    for kb in range(KD):
                        ins = pe.matmul(bank[4 + q][:, 0:NE], xinT[q][:, kb, :], gw[:, kb, :], start=(kb == 0), stop=(kb == KD - 1))
                    ins.then_inc(s_gs, 1)
            pe.wait_ge(w_in[1], 64)
            pe.wait_ge(s_xTall, NT)
            pe.wait_ge(s_gate, NT)

            def shared(g, dyn):
                for i in range(KD):
                    for j, w in enumerate((ws1, ws3)):
                        for kb in range(KD):
                            ins = pe.matmul(bank[2 * i + j][:, :], w[:, kb, i * P:(i + 1) * P],
                                            flat2(flat2b(xT4[:, bass.ds(g, 1), kb:kb + 1, :])), start=(kb == 0), stop=(kb == KD - 1))
                        ins.then_inc(s_h1, 1)
                for q in range(4):
                    for i in range(KD):
                        pe.wait_ge(s_gsh, g * 2 + i + 1)
                        ins = pe.matmul(bank[4 + q][:, 0:D], gsh[i][:, q * P:(q + 1) * P], ws2[:, i, :], start=(i == 0), stop=(i == KD - 1))
                    ins.then_inc(s_zp, 1)
            pe.wait_ge(s_mask, 1)
            pe.matmul(bank[6][:, :], cst[:, C_TRI:C_TRI + P], mask.rearrange("p t e -> p (t e)"), start=True, stop=True)
            pe.matmul(bank[7][:, :], cst[:, C_ONE:C_ONE + P], mask.rearrange("p t e -> p (t e)"), start=True, stop=True).then_inc(s_rank, 1)
            pe.wait_ge(s_slot, 1)
            with pe.Fori(0, NG) as g:
                pe.wait_ge(s_z, g * 4 + 1)
                shared(g, True)
            pe.wait_ge(w_in[3], 48)
            pe.wait_ge(s_z, NT + 1)
            pe.sem_inc(s_xt, U0)
            with pe.Fori(0, NTL0 // U0) as h:
                for u in range(U0):
                    n = h * U0 + u
                    pe.wait_ge(x_in[u], h * 16 + 16)
                    pe.wait_ge(s_yo, n + 1)
                    for kb in range(KD):
                        ins = pe.transpose(bank[u][:, kb * P:(kb + 1) * P], xin[u][:, kb * P:(kb + 1) * P], ident)
                    ins.then_inc(s_xt, 1)
                for u in range(U0):
                    n = h * U0 + u
                    e = pe.value_load(etile[0:1, bass.ds(n, 1)], min_val=0, max_val=NE - 1)
                    pe.wait_ge(s_xe, n + 1)
                    for kb in range(KD):
                        ins = pe.matmul(bank[u][:, D:2 * D], xinT[u][:, kb, :], flat2(flat2b(w13[:, kb:kb + 1, bass.ds(e, 1), :])),
                                        start=(kb == 0), stop=(kb == KD - 1))
                    ins.then_inc(s_hh, 1)
                for u in range(U0):
                    pe.wait_ge(s_g, h * U0 + u + 1)
                    pe.transpose(bank[u][:, 0:P], gg[u], ident).then_inc(s_gt, 1)
                for u in range(U0):
                    n = h * U0 + u
                    e = pe.value_load(etile[0:1, bass.ds(n, 1)], min_val=0, max_val=NE - 1)
                    pe.wait_ge(s_ge, n + 1)
                    pe.matmul(bank[u][:, D:2 * D], gT[u], flat2(w2[:, bass.ds(e, 1), :]), start=True, stop=True).then_inc(s_yp, 1)

        @block.vector
        def _(dve):
            chain = Chain(dve, s_dve)
            k["stats_loop"](dve, None, s_st)
            k["rstd_steps"](dve, chain, s_var, s_root)
            dve.wait_ge(w_in[0], 32)
            with dve.Fori(0, NT // 4) as h:
                for q in range(4):
                    k["norm_tile"](dve, xn[q][:, :], h * 4 + q).then_inc(s_xn, 1)
                for q in range(4):
                    dve.wait_ge(s_tp, h * 4 + q + 1)
                    dve.wait_ge(s_xTall, h * 4 + q + 1)
                    dve.tensor_copy(xinT[q][:, :, :], bank[q][:, 0:D].rearrange("p (k n) -> p k n", k=KD)).then_inc(s_xT, 1)
                for q in range(4):
                    dve.wait_ge(s_gs, h * 4 + q + 1)
                    dve.tensor_copy(flat2(sr[:, bass.ds(h * 4 + q, 1), :]), bank[4 + q][:, 0:NE]).then_inc(s_gate, 1)
            dve.wait_ge(s_gate, NT)

            def wide(ap, n=NE):
                return ap.unsqueeze(2).to_broadcast([P, NT, n])

            chain(dve.tensor_reduce(mx, sr, AX.X, ALU.max))
            dve.tensor_tensor(sr, sr, wide(mx), ALU.subtract).then_inc(s_max, 1)
            dve.wait_ge(s_exp, 1)
            chain(dve.tensor_reduce(mx, scb, AX.X, ALU.add))
            chain(dve.reciprocal(t1, mx))
            chain(dve.tensor_tensor(sr, scb, wide(t1), ALU.mult))
            chain(dve.tensor_tensor(scb, sr, gb[:, :].unsqueeze(1).to_broadcast([P, NT, NE]), ALU.add))
            v4 = scb.rearrange("p t (g e) -> p (t g) e", e=GRP)
            hi1, lo1, hi2, lo2, gs, gt = (small[:, i, :] for i in range(6))
            chain(dve.tensor_tensor(hi1, v4[:, :, 0], v4[:, :, 1], ALU.max))
            chain(dve.tensor_tensor(lo1, v4[:, :, 0], v4[:, :, 1], ALU.min))
            chain(dve.tensor_tensor(hi2, v4[:, :, 2], v4[:, :, 3], ALU.max))
            chain(dve.tensor_tensor(lo2, v4[:, :, 2], v4[:, :, 3], ALU.min))
            chain(dve.tensor_tensor(gs, hi1, hi2, ALU.max))
            chain(dve.tensor_tensor(gt, hi1, hi2, ALU.min))
            chain(dve.tensor_tensor(lo1, lo1, lo2, ALU.max))
            chain(dve.tensor_tensor(gt, gt, lo1, ALU.max))
            chain(dve.tensor_tensor(gs, gs, gt, ALU.add))
            rk = small[:, 6, :].rearrange("p (t g) -> p t g", g=G4)
            cc = small[:, 7, :].rearrange("p (t g) -> p t g", g=G4)
            g3 = gs.rearrange("p (t g) -> p t g", g=G4)
            chain(dve.tensor_scalar(rk, cst[:, C_IOTA:C_IOTA + G4].unsqueeze(1).to_broadcast([P, NT, G4]),
                                    -1.0, float(G4 - 1), ALU.mult, ALU.add))
            for d in range(1, G4):
                chain(dve.tensor_tensor(cc[:, :, 0:G4 - d], g3[:, :, 0:G4 - d], g3[:, :, d:G4], ALU.is_ge))
                chain(dve.tensor_tensor(rk[:, :, d:G4], rk[:, :, d:G4], cc[:, :, 0:G4 - d], ALU.add))
                chain(dve.tensor_tensor(rk[:, :, 0:G4 - d], rk[:, :, 0:G4 - d], cc[:, :, 0:G4 - d], ALU.subtract))
            chain(dve.tensor_scalar(small[:, 6, :], small[:, 6, :], 1.5, -BIG, ALU.is_gt, ALU.mult))
            chain(dve.tensor_tensor(v4, v4, small[:, 6, :].unsqueeze(2).to_broadcast([P, NT * G4, GRP]), ALU.add))
            chain(dve.tensor_scalar(em[:, :], cst[:, C_IOTA:C_IOTA + NE], float(-NE), None, ALU.add))
            pick_first_max(dve, chain, oh1, mx, scb, em[:, :], t3, t1, NE)
            chain(dve.scalar_tensor_tensor(scb, oh1, -2.0 * BIG, scb, ALU.mult, ALU.add))
            pick_first_max(dve, chain, oh2, mx, scb, em[:, :], t3, t1, NE)
            for i, oh in enumerate((oh1, oh2)):
                chain(dve.tensor_tensor(t3, sr, oh, ALU.mult))
                chain(dve.tensor_reduce(wk[:, i, :], t3, AX.X, ALU.add))
            assign_slots(dve, chain, r, (oh1, oh2), [s[:, :] for s in slots], etile[:, :], NE, NTL0,
                         bank[6][:, :].rearrange("p (t e) -> p t e", e=NE), bank[7][:, :].rearrange("p (t e) -> p t e", e=NE),
                         cst, s_mask, s_rank)
            dve.engine_nop().then_inc(s_slot, 1)
            dve.sem_inc(s_z, 1)
            def row(t):
                if t >= 4:
                    dve.wait_ge(sct[t % 4], 16 * K0 * (t // 4))
                k["norm_tile"](dve, xn[t % 4][:, :], t).then_inc(s_row, 1)

            for g in range(NG):
                for q in range(4):
                    row(g * 4 + q)
                for i in range(KD):
                    dve.wait_ge(s_si, g * 4 + 2 * i + 2)
                    dve.tensor_tensor(gsh[i][:, :], gsh[i][:, :], ssh[i][:, :], ALU.mult).then_inc(s_gsh, 1)
            dve.wait_ge(w_in[3], 48)
            dve.wait_ge(w_in[4], 16)
            dve.sem_inc(s_yo, U0)
            with dve.Fori(0, NTL0 // U0) as h:
                for u in range(U0):
                    n = h * U0 + u
                    e = dve.value_load(etile[0:1, bass.ds(n, 1)], min_val=0, max_val=NE - 1)
                    dve.wait_ge(s_hh, n + 1)
                    dve.tensor_tensor(hb[u], bank[u][:, D:2 * D], flat2(b13[:, bass.ds(e, 1), :]), ALU.add).then_inc(s_hb, 1)
                for u in range(U0):
                    dve.wait_ge(s_sg, h * U0 + u + 1)
                    dve.tensor_tensor(gg[u], sg[u], hb[u][:, I0:2 * I0], ALU.mult).then_inc(s_g, 1)
                for u in range(U0):
                    n = h * U0 + u
                    e = dve.value_load(etile[0:1, bass.ds(n, 1)], min_val=0, max_val=NE - 1)
                    dve.wait_ge(s_yp, n + 1)
                    dve.wait_ge(y_out[u], h * 16 + 16)
                    dve.tensor_tensor(yo[u], bank[u][:, D:2 * D], flat2(b2[:, bass.ds(e, 1), :]), ALU.add).then_inc(s_yo, 1)
            dve.wait_ge(w_in[2], 16)
            add = Chain(dve, s_c0)
            for t in range(NT):
                xt = xres[:, t, :]
                add(dve.tensor_tensor(xt, xt, z4[:, t // 4, t % 4, :], ALU.add))
                add(dve.tensor_tensor(xt, xt, bs2[:, :], ALU.add))
                dve.wait_ge(gat[t % 4], 16 * K0 * (t // 4 + 1))
                add(dve.scalar_tensor_tensor(xt, xn[t % 4][:, :], wk[:, 0, t:t + 1], xt, ALU.mult, ALU.add))
                dve.scalar_tensor_tensor(xt, xin[t % 4][:, :], wk[:, 1, t:t + 1], xt, ALU.mult, ALU.add).then_inc(s_cb, 1)


def phase_xattn(nc, a, out_tok, k):
    sb, pb, sem = k["sb"], k["pb"], k["sem"]
    cst, ident, xres, rstd, nmr, lnt = (k[n] for n in ("cst", "ident", "xres", "rstd", "nmr", "lnt"))
    ones = cst[:, C_ONE:C_ONE + P]
    with ExitStack() as ctx:
        ctx_sb = sb(ctx, "a_ctx", [C, B, D])
        wqv = sb(ctx, "a_wqv", [P, 4, KD, D])
        wsim = sb(ctx, "a_wsim", [P, 3, KD])
        bsim = sb(ctx, "a_bsim", [1, 1])
        bqv = sb(ctx, "a_bqv", [P, D])

        def two(name, shape):
            return [sb(ctx, f"a_{name}{u}", shape) for u in range(2)]
        xn, cS, hcT, cT, qmod = two("xn", [P, TPB, D]), two("cS", [C, D]), two("hcT", [P, KD, S]), two("cT", [P, KD, C]), two("qmod", [P, KD, C])
        brow, mx, nmx, ssum, att, attT = two("brow", [1, C]), two("mx", [P, TPB]), two("nmx", [P, TPB]), two("ssum", [P, 2 * TPB]), two("att", [P, TPB, C]), two("attT", [C, S])
        hqT, prT, wp = two("hqT", [P, KD, S]), two("prT", [P, KD, S]), two("wp", [P, KD, D])
        gmx, erow, esum, battn, tmp = two("gmx", [1, 1]), two("erow", [1, S]), two("esum", [1, 2]), two("battn", [P, TPB]), two("tmp", [P, TPB, D])
        A, Bk, Ck, Dk = ([pb(ctx, f"a_{n}{u}", [P, 512]) for u in range(2)] for n in "ABCD")

        w_in = [sem(f"a_w_in{i}") for i in range(3)]
        names = ("st var root dve xn cS tp ctp hcT qmod cTs r brow sim mx nmx exp rs att attT attE rowm gmx erow es bcol bcs hcb wp hq hqE pr out tmp add").split()
        q = {n: sem("a_" + n) for n in names}
        block = ctx.enter_context(nc.Block())

        @block.sync
        def _(sp):
            sp.dma_start(ctx_sb[:, :, :], a["ctx_1024"].rearrange("b i d -> i b d")).then_inc(w_in[0], 16)
            sp.dma_start(wsim[:, :, :], a["wsim"]).then_inc(w_in[0], 16)
            sp.dma_start(bsim[:, :], a["b_sim"]).then_inc(w_in[0], 16)
            sp.dma_start(wqv[:, :, :, :], a["wqv"]).then_inc(w_in[1], 16)
            sp.dma_start(bqv[:, :], a["L1_xattn_b_qv"].partition_broadcast(P)).then_inc(w_in[1], 16)
            for kb in range(KD):
                sp.dma_start(k["l1_w1"][:, kb, :, :], a["l1_w1"][:, kb, :, :]).then_inc(k["s_w1"], 16)

        @block.scalar
        def _(act):
            act.wait_ge(q["var"], 1)
            act.activation(lnt[:, 1, :], lnt[:, 0, :], ACT.Sqrt).then_inc(q["root"], 1)
            act.wait_ge(w_in[0], 48)
            with act.Fori(0, B // 2) as h:
                for u in range(2):
                    b = h * 2 + u
                    act.wait_ge(q["add"], b + 1)
                    act.copy(cS[u][:, :], flat2(ctx_sb[:, bass.ds(b, 1), :])).then_inc(q["cS"], 1)
                for u in range(2):
                    b = h * 2 + u
                    act.wait_ge(q["ctp"], b + 1)
                    act.copy(cT[u][:, :, :], Bk[u][:, 0:2 * C].rearrange("p (k c) -> p k c", k=KD)).then_inc(q["cTs"], 1)
                    act.wait_ge(q["tp"], b + 1)
                    act.copy(hcT[u][:, :, :], A[u][:, :].rearrange("p (k n) -> p k n", k=KD)).then_inc(q["hcT"], 1)
                for u in range(2):
                    b = h * 2 + u
                    act.wait_ge(q["nmx"], b + 1)
                    for i in range(TPB):
                        act.activation(att[u][:, i, :], Ck[u][:, i * P:i * P + C], ACT.Exp, bias=nmx[u][:, i:i + 1],
                                       accum_out=ssum[u][:, i:i + 1]).then_inc(q["exp"], 1)
                for u in range(2):
                    b = h * 2 + u
                    act.wait_ge(q["gmx"], b + 1)
                    act.activation(erow[u][:, :], Bk[u][0:1, 0:S], ACT.Exp, bias=gmx[u][:, :],
                                   accum_out=esum[u][:, 0:1]).then_inc(q["erow"], 1)
                    act.wait_ge(q["attT"], b + 1)
                    act.copy(attT[u][:, :], Dk[u][0:C, 0:S]).then_inc(q["attE"], 1)
                for u in range(2):
                    b = h * 2 + u
                    act.wait_ge(q["hq"], b + 1)
                    act.copy(hqT[u][:, :, :], A[u][:, :].rearrange("p (k n) -> p k n", k=KD)).then_inc(q["hqE"], 1)

        @block.tensor
        def _(pe):
            with pe.Fori(0, B // 2) as h:
                for u in range(2):
                    b = h * 2 + u
                    pe.wait_ge(q["cS"], b + 1)
                    for kb in range(KD):
                        ins = pe.transpose(Bk[u][:, kb * C:(kb + 1) * C], cS[u][:, kb * P:(kb + 1) * P], ident[0:C, 0:C])
                    ins.then_inc(q["ctp"], 1)
                    pe.wait_ge(q["xn"], b + 1)
                    for i in range(TPB):
                        for kb in range(KD):
                            ins = pe.transpose(A[u][:, kb * S + i * P:kb * S + (i + 1) * P], xn[u][:, i, kb * P:(kb + 1) * P], ident)
                    ins.then_inc(q["tp"], 1)
                for u in range(2):
                    b = h * 2 + u
                    pe.wait_ge(q["cTs"], b + 1)
                    for kb in range(KD):
                        ins = pe.matmul(Dk[u][0:1, 0:C], wsim[:, 1, kb:kb + 1], cT[u][:, kb, :], start=(kb == 0), stop=(kb == KD - 1))
                    ins.then_inc(q["r"], 1)
                for u in range(2):
                    b = h * 2 + u
                    pe.wait_ge(q["hcT"], b + 1)
                    pe.wait_ge(q["brow"], b + 1)
                    for i in range(TPB):
                        for kb in range(KD):
                            pe.matmul(Ck[u][:, i * P:i * P + C], hcT[u][:, kb, i * P:(i + 1) * P], qmod[u][:, kb, :], start=(kb == 0), stop=False)
                        ins = pe.matmul(Ck[u][:, i * P:i * P + C], ones[0:1, :], brow[u][:, :], start=False, stop=True)
                    ins.then_inc(q["sim"], 1)
                for u in range(2):
                    b = h * 2 + u
                    pe.wait_ge(q["mx"], b + 1)
                    for i in range(TPB):
                        ins = pe.matmul(Bk[u][0:1, i * P:(i + 1) * P], mx[u][:, i:i + 1], ident, start=True, stop=True)
                    ins.then_inc(q["rowm"], 1)
                for u in range(2):
                    b = h * 2 + u
                    pe.wait_ge(q["att"], b + 1)
                    for i in range(TPB):
                        ins = pe.transpose(Dk[u][0:C, i * P:(i + 1) * P], att[u][:, i, :], ident)
                    ins.then_inc(q["attT"], 1)
                for u in range(2):
                    b = h * 2 + u
                    pe.wait_ge(q["attE"], b + 1)
                    for kb in range(KD):
                        ins = pe.matmul(A[u][:, kb * S:(kb + 1) * S], cS[u][:, kb * P:(kb + 1) * P], attT[u][:, :], start=True, stop=True)
                    ins.then_inc(q["hq"], 1)
                for u in range(2):
                    b = h * 2 + u
                    pe.wait_ge(q["es"], b + 1)
                    for i in range(TPB):
                        ins = pe.matmul(Ck[u][:, i:i + 1], erow[u][:, i * P:(i + 1) * P], esum[u][:, 1:2], start=True, stop=True)
                    ins.then_inc(q["bcol"], 1)
                for u in range(2):
                    b = h * 2 + u
                    pe.wait_ge(q["bcs"], b + 1)
                    for kb in range(KD):
                        for i in range(TPB):
                            ins = pe.matmul(Ck[u][:, 8 + kb:9 + kb], xn[u][:, i, kb * P:(kb + 1) * P], battn[u][:, i:i + 1],
                                            start=(i == 0), stop=(i == TPB - 1))
                    ins.then_inc(q["hcb"], 1)
                pe.wait_ge(w_in[1], 32)
                for u in range(2):
                    b = h * 2 + u
                    pe.wait_ge(q["hqE"], b + 1)
                    pe.wait_ge(q["pr"], b + 1)
                    pe.wait_ge(q["wp"], b + 1)
                    for i in range(TPB):
                        n = 0
                        for part, rhs in ((hqT, lambda kb: wqv[:, 1, kb, :]), (prT, lambda kb: wqv[:, 2, kb, :]), (hcT, lambda kb: wp[u][:, kb, :])):
                            for kb in range(KD):
                                ins = pe.matmul(Bk[u][:, i * D:(i + 1) * D], part[u][:, kb, i * P:(i + 1) * P], rhs(kb), start=(n == 0), stop=(n == 5))
                                n += 1
                    ins.then_inc(q["out"], 1)

        @block.vector
        def _(dve):
            dve.sem_inc(q["add"], 2)
            chain = Chain(dve, q["dve"])
            k["stats_loop"](dve, None, q["st"])
            k["rstd_steps"](dve, chain, q["var"], q["root"])
            dve.wait_ge(w_in[0], 48)
            dve.wait_ge(w_in[1], 32)
            with dve.Fori(0, B // 2) as h:
                for u in range(2):
                    for i in range(TPB):
                        ins = k["norm_tile"](dve, xn[u][:, i, :], (h * 2 + u) * TPB + i)
                    ins.then_inc(q["xn"], 1)
                for u in range(2):
                    b = h * 2 + u
                    dve.wait_ge(q["cTs"], b + 1)
                    for kb in range(KD):
                        dve.tensor_scalar(qmod[u][:, kb, :], cT[u][:, kb, :], wsim[:, 2, kb:kb + 1], wsim[:, 0, kb:kb + 1],
                                          ALU.mult, ALU.add).then_inc(q["qmod"], 1)
                    dve.wait_ge(q["r"], b + 1)
                    dve.tensor_scalar(brow[u][:, :], Dk[u][0:1, 0:C], bsim[:, :], None, ALU.add).then_inc(q["brow"], 1)
                for u in range(2):
                    b = h * 2 + u
                    dve.wait_ge(q["sim"], b + 1)
                    dve.tensor_reduce(mx[u][:, :], Ck[u][:, 0:2 * P].rearrange("p (i c) -> p i c", i=TPB)[:, :, 0:C], AX.X, ALU.max).then_inc(q["mx"], 1)
                    dve.wait_ge(q["mx"], b + 1)
                    dve.tensor_scalar(nmx[u][:, :], mx[u][:, :], -1.0, None, ALU.mult).then_inc(q["nmx"], 1)
                for u in range(2):
                    b = h * 2 + u
                    dve.wait_ge(q["rowm"], b + 1)
                    dve.tensor_reduce(gmx[u][:, :], Bk[u][0:1, 0:S], AX.X, ALU.max, negate=True).then_inc(q["gmx"], 1)
                    dve.wait_ge(q["exp"], b * TPB + TPB)
                    dve.reciprocal(ssum[u][:, TPB:2 * TPB], ssum[u][:, 0:TPB]).then_inc(q["rs"], 1)
                    dve.wait_ge(q["rs"], b + 1)
                    for i in range(TPB):
                        ins = dve.tensor_scalar(att[u][:, i, :], att[u][:, i, :], ssum[u][:, TPB + i:TPB + i + 1], None, ALU.mult)
                    ins.then_inc(q["att"], 1)
                for u in range(2):
                    b = h * 2 + u
                    dve.wait_ge(q["erow"], b + 1)
                    dve.reciprocal(esum[u][:, 1:2], esum[u][:, 0:1]).then_inc(q["es"], 1)
                for u in range(2):
                    b = h * 2 + u
                    dve.wait_ge(q["bcol"], b + 1)
                    dve.tensor_copy(battn[u][:, :], Ck[u][:, 0:TPB]).then_inc(q["bcs"], 1)
                for u in range(2):
                    b = h * 2 + u
                    dve.wait_ge(q["hqE"], b + 1)
                    dve.tensor_tensor(prT[u][:, :, :], hcT[u][:, :, :], hqT[u][:, :, :], ALU.mult).then_inc(q["pr"], 1)
                    dve.wait_ge(q["hcb"], b + 1)
                    for kb in range(KD):
                        ins = dve.scalar_tensor_tensor(wp[u][:, kb, :], wqv[:, 3, kb, :], Ck[u][:, 8 + kb:9 + kb], wqv[:, 0, kb, :], ALU.mult, ALU.add)
                    ins.then_inc(q["wp"], 1)
                for u in range(2):
                    b = h * 2 + u
                    dve.wait_ge(q["out"], b + 1)
                    dve.tensor_tensor(tmp[u][:, :, :], Bk[u][:, :].rearrange("p (i d) -> p i d", i=TPB),
                                      bqv[:, :].unsqueeze(1).to_broadcast([P, TPB, D]), ALU.add).then_inc(q["tmp"], 1)
                for u in range(2):
                    b = h * 2 + u
                    dve.wait_ge(q["tmp"], b + 1)
                    xb = xres[:, bass.ds(b * TPB, TPB), :]
                    dve.tensor_tensor(xb, tmp[u][:, :, :], xb, ALU.add).then_inc(q["add"], 1)


def phase_moe1(nc, a, out_tok, k):
    sb, pb, sem = k["sb"], k["pb"], k["sem"]
    cst, ident, xres, rstd, nmr, lnt, st6, mv, w1 = (k[n] for n in ("cst", "ident", "xres", "rstd", "nmr", "lnt", "st6", "mv", "l1_w1"))
    xs, ys = k["xs1"], k["ys1"]
    NE = E1
    with ExitStack() as ctx:
        w2 = sb(ctx, "f_w2", [P, FB, NE, D])
        b1 = sb(ctx, "f_b1", [P, NE, FB])
        b2 = sb(ctx, "f_b2", [P, NE, D])
        lgb = sb(ctx, "f_lgb", [P, NE, 2 * KD])
        cw = sb(ctx, "f_cw", [P, KD, NE])
        xn = [sb(ctx, f"f_xn{u}", [P, D]) for u in range(4)]
        xT = [sb(ctx, f"f_xT{u}", [P, KD, P]) for u in range(4)]
        arena = sb(ctx, "f_arena", [P, 2048 + 2048])
        hs = [arena[:, 1024 * u:1024 * u + 1024] for u in range(U1)]
        hT = [arena[:, 2048 + 1024 * u:3072 + 1024 * u].rearrange("p (f n) -> p f n", f=FB) for u in range(U1)]
        yo = [sb(ctx, f"f_yo{u}", [P, D]) for u in range(U1)]
        big = [arena[:, 256 * i:256 * i + 256].rearrange("p (t e) -> p t e", e=NE) for i in range(5)]
        aff, oh, t3 = big[0], big[1], big[2]
        em = sb(ctx, "f_em", [P, NE])
        sm = sb(ctx, "f_sm", [P, 8, NT])
        top, t1, alpha = sm[:, 0, :], sm[:, 1, :], sm[:, 2, :]
        rs2, nm2 = sb(ctx, "f_rs2", [P, NT]), sb(ctx, "f_nm2", [P, NT])
        slot = sb(ctx, "f_slot", [P, NT], U32)
        etile = sb(ctx, "f_etile", [1, NTL1], I32)
        r = {"totE": big[3].rearrange("p t e -> p (t e)").rearrange("p (e t) -> p e t", e=NE), "t3": t3,
             "cum": big[4].rearrange("p t e -> p (t e)").rearrange("p (e t) -> p e t", e=NE), "sst": sb(ctx, "f_sst", [P, NE + 1])[:, :],
             "ti": sb(ctx, "f_ti", [P, NE], I32)[:, :], "red": sm[:, 3, :],
             "cmp": sb(ctx, "f_cmp", [1, NTL1, NE])[:, :, :], "tsum": sb(ctx, "f_tsum", [1, NTL1])[:, :]}
        for i, n in enumerate(("cnt", "tl", "tend", "delta")):
            r[n] = sm[:, 4 + i, 0:NE]
        bank = [pb(ctx, f"f_bank{u}", [P, 512]) for u in range(8)]

        w_in = [sem(f"f_w_in{i}") for i in range(2)]
        names = ("st var root dve xn tp xT gs gate var2 root2 exp1 exp2 mask rank slot row xt xe hh hs1 hs2 t ht1 ht2 yp yo cb add").split()
        q = {n: sem("f_" + n) for n in names}
        sct = [sem(f"f_sct{u}") for u in range(4)]
        gat = [sem(f"f_gat{u}") for u in range(4)]
        x_in = [sem(f"f_x_in{u}") for u in range(U1)]
        y_out = [sem(f"f_y_out{u}") for u in range(U1)]
        s_res = sem("f_res")
        block = ctx.enter_context(nc.Block())
        xin = xn

        @block.sync
        def _(sp):
            sp.dma_start(cw[:, :, :], a["cw"]).then_inc(w_in[0], 16)
            for dst, name in ((b1[:, :, :], "b1"), (lgb[:, :, :], "lgb")):
                sp.dma_start(dst, a[name]).then_inc(w_in[1], 16)
            sp.dma_start(b2[:, :, :].rearrange("p e n -> p (e n)"), a["L1_ffn_b2"].rearrange("e n -> (e n)").partition_broadcast(P)).then_inc(w_in[1], 16)
            for c in range(4):
                sp.dma_start(w2[:, 2 * c:2 * c + 2, :, :], a["l1_w2"][:, 2 * c:2 * c + 2, :, :]).then_inc(w_in[1], 16)
            for u in range(U1):
                sp.sem_inc(y_out[u], 16)
            for u in range(4):
                sp.wait_ge(sct[u], 16 * NT // 4)
            with sp.Fori(0, NTL1 // U1) as h:
                for u in range(U1):
                    n = h * U1 + u
                    sp.wait_ge(q["xt"], n + 1)
                    sp.dma_start(xin[u][:, :], xs[bass.ds(n * P, P), :]).then_inc(x_in[u], 16)
                for u in range(U1):
                    n = h * U1 + u
                    sp.wait_ge(q["yo"], n + 1 + U1)
                    sp.dma_start(ys[bass.ds(n * P, P), :], yo[u][:, :]).then_inc(y_out[u], 16)
            for t in range(0, NT, 4):
                sp.wait_ge(q["cb"], t + 4)
                sp.dma_start(out_tok[:, t:t + 4, :], xres[:, t:t + 4, :]).then_inc(s_res, 16)
            sp.wait_ge(s_res, 16 * NT // 4)

        @block.gpsimd
        def _(pool):
            pool.wait_ge(q["slot"], 1)
            pool.wait_ge(k["s_zero"], 16 * k["n_zero"])
            for t in range(NT):
                pool.wait_ge(q["row"], t + 1)
                pool.indirect_dma_start(out=xs, out_offset=bass.IndirectOffsetOnAxis(ap=slot[:, t:t + 1], axis=0),
                                        in_=xn[t % 4][:, :], in_offset=None).then_inc(sct[t % 4], 16)
            for u in range(U1):
                pool.wait_ge(y_out[u], 16 * (NTL1 // U1 + 1))
            for t in range(NT):
                if t >= 4:
                    pool.wait_ge(q["cb"], t - 3)
                pool.indirect_dma_start(out=xn[t % 4][:, :], out_offset=None, in_=ys,
                                        in_offset=bass.IndirectOffsetOnAxis(ap=slot[:, t:t + 1], axis=0)).then_inc(gat[t % 4], 16)

        @block.scalar
        def _(act):
            act.wait_ge(q["var"], 1)
            act.activation(lnt[:, 1, :], lnt[:, 0, :], ACT.Sqrt).then_inc(q["root"], 1)
            act.wait_ge(q["var2"], 1)
            act.activation(lnt[:, 1, :], lnt[:, 0, :], ACT.Sqrt).then_inc(q["root2"], 1)
            act.wait_ge(q["exp1"], 1)
            act.activation(alpha, top, ACT.Exp, scale=-1.0).then_inc(q["exp2"], 1)
            act.wait_ge(w_in[1], 16 * 7)
            act.wait_ge(q["slot"], 1)
            with act.Fori(0, NTL1 // U1) as h:
                es = []
                for u in range(U1):
                    n = h * U1 + u
                    e = act.value_load(etile[0:1, bass.ds(n, 1)], min_val=0, max_val=NE - 1)
                    es.append(e)
                    act.wait_ge(q["xt"], n + 1 + U1)
                    for kb in range(KD):
                        act.activation(xT[u][:, kb, :], bank[4 * u + 2][:, kb * P:(kb + 1) * P], ACT.Identity,
                                       scale=flat2(lgb[:, bass.ds(e, 1), kb:kb + 1]), bias=flat2(lgb[:, bass.ds(e, 1), KD + kb:KD + kb + 1])).then_inc(q["xe"], 1)
                for u in range(U1):
                    n = h * U1 + u
                    act.wait_ge(q["hh"], n + 1)
                    act.copy(hs[u][:, 512:1024], bank[4 * u + 1][:, :]).then_inc(q["hs2"], 1)
                for u in range(U1):
                    n = h * U1 + u
                    act.wait_ge(q["t"], n * 2 + 2)
                    for f in range(FB // 2, FB):
                        act.activation(hT[u][:, f, :], bank[4 * u + 3][:, (f - 4) * P:(f - 3) * P], ACT.Relu,
                                       bias=flat2(b1[:, bass.ds(es[u], 1), f:f + 1])).then_inc(q["ht2"], 1)

        @block.tensor
        def _(pe):
            pe.wait_ge(w_in[0], 16)
            with pe.Fori(0, NT // 4) as h:
                for i in range(4):
                    pe.wait_ge(q["xn"], h * 4 + i + 1)
                    for kb in range(KD):
                        ins = pe.transpose(bank[i][:, kb * P:(kb + 1) * P], xn[i][:, kb * P:(kb + 1) * P], ident)
                    ins.then_inc(q["tp"], 1)
                for i in range(4):
                    pe.wait_ge(q["xT"], h * 4 + i + 1)
                    for kb in range(KD):
                        ins = pe.matmul(bank[4 + i][:, 0:NE], xT[i][:, kb, :], cw[:, kb, :], start=(kb == 0), stop=(kb == KD - 1))
                    ins.then_inc(q["gs"], 1)
            pe.wait_ge(q["mask"], 1)
            pe.matmul(bank[6][:, 0:NT * NE], cst[:, C_TRI:C_TRI + P], oh.rearrange("p t e -> p (t e)"), start=True, stop=True)
            pe.matmul(bank[7][:, 0:NT * NE], cst[:, C_ONE:C_ONE + P], oh.rearrange("p t e -> p (t e)"), start=True, stop=True).then_inc(q["rank"], 1)
            pe.wait_ge(q["slot"], 1)
            pe.wait_ge(k["s_w1"], 16 * KD)
            pe.wait_ge(w_in[1], 16 * 7)
            pe.sem_inc(q["xt"], U1)
            with pe.Fori(0, NTL1 // U1) as h:
                es = []
                for u in range(U1):
                    n = h * U1 + u
                    es.append(pe.value_load(etile[0:1, bass.ds(n, 1)], min_val=0, max_val=NE - 1))
                    pe.wait_ge(x_in[u], h * 16 + 16)
                    for kb in range(KD):
                        ins = pe.transpose(bank[4 * u + 2][:, kb * P:(kb + 1) * P], xin[u][:, kb * P:(kb + 1) * P], ident)
                    ins.then_inc(q["xt"], 1)
                for u in range(U1):
                    n = h * U1 + u
                    pe.wait_ge(q["xe"], n * KD + KD)
                    pe.wait_ge(q["yo"], n + 1)
                    for c in range(2):
                        for kb in range(KD):
                            ins = pe.matmul(bank[4 * u + c][:, :], xT[u][:, kb, :],
                                            flat2(flat2b(w1[:, kb:kb + 1, bass.ds(es[u], 1), c * 512:(c + 1) * 512])), start=(kb == 0), stop=(kb == KD - 1))
                    ins.then_inc(q["hh"], 1)
                for u in range(U1):
                    n = h * U1 + u
                    pe.wait_ge(q["hs1"], n + 1)
                    pe.wait_ge(q["hs2"], n + 1)
                    for f in range(FB):
                        ins = pe.transpose(bank[4 * u + 2 + f // 4][:, (f % 4) * P:(f % 4 + 1) * P], hs[u][:, f * P:(f + 1) * P], ident)
                        if f % 4 == 3:
                            ins.then_inc(q["t"], 1)
                for u in range(U1):
                    n = h * U1 + u
                    pe.wait_ge(q["ht1"], (n + 1) * (FB // 2))
                    pe.wait_ge(q["ht2"], (n + 1) * (FB // 2))
                    for f in range(FB):
                        ins = pe.matmul(bank[4 * u][:, 0:D], hT[u][:, f, :], flat2(flat2b(w2[:, f:f + 1, bass.ds(es[u], 1), :])), start=(f == 0), stop=(f == FB - 1))
                    ins.then_inc(q["yp"], 1)

        @block.vector
        def _(dve):
            chain = Chain(dve, q["dve"])
            k["stats_loop"](dve, None, q["st"])
            k["rstd_steps"](dve, chain, q["var"], q["root"])
            dve.wait_ge(w_in[0], 16)
            with dve.Fori(0, NT // 4) as h:
                for i in range(4):
                    k["norm_tile"](dve, xn[i][:, :], h * 4 + i).then_inc(q["xn"], 1)
                for i in range(4):
                    dve.wait_ge(q["xn"], h * 4 + i + 1)
                    dve.bn_stats(flat2(st6[:, bass.ds(h * 4 + i, 1), :]), xn[i][:, :]).then_inc(q["st"], 1)
                for i in range(4):
                    dve.wait_ge(q["tp"], h * 4 + i + 1)
                    dve.tensor_copy(xT[i][:, :, :], bank[i][:, 0:D].rearrange("p (k n) -> p k n", k=KD)).then_inc(q["xT"], 1)
                for i in range(4):
                    dve.wait_ge(q["gs"], h * 4 + i + 1)
                    dve.tensor_copy(flat2(aff[:, bass.ds(h * 4 + i, 1), :]), bank[4 + i][:, 0:NE]).then_inc(q["gate"], 1)
            dve.wait_ge(q["gate"], NT)
            dve.wait_ge(q["st"], 3 * NT)
            for t in range(NT):
                dve.bn_aggr(mv[:, t, :], st6[:, t, :]).then_inc(q["st"], 1)
            dve.wait_ge(q["st"], 4 * NT)
            ve, t0, tt = lnt[:, 0, :], lnt[:, 1, :], lnt[:, 2, :]
            dve.tensor_scalar(ve, mv[:, :, 1], EPS, None, ALU.add).then_inc(q["var2"], 1)
            dve.wait_ge(q["root2"], 1)
            chain(dve.reciprocal(tt, t0))
            chain(dve.tensor_tensor(tt, ve, tt, ALU.mult))
            chain(dve.tensor_tensor(tt, tt, t0, ALU.add))
            chain(dve.tensor_scalar(tt, tt, 0.5, None, ALU.mult))
            chain(dve.reciprocal(t0, tt))
            chain(dve.tensor_tensor(rs2[:, :], rstd[:, :], t0, ALU.mult))
            chain(dve.tensor_tensor(tt, nmr[:, :], mv[:, :, 0], ALU.subtract))
            chain(dve.tensor_tensor(nm2[:, :], tt, t0, ALU.mult))
            chain(dve.tensor_scalar(em[:, :], cst[:, C_IOTA:C_IOTA + NE], float(-NE), None, ALU.add))
            pick_first_max(dve, chain, oh, top, aff, em[:, :], t3, t1, NE)
            dve.engine_nop().then_inc(q["exp1"], 1)
            dve.wait_ge(q["exp2"], 1)
            chain(dve.tensor_scalar(alpha, alpha, 1.0, None, ALU.add))
            chain(dve.reciprocal(alpha, alpha))
            assign_slots(dve, chain, r, (oh,), [slot[:, :]], etile[:, :], NE, NTL1,
                         bank[6][:, 0:NT * NE].rearrange("p (t e) -> p t e", e=NE), bank[7][:, 0:NT * NE].rearrange("p (t e) -> p t e", e=NE),
                         cst, q["mask"], q["rank"])
            dve.engine_nop().then_inc(q["slot"], 1)
            for t in range(NT):
                if t >= 4:
                    dve.wait_ge(sct[t % 4], 16 * (t // 4))
                dve.tensor_scalar(xn[t % 4][:, :], xres[:, t, :], rs2[:, t:t + 1], nm2[:, t:t + 1], ALU.mult, ALU.add).then_inc(q["row"], 1)
            dve.wait_ge(w_in[1], 16 * 7)
            dve.sem_inc(q["yo"], U1)
            with dve.Fori(0, NTL1 // U1) as h:
                es = []
                for u in range(U1):
                    n = h * U1 + u
                    es.append(dve.value_load(etile[0:1, bass.ds(n, 1)], min_val=0, max_val=NE - 1))
                    dve.wait_ge(q["hh"], n + 1)
                    dve.tensor_copy(hs[u][:, 0:512], bank[4 * u][:, :]).then_inc(q["hs1"], 1)
                for u in range(U1):
                    n = h * U1 + u
                    dve.wait_ge(q["t"], n * 2 + 1)
                    for f in range(FB // 2):
                        dve.tensor_scalar(hT[u][:, f, :], bank[4 * u + 2][:, f * P:(f + 1) * P], flat2(b1[:, bass.ds(es[u], 1), f:f + 1]), 0.0,
                                          ALU.add, ALU.max).then_inc(q["ht1"], 1)
                for u in range(U1):
                    n = h * U1 + u
                    dve.wait_ge(q["yp"], n + 1)
                    dve.wait_ge(y_out[u], h * 16 + 16)
                    dve.tensor_tensor(yo[u][:, :], bank[4 * u][:, 0:D], flat2(b2[:, bass.ds(es[u], 1), :]), ALU.add).then_inc(q["yo"], 1)
            for u in range(U1):
                dve.wait_ge(y_out[u], 16 * (NTL1 // U1 + 1))
            add = Chain(dve, q["add"])
            for t in range(NT):
                xt, tmp = xres[:, t, :], yo[t % 2][:, :]
                add(dve.tensor_scalar(tmp, xt, rstd[:, t:t + 1], nmr[:, t:t + 1], ALU.mult, ALU.add))
                add(dve.tensor_tensor(xt, xt, tmp, ALU.add))
                dve.wait_ge(gat[t % 4], 16 * (t // 4 + 1))
                dve.scalar_tensor_tensor(xt, xn[t % 4][:, :], alpha[:, t:t + 1], xt, ALU.mult, ALU.add).then_inc(q["cb"], 1)


def lay_out(inputs):
    w = {n: np.asarray(v) for n, v in inputs.items()}

    def blocks(m):
        return m.reshape(-1, P, m.shape[-1]).transpose(1, 0, 2)

    we = np.concatenate([w["L0_ffn_We1"], w["L0_ffn_We3"]], axis=2)
    return {
        "gate_w": blocks(w["L0_ffn_gate_w"].T),
        "ws1": blocks(w["L0_ffn_ws1"]), "ws3": blocks(w["L0_ffn_ws3"]), "ws2": blocks(w["L0_ffn_ws2"]),
        "bs13": np.stack([w["L0_ffn_bs1"], w["L0_ffn_bs3"]]).reshape(2, KD, P).transpose(2, 0, 1),
        "w13": we.reshape(E0, KD, P, 2 * I0).transpose(2, 1, 0, 3),
        "w2": w["L0_ffn_We2"].transpose(1, 0, 2),
        "wsim": w["L1_xattn_w_sim"].reshape(3, KD, P).transpose(2, 0, 1),
        "b_sim": w["L1_xattn_b_sim"].reshape(1, 1),
        "wqv": w["L1_xattn_W_qv"].reshape(4, KD, P, D).transpose(2, 0, 1, 3),
        "cw": blocks(w["L1_ffn_centroids"].T),
        "l1_w1": w["L1_ffn_w1"].reshape(E1, F1, KD, P).transpose(3, 2, 0, 1),
        "l1_w2": w["L1_ffn_w2"].reshape(E1, D, FB, P).transpose(3, 2, 0, 1),
        "b1": w["L1_ffn_b1"].reshape(E1, FB, P).transpose(2, 0, 1),
        "lgb": np.concatenate([w["L1_ffn_ln_g"].reshape(E1, KD, P), w["L1_ffn_ln_b"].reshape(E1, KD, P)], axis=1).transpose(2, 0, 1),
        "b13": np.concatenate([w["L0_ffn_be1"], w["L0_ffn_be3"]], axis=1),
    }


_INS = ["x", "ctx_1024", "L0_ffn_gate_b", "L0_ffn_bs2", "L0_ffn_be2", "L1_xattn_b_qv", "L1_ffn_b2"]


def kernel(**inputs):
    import concourse.bacc as bacc
    from concourse.bass_utils import run_bass_kernel_spmd

    nc = bacc.Bacc("TRN2", target_bir_lowering=False, num_devices=1)
    arrays, a = {}, {}

    def give(name, arr):
        arr = np.ascontiguousarray(arr)
        arrays[f"in_{name}"] = arr
        a[name] = nc.dram_tensor(f"in_{name}", arr.shape, mybir.dt.from_np(arr.dtype), kind="ExternalInput").ap()

    for name in _INS:
        give(name, inputs[name])
    for name, arr in lay_out(inputs).items():
        give(name, arr)
    give("cst", constants())
    give("zeros", np.zeros((P, 1), np.float32))
    out = nc.dram_tensor("out_0", (B, S, D), F32, kind="ExternalOutput").ap()
    program(nc, a, out)
    r = run_bass_kernel_spmd(nc, [arrays], core_ids=[0])
    return r.results[0]["out_0"]
```

```python
from contextlib import ExitStack

import numpy as np
import concourse.bass as bass
from concourse import mybir

ALU = mybir.AluOpType
ACT = mybir.ActivationFunctionType
AX = mybir.AxisListType
F32 = mybir.dt.float32
I32 = mybir.dt.int32
U32 = mybir.dt.uint32

P = 128
B, S, D = 16, 256, 256
C = 77
TOK = B * S
NT = TOK // P
TPB = S // P
KD = D // P
EPS = 1e-5
BIG = 1e30

LANES = 8
RPL = C // (LANES - 1)
WCOL = 64
NCOL = S // WCOL
STEPS = NCOL + LANES - 2
PADL = WCOL + 1
SKEW = PADL + STEPS * WCOL
assert RPL * (LANES - 1) == C

C_ID, C_TRI, C_ONE, C_IOTA = 0, 128, 256, 384
C_WIDE = C_IOTA + 256


def constants():
    c = np.zeros((P, C_WIDE), np.float32)
    c[:, C_ID:C_ID + P] = np.eye(P)
    c[:, C_TRI:C_TRI + P] = np.triu(np.ones((P, P)), 1)
    c[:, C_ONE:C_ONE + P] = 1.0
    c[:, C_IOTA:C_IOTA + 256] = np.arange(256)
    return c


def flat2b(ap):
    return ap.rearrange("p a b n -> p (a b) n")


def flat3(ap):
    return ap.rearrange("p a k n -> p (a k) n")


def flat2(ap):
    return ap.rearrange("p a n -> p (a n)")


E0, K0, I0 = 16, 2, 128
GRP = 4
U0 = 4
NTL0 = -(-((TOK * K0 + E0 * (P - 1)) // P) // (2 * U0)) * 2 * U0


E1, F1 = 8, 1024
FB = F1 // P
U1 = 2
NTL1 = -(-((TOK + E1 * (P - 1)) // P) // 4) * 4


def pick_first_max(dve, chain, oh, top, v, rev, t3, t1, ne):
    def wide(ap):
        return ap.unsqueeze(2).to_broadcast([P, NT, ne])
    chain(dve.tensor_reduce(top, v, AX.X, ALU.max))
    chain(dve.tensor_tensor(t3, v, wide(top), ALU.is_ge))
    chain(dve.tensor_tensor(t3, t3, rev.unsqueeze(1).to_broadcast([P, NT, ne]), ALU.mult))
    chain(dve.tensor_reduce(t1, t3, AX.X, ALU.min))
    chain(dve.tensor_tensor(oh, rev.unsqueeze(1).to_broadcast([P, NT, ne]), wide(t1), ALU.is_equal))


def assign_slots(dve, chain, r, ohs, slots, etile, ne, ntl, rank_ps, tot_ps, cst, s_mask, s_rank):
    totE, cum, sst, cnt, ti, tl, tend, delta, red, cmp = (r[n] for n in (
        "totE", "cum", "sst", "cnt", "ti", "tl", "tend", "delta", "red", "cmp"))
    t3 = r["t3"]
    if len(ohs) == 2:
        chain(dve.tensor_tensor(r["mask"], ohs[0], ohs[1], ALU.add))
    dve.engine_nop().then_inc(s_mask, 1)
    dve.wait_ge(s_rank, 1)
    chain(dve.tensor_copy(totE.rearrange("p e t -> p t e"), tot_ps))
    flat, cumf = totE.rearrange("p e t -> p (e t)"), cum.rearrange("p e t -> p (e t)")
    chain(dve.tensor_tensor_scan(cumf, flat, flat, 0.0, ALU.add, ALU.max))
    chain(dve.memset(sst[:, 0:1], 0.0))
    chain(dve.tensor_copy(sst[:, 1:ne + 1], cum[:, :, NT - 1]))
    chain(dve.tensor_tensor(cnt, sst[:, 1:ne + 1], sst[:, 0:ne], ALU.subtract))
    chain(dve.tensor_scalar(ti, cnt, float(P - 1), None, ALU.add))
    chain(dve.tensor_scalar(ti, ti, 7, None, ALU.arith_shift_right))
    chain(dve.tensor_copy(tl, ti))
    chain(dve.tensor_tensor_scan(tend, tl, tl, 0.0, ALU.add, ALU.max))
    chain(dve.tensor_tensor(delta, tend, tl, ALU.subtract))
    chain(dve.scalar_tensor_tensor(delta, delta, float(P), sst[:, 0:ne], ALU.mult, ALU.subtract))
    chain(dve.tensor_tensor(cumf, cumf, flat, ALU.subtract))
    chain(dve.tensor_tensor(cum, cum, delta.unsqueeze(2).to_broadcast([P, ne, NT]), ALU.add))
    chain(dve.tensor_tensor(t3, rank_ps, cum.rearrange("p e t -> p t e"), ALU.add))
    for oh, slot in zip(ohs, slots):
        chain(dve.tensor_tensor(totE.rearrange("p e t -> p (e t)").rearrange("p (t e) -> p t e", e=ne), oh, t3, ALU.mult))
        chain(dve.tensor_reduce(red, totE.rearrange("p e t -> p (e t)").rearrange("p (t e) -> p t e", e=ne), AX.X, ALU.add))
        chain(dve.tensor_copy(slot, red))
    chain(dve.tensor_tensor(cmp, tend[0:1, :].unsqueeze(1).to_broadcast([1, ntl, ne]),
                            cst[0:1, C_IOTA:C_IOTA + ntl].unsqueeze(2).to_broadcast([1, ntl, ne]), ALU.is_le))
    chain(dve.tensor_reduce(r["tsum"], cmp, AX.X, ALU.add))
    chain(dve.tensor_scalar(etile, r["tsum"], float(ne - 1), None, ALU.min))


class Chain:

    def __init__(self, eng, sem, base=0):
        self.eng, self.sem, self.base, self.n = eng, sem, base, 0

    def __call__(self, ins):
        self.n += 1
        ins.then_inc(self.sem, 1)
        self.eng.wait_ge(self.sem, self.base + self.n)


def program(nc, a, out, dbg=None):
    with ExitStack() as top:
        build(nc, top, a, out)


def build(nc, top, a, out):
    def sb(ctx, name, shape, dt=F32):
        return ctx.enter_context(nc.sbuf_tensor(name, shape, dt))

    def pb(ctx, name, shape, dt=F32):
        return ctx.enter_context(nc.psum_tensor(name, shape, dt))

    def sem(name):
        return top.enter_context(nc.semaphore(name))

    cst = sb(top, "cst", [P, C_WIDE])
    ident = cst[:, C_ID:C_ID + P]
    xres = sb(top, "xres", [P, NT, D])
    ctx_all = sb(top, "ctx_sb", [P, B, D])
    ctx_sb = ctx_all[0:C, :, :]
    mv = sb(top, "mv", [P, NT, 2])
    rstd = sb(top, "rstd", [P, NT])
    nmr = sb(top, "nmr", [P, NT])
    st6 = sb(top, "st6", [P, NT, 6])
    lnt = sb(top, "lnt", [P, 3, NT])
    rows = [sb(top, f"rows{g}", [P, 4, D]) for g in range(2)]
    slots = [sb(top, f"slot{i}", [P, NT], U32) for i in range(K0)]
    wk = sb(top, "wk", [P, K0, NT])
    s_cst = sem("s_cst")

    x_tok = a["x"].rearrange("b s d -> (b s) d").rearrange("(t p) d -> p t d", p=P)
    out_tok = out.rearrange("b s d -> (b s) d").rearrange("(t p) d -> p t d", p=P)

    def stats_loop(dve, load_sems, s_st):
        per = 8
        if load_sems is None:
            with dve.Fori(0, NT // per) as c:
                for u in range(per):
                    t = c * per + u
                    dve.bn_stats(st6[:, bass.ds(t, 1), :].rearrange("p a s -> p (a s)"),
                                 xres[:, bass.ds(t, 1), :].rearrange("p a d -> p (a d)")).then_inc(s_st, 1)
        else:
            for c in range(NT // per):
                dve.wait_ge(load_sems[c], 16)
                for u in range(per):
                    dve.bn_stats(st6[:, c * per + u, :], xres[:, c * per + u, :]).then_inc(s_st, 1)
        dve.wait_ge(s_st, NT)
        aggregate(dve, s_st, NT)

    def aggregate(dve, s_st, base=0):
        for t in range(NT):
            dve.bn_aggr(mv[:, t, :], st6[:, t, :]).then_inc(s_st, 1)
        dve.wait_ge(s_st, base + NT)

    def norm_tile(dve, dst, t):
        return dve.tensor_scalar(dst, flat2(xres[:, bass.ds(t, 1), :]), rstd[:, bass.ds(t, 1)], nmr[:, bass.ds(t, 1)],
                                 ALU.mult, ALU.add)

    def rstd_steps(dve, chain, s_var, s_root):
        ve, t0, t1 = lnt[:, 0, :], lnt[:, 1, :], lnt[:, 2, :]
        dve.tensor_scalar(ve, mv[:, :, 1], EPS, None, ALU.add).then_inc(s_var, 1)
        dve.wait_ge(s_root, 1)
        chain(dve.reciprocal(t1, t0))
        chain(dve.tensor_tensor(t1, ve, t1, ALU.mult))
        chain(dve.tensor_tensor(t1, t1, t0, ALU.add))
        chain(dve.tensor_scalar(t1, t1, 0.5, None, ALU.mult))
        chain(dve.reciprocal(rstd[:, :], t1))
        chain(dve.scalar_tensor_tensor(nmr[:, :], mv[:, :, 0], -1.0, rstd[:, :], ALU.mult, ALU.mult))

    xs0 = nc.dram_tensor("xs0", [NTL0 * P, D], F32).ap()
    ys0 = nc.dram_tensor("ys0", [NTL0 * P, D], F32).ap()
    xs1 = nc.dram_tensor("xs1", [NTL1 * P, D], F32).ap()
    ys1 = nc.dram_tensor("ys1", [NTL1 * P, D], F32).ap()
    s_zero = sem("s_zero")
    n_zero = (NTL0 + NTL1) * D // 1024

    def zero_fill(sp, zbuf):
        for rows in (xs0, xs1):
            v = rows.rearrange("(p r) d -> p (r d)", p=P)
            for c in range(v.shape[1] // 1024):
                sp.dma_start(v[:, c * 1024:(c + 1) * 1024], zbuf[:, :]).then_inc(s_zero, 16)

    with ExitStack() as warp_sems:
        old_sems = []

        def warp_sem(name):
            old_sems.append(warp_sems.enter_context(nc.semaphore(name)))
            return old_sems[-1]

        phase_warp(nc, a, out_tok, locals())
        phase_moe0(nc, a, out_tok, locals())
    with ExitStack() as late:
        l1_w1 = sb(late, "l1_w1", [P, KD, E1, F1])
        s_w1 = sem("s_w1")
        phase_xattn(nc, a, out_tok, locals())
        phase_moe1(nc, a, out_tok, locals())


def phase_warp(nc, a, out_tok, k):
    sb, pb, sem = k["sb"], k["pb"], k["warp_sem"]
    cst, ident, xres, rstd, nmr, lnt, st6 = (k[n] for n in ("cst", "ident", "xres", "rstd", "nmr", "lnt", "st6"))
    x_tok, s_cst = k["x_tok"], k["s_cst"]
    with ExitStack() as ctx:
        ctx_sb = k["ctx_sb"]
        DSK = RPL * STEPS * WCOL
        RSK = (RPL + 1) * SKEW
        CH = (LANES - 1) * RPL * S
        arena = sb(ctx, "w_arena", [P, max(DSK + RSK, CH)])
        dskew = arena[:, 0:DSK].rearrange("p (r w) -> p r w", r=RPL)
        rskew = arena[:, DSK:DSK + RSK].rearrange("p (r w) -> p r w", r=RPL + 1)
        chain_tab = arena[0:B, 0:CH].rearrange("p (r w) -> p r w", w=S)
        rrow = sb(ctx, "w_rrow", [P, RPL + 1, S + 1])
        up = sb(ctx, "w_up", [P, RPL, S])
        gv = sb(ctx, "w_gv", [P, RPL, S])
        jr = sb(ctx, "w_jr", [P, RPL, S])
        junk = sb(ctx, "w_junk", [B, S])
        c2 = sb(ctx, "w_c2", [B, C + 1])
        cs = sb(ctx, "w_cs", [C, 2, B])
        minw = sb(ctx, "w_min", [P, WCOL])
        zbuf = sb(ctx, "w_zbuf", [P, 1024])
        aa = sb(ctx, "w_aa", [C, B])
        iota15 = sb(ctx, "w_iota15", [C, S])
        iota2 = sb(ctx, "w_iota2", [C, S])
        halfneg = sb(ctx, "w_halfneg", [P, C])
        xn = [k["rows"][u][:, 0:TPB, :] for u in range(2)]
        xT = [sb(ctx, f"w_xT{u}", [P, KD, S]) for u in range(2)]
        xsq = [k["rows"][u][:, TPB:TPB + KD, :] for u in range(2)]
        cT = [sb(ctx, f"w_cT{u}", [P, KD, C]) for u in range(2)]
        d2 = [sb(ctx, f"w_d2{u}", [C, S]) for u in range(2)]
        y0 = [sb(ctx, f"w_y0{u}", [C, S]) for u in range(2)]
        ysq = [sb(ctx, f"w_ysq{u}", [C, S]) for u in range(2)]
        ri = [sb(ctx, f"w_ri{u}", [C, S]) for u in range(2)]
        path = [sb(ctx, f"w_path{u}", [C, S]) for u in range(2)]
        pm = [k["rows"][u][0:C, 0, :] for u in range(2)]
        tpx = [pb(ctx, f"w_tpx{u}", [P, KD, S]) for u in range(2)]
        tpc = [pb(ctx, f"w_tpc{u}", [P, KD, S]) for u in range(2)]
        dps = [pb(ctx, f"w_dps{u}", [P, 2 * S]) for u in range(2)]
        xps = tpx
        dscr = nc.dram_tensor("dscr", [B, C, S], F32).ap()

        x_in = [sem(f"w_x_in{c}") for c in range(4)]
        c_in = sem("w_c_in")
        s_st, s_var, s_root, s_dve = sem("w_st"), sem("w_var"), sem("w_root"), sem("w_dve")
        s_init = sem("w_init")
        s_ln, s_xnp, s_tp, s_xT, s_sq, s_dd, s_d2 = (sem("w_" + n) for n in ("ln", "xn", "tp", "xT", "sq", "dd", "d2"))
        s_y0, s_ysq, s_res, s_ri, s_cor, s_y = (sem("w_" + n) for n in ("y0", "ysq", "res", "ri", "cor", "y"))
        s_aa, s_cT, s_ctp, s_cTs = sem("w_aa_s"), sem("w_cT_s"), sem("w_ctp"), sem("w_cTs")
        d_out = [sem(f"w_d_out{u}") for u in range(2)]
        d_in, s_dp, s_dpm, r_un, s_g, t_in, s_c2, s_c2t, s_cs = (
            sem("w_" + n) for n in ("d_in", "dp", "dpm", "r_un", "g", "t_in", "c2_s", "c2t", "cs_s"))
        s_pm, s_path, s_ex, s_add, s_dmp, s_gch, s_bt = (sem("w_" + n) for n in ("pm_s", "path_s", "ex", "add", "dmp", "gch", "bt"))
        s_corner, s_st2 = k["sem"]("w_corner"), sem("w_st2")
        s_zb = sem("w_zb")

        block = ctx.enter_context(nc.Block())

        @block.sync
        def _(sp):
            sp.dma_start(cst[:, :], a["cst"]).then_inc(s_cst, 16)
            for c in range(4):
                sp.dma_start(xres[:, 8 * c:8 * c + 8, :], x_tok[:, 8 * c:8 * c + 8, :]).then_inc(x_in[c], 16)
            sp.dma_start(ctx_sb[:, :, :], a["ctx_1024"].rearrange("b i d -> i b d")).then_inc(c_in, 16)
            with sp.Fori(0, B // 2) as h:
                for u in range(2):
                    sp.wait_ge(s_y, h * 2 + u + 1)
                    sp.dma_start(dscr[bass.ds(h * 2 + u, 1), :, :].rearrange("a i j -> (a i) j"),
                                 ysq[u][:, :]).then_inc(d_out[u], 16)
            for u in range(2):
                sp.wait_ge(d_out[u], 16 * (B // 2))
            sp.wait_ge(s_init, 2)
            for lane in range(1, LANES):
                sp.dma_start(dskew[lane::LANES, :, WCOL * (lane - 1):WCOL * (lane - 1) + S],
                             dscr[:, RPL * (lane - 1):RPL * lane, :]).then_inc(d_in, 16)
            sp.wait_ge(s_zb, 1)
            k["zero_fill"](sp, zbuf)
            sp.wait_ge(s_dp, STEPS * (2 * RPL + 1))
            for lane in range(LANES):
                o = PADL - 1 + WCOL * max(lane - 1, 0)
                sp.dma_start(rrow[lane::LANES, :, :], rskew[lane::LANES, :, o:o + S + 1]).then_inc(r_un, 16)
            sp.wait_ge(s_gch, 8)
            for lane in range(LANES - 1, 0, -1):
                sp.dma_start(chain_tab[:, RPL * (lane - 1):RPL * lane, :], gv[lane::LANES, :, :]).then_inc(t_in, 16)
            sp.wait_ge(k["s_zero"], 16 * k["n_zero"])

        @block.gpsimd
        def _(pool):
            pool.memset(zbuf[:, :], 0.0).then_inc(s_zb, 1)
            pool.memset(dskew, BIG).then_inc(s_init, 1)
            pool.memset(rskew, BIG).then_inc(s_init, 1)
            pool.iota(jr[:, :, :], pattern=[[512, RPL], [1, S]], base=1, channel_multiplier=0,
                      allow_small_or_imprecise_dtypes=True).then_inc(s_dmp, 1)
            pool.wait_ge(s_init, 2)
            pool.dma_start(rskew[1::LANES, 0, PADL - 1:PADL], a["zeros"][0:B, :]).then_inc(s_corner, 16)

            def squares(b, u):
                pool.wait_ge(s_xT, b + 1)
                pool.tensor_tensor(xsq[u], xT[u][:, :, :], xT[u][:, :, :], ALU.mult).then_inc(s_sq, 1)

            def residual(b, u):
                pool.wait_ge(s_ysq, b + 1)
                pool.tensor_tensor(d2[u][:, :], d2[u][:, :], ysq[u][:, :], ALU.subtract).then_inc(s_res, 1)
                pool.wait_ge(s_cor, b + 1)
                pool.tensor_tensor(ysq[u][:, :], y0[u][:, :], d2[u][:, :], ALU.add).then_inc(s_y, 1)

            squares(0, 0)
            squares(1, 1)
            residual(0, 0)
            with pool.Fori(1, B // 2) as h:
                squares(h * 2, 0)
                residual(h * 2 - 1, 1)
                squares(h * 2 + 1, 1)
                residual(h * 2, 0)
            residual(B - 1, 1)

        @block.scalar
        def _(act):
            act.wait_ge(c_in, 16)
            for b in range(B):
                if b >= 2:
                    act.wait_ge(s_aa, b - 1)
                act.activation(ysq[b % 2][:, :], ctx_sb[:, b, :], ACT.Square, accum_out=aa[:, b:b + 1]).then_inc(s_aa, 1)
            act.wait_ge(s_var, 1)
            act.activation(lnt[:, 1, :], lnt[:, 0, :], ACT.Sqrt).then_inc(s_root, 1)
            act.wait_ge(s_aa, B)

            def root(b, u, fresh=False):
                act.wait_ge(s_dd, b + 1)
                if not fresh:
                    act.wait_ge(s_y, b - 1)
                act.activation(d2[u][:, :], dps[u][0:C, 0:S], ACT.Relu, bias=aa[:, bass.ds(b, 1)], scale=-2.0).then_inc(s_d2, 1)
                act.wait_ge(s_d2, b + 1)
                act.activation(y0[u][:, :], d2[u][:, :], ACT.Sqrt).then_inc(s_y0, 1)
                act.wait_ge(s_y0, b + 1)
                if not fresh:
                    act.wait_ge(d_out[u], (b - u) * 8)
                act.activation(ysq[u][:, :], y0[u][:, :], ACT.Square).then_inc(s_ysq, 1)

            root(0, 0, fresh=True)
            root(1, 1, fresh=True)
            with act.Fori(1, B // 2) as h:
                root(h * 2, 0)
                root(h * 2 + 1, 1)

        @block.tensor
        def _(pe):
            pe.wait_ge(s_cst, 16)
            pe.wait_ge(c_in, 16)

            def turn(b, u, fresh=False):
                if not fresh:
                    pe.wait_ge(s_cTs, b - 1)
                pe.wait_ge(s_ctp, b + 1)
                for i in range(TPB):
                    for kb in range(KD):
                        ins = pe.transpose(tpx[u][:, kb, i * P:(i + 1) * P], xn[u][:, i, kb * P:(kb + 1) * P], ident)
                ins.then_inc(s_tp, 1)
                for kb in range(KD):
                    ins = pe.transpose(tpc[u][:, kb, 0:C], path[u][:, kb * P:(kb + 1) * P], ident[0:C, 0:C])
                ins.then_inc(s_cT, 1)

            def products(b, u, fresh=False):
                if not fresh:
                    pe.wait_ge(s_d2, b - 1)
                pe.wait_ge(s_cTs, b + 1)
                for kb in range(KD):
                    pe.matmul(dps[u][0:C, 0:S], cT[u][:, kb, :], xT[u][:, kb, :], start=(kb == 0), stop=False)
                pe.wait_ge(s_sq, b + 1)
                for kb in range(KD):
                    ins = pe.matmul(dps[u][0:C, 0:S], halfneg[:, :], xsq[u][:, kb, :], start=False, stop=(kb == KD - 1))
                ins.then_inc(s_dd, 1)

            pe.wait_ge(s_bt, 1)
            turn(0, 0, fresh=True)
            turn(1, 1, fresh=True)
            products(0, 0, fresh=True)
            turn(2, 0)
            products(1, 1, fresh=True)
            with pe.Fori(1, B // 2 - 1) as h:
                turn(h * 2 + 1, 1)
                products(h * 2, 0)
                turn(h * 2 + 2, 0)
                products(h * 2 + 1, 1)
            turn(B - 1, 1)
            products(B - 2, 0)
            products(B - 1, 1)
            pe.wait_ge(s_c2, 1)
            pe.transpose(tpx[0][0:C, 0, 0:B], c2[:, 0:C], ident[0:B, 0:B])
            pe.transpose(tpx[0][0:C, 0, B:2 * B], c2[:, 1:C + 1], ident[0:B, 0:B]).then_inc(s_c2t, 1)
            def expand(b, u, fresh=False):
                if not fresh:
                    pe.wait_ge(s_add, b - 1)
                pe.wait_ge(s_path, b + 1)
                for i in range(TPB):
                    ins = pe.matmul(xps[u][:, i, :], path[u][:, i * P:(i + 1) * P],
                                    ctx_sb[:, bass.ds(b, 1), :].rearrange("p a d -> p (a d)"), start=True, stop=True)
                ins.then_inc(s_ex, 1)

            expand(0, 0, fresh=True)
            expand(1, 1, fresh=True)
            with pe.Fori(1, B // 2) as h:
                expand(h * 2, 0)
                expand(h * 2 + 1, 1)

        @block.vector
        def _(dve):
            dve.memset(halfneg[:, :], -0.5).then_inc(s_bt, 1)
            chain = Chain(dve, s_dve)
            dve.wait_ge(s_cst, 16)
            dve.tensor_scalar(iota15[:, :], cst[0:C, C_IOTA:C_IOTA + S], 1.5, None, ALU.add).then_inc(s_bt, 1)
            dve.tensor_scalar(iota2[:, :], cst[0:C, C_IOTA:C_IOTA + S], 2.0, None, ALU.add).then_inc(s_bt, 1)
            k["stats_loop"](dve, x_in, s_st)
            k["rstd_steps"](dve, chain, s_var, s_root)
            dve.wait_ge(c_in, 16)

            def fetch(b, u):
                for i in range(TPB):
                    k["norm_tile"](dve, xn[u][:, i, :], b * TPB + i)
                dve.tensor_copy(path[u][:, :], flat2(ctx_sb[:, bass.ds(b, 1), :])).then_inc(s_ctp, 1)

            def turned(b, u):
                dve.wait_ge(s_tp, b + 1)
                dve.tensor_copy(xT[u][:, :, :], tpx[u][:, :, :]).then_inc(s_xT, 1)
                dve.wait_ge(s_cT, b + 1)
                dve.tensor_copy(cT[u][:, :, :], tpc[u][:, :, 0:C]).then_inc(s_cTs, 1)

            def correction(b, u):
                dve.wait_ge(s_y0, b + 1)
                dve.tensor_scalar(ri[u][:, :].bitcast(I32), y0[u][:, :].bitcast(I32), -1.0, float(0x7EF311C7),
                                  ALU.mult, ALU.add).then_inc(s_ri, 1)
                dve.wait_ge(s_ri, b + 1)
                dve.wait_ge(s_res, b + 1)
                dve.scalar_tensor_tensor(d2[u][:, :], d2[u][:, :], 0.5, ri[u][:, :], ALU.mult, ALU.mult).then_inc(s_cor, 1)

            fetch(0, 0)
            fetch(1, 1)
            turned(0, 0)
            fetch(2, 0)
            turned(1, 1)
            fetch(3, 1)
            correction(0, 0)
            with dve.Fori(1, B // 2 - 1) as h:
                turned(h * 2, 0)
                fetch(h * 2 + 2, 0)
                correction(h * 2 - 1, 1)
                turned(h * 2 + 1, 1)
                fetch(h * 2 + 3, 1)
                correction(h * 2, 0)
            turned(B - 2, 0)
            correction(B - 3, 1)
            turned(B - 1, 1)
            correction(B - 2, 0)
            correction(B - 1, 1)
            dve.wait_ge(d_in, 16 * (LANES - 1))
            dve.wait_ge(s_corner, 16)
            dp = Chain(dve, s_dp)
            mask = [max(q - 1, 0) for q in range(32)]
            for s in range(STEPS):
                o = s * WCOL + PADL
                dp(dve.stream_shuffle(rskew[:, 0, o:o + WCOL], rskew[:, RPL, o - WCOL:o], mask))
                for r in range(RPL):
                    dp(dve.tensor_tensor(minw[:, :], rskew[:, r, o:o + WCOL], rskew[:, r, o - 1:o + WCOL - 1], ALU.min))
                    dp(dve.tensor_tensor_scan(rskew[:, r + 1, o:o + WCOL], minw[:, :], dskew[:, r, s * WCOL:(s + 1) * WCOL],
                                              rskew[:, r + 1, o - 1:o], ALU.min, ALU.add))
            g = Chain(dve, s_gch)
            dve.wait_ge(r_un, 16 * LANES)
            dve.wait_ge(s_dmp, 1)
            over, diag, left = rrow[:, 0:RPL, 1:S + 1], rrow[:, 0:RPL, 0:S], rrow[:, 1:RPL + 1, 0:S]
            g(dve.tensor_tensor(up[:, :, :], over, diag, ALU.is_lt))
            g(dve.scalar_tensor_tensor(up[:, :, :], up[:, :, :], 0.75, jr[:, :, :], ALU.mult, ALU.add))
            g(dve.tensor_tensor(gv[:, :, :], over, diag, ALU.min))
            g(dve.tensor_tensor(gv[:, :, :], gv[:, :, :], left, ALU.is_le))
            g(dve.tensor_tensor(up[:, :, :], up[:, :, :], gv[:, :, :], ALU.mult))
            flat = up[:, :, :].rearrange("p r w -> p (r w)")
            runs = rrow[:, :, :].rearrange("p r w -> p (r w)")[:, 0:RPL * S]
            g(dve.tensor_tensor_scan(runs, flat, flat, 0.0, ALU.max, ALU.max))
            run3 = runs.rearrange("p (r w) -> p r w", w=S)
            g(dve.tensor_tensor(gv[:, :, 1:S], run3[:, :, 1:S], run3[:, :, 0:S - 1], ALU.subtract))
            g(dve.scalar_tensor_tensor(gv[:, :, 0:1], run3[:, :, 0:1], 1.0, jr[:, :, 0:1], ALU.add, ALU.subtract))
            dve.memset(c2[:, :], float(S + 1)).then_inc(s_bt, 1)
            for lane in range(LANES - 1, 0, -1):
                dve.wait_ge(t_in, 16 * (LANES - 1))
                for r in range(RPL - 1, -1, -1):
                    i = RPL * (lane - 1) + r
                    dve.wait_ge(s_bt, 4 + C - 1 - i)
                    dve.scalar_tensor_tensor(junk[:, :], iota15[0:B, :], c2[:, i + 1:i + 2], chain_tab[:, i, :],
                                             ALU.is_le, ALU.mult, accum_out=c2[:, i:i + 1]).then_inc(s_bt, 1)
            dve.wait_ge(s_bt, 4 + C)
            dve.engine_nop().then_inc(s_c2, 1)
            dve.wait_ge(s_c2t, 1)
            dve.tensor_copy(cs[:, :, :], tpx[0][0:C, 0, 0:2 * B].rearrange("p (a b) -> p a b", a=2)).then_inc(s_cs, 1)
            dve.wait_ge(s_cs, 1)
            def paths(b, u):
                dve.tensor_scalar(pm[u], iota2[:, :], cs[:, 0, bass.ds(b, 1)], None, ALU.is_gt).then_inc(s_pm, 1)
                dve.wait_ge(s_pm, b + 1)
                dve.scalar_tensor_tensor(path[u][:, :], iota15[:, :], cs[:, 1, bass.ds(b, 1)], pm[u],
                                         ALU.is_le, ALU.mult).then_inc(s_path, 1)

            def add_rows(b, u, first=False):
                if not first:
                    dve.wait_ge(s_add, b)
                dve.wait_ge(s_ex, b + 1)
                xb = xres[:, bass.ds(b * TPB, TPB), :]
                dve.tensor_tensor(xb, xps[u][:, :, :], xb, ALU.add).then_inc(s_add, 1)
                if not first:
                    stats(b - 1)

            def stats(b):
                for i in range(TPB):
                    t = b * TPB + i
                    dve.bn_stats(flat2(st6[:, bass.ds(t, 1), :]), flat2(xres[:, bass.ds(t, 1), :])).then_inc(s_st2, 1)

            paths(0, 0)
            paths(1, 1)
            add_rows(0, 0, first=True)
            paths(2, 0)
            add_rows(1, 1)
            with dve.Fori(1, B // 2 - 1) as h:
                paths(h * 2 + 1, 1)
                add_rows(h * 2, 0)
                paths(h * 2 + 2, 0)
                add_rows(h * 2 + 1, 1)
            paths(B - 1, 1)
            add_rows(B - 2, 0)
            add_rows(B - 1, 1)
            dve.wait_ge(s_add, B)
            stats(B - 1)


def phase_moe0(nc, a, out_tok, k):
    sb, pb, sem = k["sb"], k["pb"], k["sem"]
    cst, ident, xres, rstd, nmr, lnt = (k[n] for n in ("cst", "ident", "xres", "rstd", "nmr", "lnt"))
    xs, ys, rows, slots, wk = (k[n] for n in ("xs0", "ys0", "rows", "slots", "wk"))
    NE, G4 = E0, E0 // GRP
    NG = TOK // 512
    with ExitStack() as ctx:
        w13 = sb(ctx, "e_w13", [P, KD, NE, 2 * I0])
        w2 = sb(ctx, "e_w2", [P, NE, D])
        b13 = sb(ctx, "e_b13", [P, NE, 2 * I0])
        b2 = sb(ctx, "e_b2", [P, NE, D])
        ws1 = sb(ctx, "e_ws1", [P, KD, 2 * I0])
        ws3 = sb(ctx, "e_ws3", [P, KD, 2 * I0])
        ws2 = sb(ctx, "e_ws2", [P, KD, D])
        bs13 = sb(ctx, "e_bs13", [P, 2, KD])
        bs2 = sb(ctx, "e_bs2", [P, D])
        gw = sb(ctx, "e_gw", [P, KD, NE])
        gb = sb(ctx, "e_gb", [P, NE])
        xT = sb(ctx, "e_xT", [P, NG, KD * 512])
        xT4 = xT[:, :, :].rearrange("p g (k n) -> p g k n", k=KD)
        EARLY = 3
        xn = [rows[0][:, u, :] for u in range(4)]
        arena = sb(ctx, "e_arena", [P, 3072])
        shared_buf = [sb(ctx, f"e_sh{i}", [P, 1024]) for i in range(2)]
        gsh, ssh = ([buf[:, 512 * i:512 * i + 512] for i in range(KD)] for buf in shared_buf)
        gate_xT = shared_buf[0][:, :].rearrange("p (u k n) -> p u k n", u=4, k=KD)
        def expert_buf(o, w):
            flat = xT[:, :, :].rearrange("p g n -> p (g n)")
            return [flat[:, o + w * g:o + w * (g + 1)].rearrange("p (u n) -> p u n", u=U0) for g in range(2)]
        xinT = [v.rearrange("p u (k n) -> p u k n", k=KD) for v in expert_buf(0, 1024)]
        yo, hb, sg, gT = expert_buf(2048, 1024), expert_buf(4096, 1024), expert_buf(6144, 512), expert_buf(7168, 512)
        big = [arena[:, 512 * i:512 * i + 512].rearrange("p (t e) -> p t e", e=NE) for i in range(6)]
        sr, scb, oh1, oh2, t3, mask = big[0], big[1], big[2], big[3], big[4], big[5]
        small = sb(ctx, "e_small", [P, 8, NT * G4])
        em = sb(ctx, "e_em", [P, NE])
        mx, t1 = small[:, 0, 0:NT], small[:, 1, 0:NT]
        etile = sb(ctx, "e_etile", [1, NTL0], I32)
        r = {"totE": sr.rearrange("p t e -> p (t e)").rearrange("p (e t) -> p e t", e=NE), "t3": t3, "mask": mask,
             "cum": scb.rearrange("p t e -> p (t e)").rearrange("p (e t) -> p e t", e=NE), "sst": sb(ctx, "e_sst", [P, NE + 1])[:, :],
             "ti": sb(ctx, "e_ti", [P, NE], I32)[:, :], "red": small[:, 2, 0:NT],
             "cmp": arena[0:1, 0:NTL0 * NE].rearrange("p (t e) -> p t e", e=NE), "tsum": sb(ctx, "e_tsum", [1, NTL0])[:, :]}
        for i, n in enumerate(("cnt", "tl", "tend", "delta")):
            r[n] = small[:, 3 + i, 0:NE]
        bank = [pb(ctx, f"e_bank{u}", [P, 512]) for u in range(8)]

        w_in = [sem(f"e_w_in{i}") for i in range(5)]
        (s_st, s_var, s_root, s_dve, s_xn, s_tp, s_xT, s_xTall, s_gs, s_gate, s_exp, s_max, s_mask, s_rank, s_slot) = (
            sem("e_" + n) for n in ("st", "var", "root", "dve", "xn_s", "tp", "xT_s", "xTall", "gs", "gate", "exp", "max",
                                    "mask", "rank", "slot"))
        s_h1, s_si, s_h3, s_gsh, s_zp, s_z, s_row = (sem("e_" + n) for n in ("h1", "si", "h3", "gsh_s", "zp", "z", "row"))
        sct = [sem(f"e_sct{u}") for u in range(4)]
        x_in = [sem(f"e_x_in{g}") for g in range(2)]
        y_out = [sem(f"e_y_out{g}") for g in range(2)]
        s_xt, s_xe, s_hh, s_hb, s_sg, s_g, s_gt, s_ge, s_yp, s_yo = (
            sem("e_" + n) for n in ("xt", "xe", "hh", "hb_s", "sg_s", "g", "gt", "ge", "yp", "yo_s"))
        s_c0, s_gpool = sem("e_c0"), sem("e_gpool")

        NH = NTL0 // (2 * U0)

        def first(h, g):
            return h * (2 * U0) + g * U0

        def experts(eng, h, g):
            return [eng.value_load(etile[0:1, bass.ds(first(h, g) + u, 1)], min_val=0, max_val=NE - 1) for u in range(U0)]

        block = ctx.enter_context(nc.Block())

        @block.sync
        def _(sp):
            for old in k["old_sems"]:
                sp.sem_clear(old)
            sp.dma_start(gw[:, :, :], a["gate_w"]).then_inc(w_in[0], 16)
            sp.dma_start(gb[:, :], a["L0_ffn_gate_b"].partition_broadcast(P)).then_inc(w_in[0], 16)
            for dst, name in ((ws1, "ws1"), (ws3, "ws3"), (ws2, "ws2")):
                sp.dma_start(dst[:, :, :], a[name]).then_inc(w_in[1], 16)
            sp.dma_start(bs13[:, :, :], a["bs13"]).then_inc(w_in[1], 16)
            sp.dma_start(bs2[:, :], a["L0_ffn_bs2"].partition_broadcast(P)).then_inc(w_in[2], 16)
            sp.dma_start(w13[:, :, :, :], a["w13"]).then_inc(w_in[3], 16)
            sp.dma_start(w2[:, :, :], a["w2"]).then_inc(w_in[3], 16)
            sp.dma_start(b13[:, :, :].rearrange("p e n -> p (e n)"),
                         a["b13"].rearrange("e n -> (e n)").partition_broadcast(P)).then_inc(w_in[3], 16)
            sp.dma_start(b2[:, :, :].rearrange("p e n -> p (e n)"),
                         a["L0_ffn_be2"].rearrange("e n -> (e n)").partition_broadcast(P)).then_inc(w_in[4], 16)
            for u in range(4):
                sp.wait_ge(sct[u], 16 * K0 * NT // 4)

            def tiles(dram, h, g):
                return dram[bass.ds(first(h, g) * P, U0 * P), :].rearrange("(u p) d -> p u d", p=P)

            def load(h, g):
                sp.dma_start(rows[g][:, :, :], tiles(xs, h, g)).then_inc(x_in[g], 16)

            def reload(h, g):
                sp.wait_ge(s_xt, first(h - 1, g) + U0)
                load(h, g)

            def store(h, g):
                sp.wait_ge(s_yo, first(h, g) + U0)
                sp.dma_start(tiles(ys, h, g), yo[g]).then_inc(y_out[g], 16)

            load(0, 0)
            load(0, 1)
            reload(1, 0)
            reload(1, 1)
            store(0, 0)
            with sp.Fori(2, NH) as h:
                reload(h, 0)
                store(h - 2, 1)
                reload(h, 1)
                store(h - 1, 0)
            store(NH - 2, 1)
            store(NH - 1, 0)
            store(NH - 1, 1)
            for g in range(2):
                sp.wait_ge(y_out[g], 16 * NH)

        @block.gpsimd
        def _(pool):
            with pool.Fori(0, EARLY) as g:
                for i in range(KD):
                    pool.wait_ge(s_si, g * 4 + 2 * i + 2)
                    pool.tensor_tensor(gsh[i], gsh[i], ssh[i], ALU.mult).then_inc(s_gpool, 1)
            pool.wait_ge(s_slot, 1)
            for t in range(NT):
                pool.wait_ge(s_row, t + 1)
                for i in range(K0):
                    pool.indirect_dma_start(out=xs, out_offset=bass.IndirectOffsetOnAxis(ap=slots[i][:, t:t + 1], axis=0),
                                            in_=xn[t % 4], in_offset=None).then_inc(sct[t % 4], 16)

        @block.scalar
        def _(act):
            act.wait_ge(s_var, 1)
            act.activation(lnt[:, 1, :], lnt[:, 0, :], ACT.Sqrt).then_inc(s_root, 1)
            with act.Fori(0, NG) as g:
                for q in range(4):
                    act.wait_ge(s_tp, g * 4 + q + 1)
                    act.copy(flat3(xT4[:, bass.ds(g, 1), :, q * P:(q + 1) * P]),
                             bank[q][:, 0:D].rearrange("p (k n) -> p k n", k=KD)).then_inc(s_xTall, 1)
            act.wait_ge(s_max, 1)
            act.activation(scb, sr, ACT.Exp).then_inc(s_exp, 1)
            act.wait_ge(w_in[1], 64)
            with act.Fori(0, NG) as g:
                for i in range(KD):
                    act.wait_ge(s_h1, g * 4 + 2 * i + 1)
                    act.activation(ssh[i], bank[2 * i][:, :], ACT.Silu, bias=bs13[:, 0, i:i + 1]).then_inc(s_si, 1)
                    act.wait_ge(s_h1, g * 4 + 2 * i + 2)
                    act.activation(gsh[i], bank[2 * i + 1][:, :], ACT.Identity, bias=bs13[:, 1, i:i + 1]).then_inc(s_si, 1)
                for q in range(2):
                    act.wait_ge(s_zp, g * 2 + q + 1)
                    act.copy(flat2(xT[:, bass.ds(g, 1), q * 512:(q + 1) * 512]), bank[4 + q][:, :]).then_inc(s_z, 1)

            def turned_in(h, g):
                for u in range(U0):
                    act.wait_ge(s_xt, first(h, g) + u + 1)
                    act.copy(xinT[g][:, u, :, :], bank[4 * g + u][:, 0:D].rearrange("p (k n) -> p k n", k=KD)).then_inc(s_xe, 1)

            def silu(h, g):
                for u in range(U0):
                    act.wait_ge(s_hb, first(h, g) + u + 1)
                    act.activation(sg[g][:, u, :], hb[g][:, u, 0:I0], ACT.Silu).then_inc(s_sg, 1)

            def turned_gated(h, g):
                for u in range(U0):
                    act.wait_ge(s_gt, first(h, g) + u + 1)
                    act.copy(gT[g][:, u, :], bank[4 * g + u][:, 0:P]).then_inc(s_ge, 1)

            def half(h, g, h_before, g_before):
                turned_gated(h_before, g_before)
                turned_in(h, g)
                silu(h, g)

            turned_in(0, 0)
            silu(0, 0)
            half(0, 1, 0, 0)
            with act.Fori(1, NH) as h:
                half(h, 0, h - 1, 1)
                half(h, 1, h, 0)
            turned_gated(NH - 1, 1)

        @block.tensor
        def _(pe):
            pe.wait_ge(w_in[0], 32)
            with pe.Fori(0, NT // 4) as h:
                for q in range(4):
                    pe.wait_ge(s_xn, h * 4 + q + 1)
                    for kb in range(KD):
                        ins = pe.transpose(bank[q][:, kb * P:(kb + 1) * P], xn[q][:, kb * P:(kb + 1) * P], ident)
                    ins.then_inc(s_tp, 1)
                for q in range(4):
                    pe.wait_ge(s_xT, h * 4 + q + 1)
                    for kb in range(KD):
                        ins = pe.matmul(bank[4 + q][:, 0:NE], gate_xT[:, q, kb, :], gw[:, kb, :], start=(kb == 0), stop=(kb == KD - 1))
                    ins.then_inc(s_gs, 1)
            pe.wait_ge(w_in[1], 64)
            pe.wait_ge(s_xTall, NT)
            pe.wait_ge(s_gate, NT)

            def shared(g, s_gated, g_gated, fresh=False):
                for i in range(KD):
                    for j, w in enumerate((ws1, ws3)):
                        for kb in range(KD):
                            ins = pe.matmul(bank[2 * i + j][:, :], w[:, kb, i * P:(i + 1) * P],
                                            flat2(flat2b(xT4[:, bass.ds(g, 1), kb:kb + 1, :])), start=(kb == 0), stop=(kb == KD - 1))
                        ins.then_inc(s_h1, 1)
                for q in range(4):
                    if q == 0 and not fresh:
                        pe.wait_ge(s_z, g * 2)
                    for i in range(KD):
                        pe.wait_ge(s_gated, (g_gated * 2) + i + 1)
                        ins = pe.matmul(bank[4 + q // 2][:, (q % 2) * D:(q % 2 + 1) * D], gsh[i][:, q * P:(q + 1) * P], ws2[:, i, :],
                                        start=(i == 0), stop=(i == KD - 1))
                    if q % 2 == 1:
                        ins.then_inc(s_zp, 1)

            shared(0, s_gpool, 0, fresh=True)
            with pe.Fori(1, EARLY - 1) as g:
                shared(g, s_gpool, g)
            pe.wait_ge(s_mask, 1)
            pe.matmul(bank[6][:, :], cst[:, C_TRI:C_TRI + P], mask.rearrange("p t e -> p (t e)"), start=True, stop=True)
            pe.matmul(bank[7][:, :], cst[:, C_ONE:C_ONE + P], mask.rearrange("p t e -> p (t e)"), start=True, stop=True).then_inc(s_rank, 1)
            shared(EARLY - 1, s_gpool, EARLY - 1)
            with pe.Fori(EARLY, NG) as g:
                shared(g, s_gsh, g - EARLY)
            pe.wait_ge(w_in[3], 48)
            pe.wait_ge(s_z, 2 * NG)
            pe.wait_ge(s_slot, 1)
            pe.wait_ge(s_c0, 2 * NG)

            def turn_in(h, g, fresh=False):
                pe.wait_ge(x_in[g], h * 16 + 16)
                for u in range(U0):
                    if not fresh:
                        pe.wait_ge(s_yo, first(h - 1, g) + u + 1)
                    for kb in range(KD):
                        ins = pe.transpose(bank[4 * g + u][:, kb * P:(kb + 1) * P], rows[g][:, u, kb * P:(kb + 1) * P], ident)
                    ins.then_inc(s_xt, 1)

            def h13(h, g, es):
                for u in range(U0):
                    pe.wait_ge(s_xe, first(h, g) + u + 1)
                    for kb in range(KD):
                        ins = pe.matmul(bank[4 * g + u][:, D:2 * D], xinT[g][:, u, kb, :],
                                        flat2(flat2b(w13[:, kb:kb + 1, bass.ds(es[u], 1), :])), start=(kb == 0), stop=(kb == KD - 1))
                    ins.then_inc(s_hh, 1)

            def turn_gated(h, g):
                for u in range(U0):
                    pe.wait_ge(s_g, first(h, g) + u + 1)
                    pe.transpose(bank[4 * g + u][:, 0:P], sg[g][:, u, :], ident).then_inc(s_gt, 1)

            def out_rows(h, g, es):
                for u in range(U0):
                    pe.wait_ge(s_ge, first(h, g) + u + 1)
                    pe.matmul(bank[4 * g + u][:, D:2 * D], gT[g][:, u, :], flat2(w2[:, bass.ds(es[u], 1), :]), start=True, stop=True).then_inc(s_yp, 1)

            def half(h, g, h_before, g_before, es_before=None, fresh=False):
                es = experts(pe, h, g)
                turn_gated(h_before, g_before)
                turn_in(h, g, fresh)
                h13(h, g, es)
                out_rows(h_before, g_before, es_before or experts(pe, h_before, g_before))
                return es

            es = experts(pe, 0, 0)
            turn_in(0, 0, fresh=True)
            h13(0, 0, es)
            half(0, 1, 0, 0, es, fresh=True)
            with pe.Fori(1, NH) as h:
                es = half(h, 0, h - 1, 1)
                half(h, 1, h, 0, es)
            turn_gated(NH - 1, 1)
            out_rows(NH - 1, 1, experts(pe, NH - 1, 1))

        @block.vector
        def _(dve):
            chain = Chain(dve, s_dve)
            k["aggregate"](dve, s_st)
            k["rstd_steps"](dve, chain, s_var, s_root)
            dve.wait_ge(w_in[0], 32)
            with dve.Fori(0, NT // 4) as h:
                for q in range(4):
                    k["norm_tile"](dve, xn[q], h * 4 + q).then_inc(s_xn, 1)
                for q in range(4):
                    dve.wait_ge(s_tp, h * 4 + q + 1)
                    dve.wait_ge(s_xTall, h * 4 + q + 1)
                    dve.tensor_copy(gate_xT[:, q, :, :], bank[q][:, 0:D].rearrange("p (k n) -> p k n", k=KD)).then_inc(s_xT, 1)
                for q in range(4):
                    dve.wait_ge(s_gs, h * 4 + q + 1)
                    dve.tensor_copy(flat2(sr[:, bass.ds(h * 4 + q, 1), :]), bank[4 + q][:, 0:NE]).then_inc(s_gate, 1)
            dve.wait_ge(s_gate, NT)

            def wide(ap, n=NE):
                return ap.unsqueeze(2).to_broadcast([P, NT, n])

            chain(dve.tensor_reduce(mx, sr, AX.X, ALU.max))
            dve.tensor_tensor(sr, sr, wide(mx), ALU.subtract).then_inc(s_max, 1)
            dve.wait_ge(s_exp, 1)
            chain(dve.tensor_reduce(mx, scb, AX.X, ALU.add))
            chain(dve.reciprocal(t1, mx))
            chain(dve.tensor_tensor(sr, scb, wide(t1), ALU.mult))
            chain(dve.tensor_tensor(scb, sr, gb[:, :].unsqueeze(1).to_broadcast([P, NT, NE]), ALU.add))
            v4 = scb.rearrange("p t (g e) -> p (t g) e", e=GRP)
            hi1, lo1, hi2, lo2, gs, gt = (small[:, i, :] for i in range(6))
            chain(dve.tensor_tensor(hi1, v4[:, :, 0], v4[:, :, 1], ALU.max))
            chain(dve.tensor_tensor(lo1, v4[:, :, 0], v4[:, :, 1], ALU.min))
            chain(dve.tensor_tensor(hi2, v4[:, :, 2], v4[:, :, 3], ALU.max))
            chain(dve.tensor_tensor(lo2, v4[:, :, 2], v4[:, :, 3], ALU.min))
            chain(dve.tensor_tensor(gs, hi1, hi2, ALU.max))
            chain(dve.tensor_tensor(gt, hi1, hi2, ALU.min))
            chain(dve.tensor_tensor(lo1, lo1, lo2, ALU.max))
            chain(dve.tensor_tensor(gt, gt, lo1, ALU.max))
            chain(dve.tensor_tensor(gs, gs, gt, ALU.add))
            rk = small[:, 6, :].rearrange("p (t g) -> p t g", g=G4)
            cc = small[:, 7, :].rearrange("p (t g) -> p t g", g=G4)
            g3 = gs.rearrange("p (t g) -> p t g", g=G4)
            chain(dve.tensor_scalar(rk, cst[:, C_IOTA:C_IOTA + G4].unsqueeze(1).to_broadcast([P, NT, G4]),
                                    -1.0, float(G4 - 1), ALU.mult, ALU.add))
            for d in range(1, G4):
                chain(dve.tensor_tensor(cc[:, :, 0:G4 - d], g3[:, :, 0:G4 - d], g3[:, :, d:G4], ALU.is_ge))
                chain(dve.tensor_tensor(rk[:, :, d:G4], rk[:, :, d:G4], cc[:, :, 0:G4 - d], ALU.add))
                chain(dve.tensor_tensor(rk[:, :, 0:G4 - d], rk[:, :, 0:G4 - d], cc[:, :, 0:G4 - d], ALU.subtract))
            chain(dve.tensor_scalar(small[:, 6, :], small[:, 6, :], 1.5, -BIG, ALU.is_gt, ALU.mult))
            chain(dve.tensor_tensor(v4, v4, small[:, 6, :].unsqueeze(2).to_broadcast([P, NT * G4, GRP]), ALU.add))
            chain(dve.tensor_scalar(em[:, :], cst[:, C_IOTA:C_IOTA + NE], float(-NE), None, ALU.add))
            pick_first_max(dve, chain, oh1, mx, scb, em[:, :], t3, t1, NE)
            chain(dve.scalar_tensor_tensor(scb, oh1, -2.0 * BIG, scb, ALU.mult, ALU.add))
            pick_first_max(dve, chain, oh2, mx, scb, em[:, :], t3, t1, NE)
            for i, oh in enumerate((oh1, oh2)):
                chain(dve.tensor_tensor(t3, sr, oh, ALU.mult))
                chain(dve.tensor_reduce(wk[:, i, :], t3, AX.X, ALU.add))
            assign_slots(dve, chain, r, (oh1, oh2), [s[:, :] for s in slots], etile[:, :], NE, NTL0,
                         bank[6][:, :].rearrange("p (t e) -> p t e", e=NE), bank[7][:, :].rearrange("p (t e) -> p t e", e=NE),
                         cst, s_mask, s_rank)
            dve.engine_nop().then_inc(s_slot, 1)
            def row(t):
                if t >= 4:
                    dve.wait_ge(sct[t % 4], 16 * K0 * (t // 4))
                k["norm_tile"](dve, xn[t % 4], t).then_inc(s_row, 1)

            def add_shared(g):
                xg = xres[:, 4 * g:4 * g + 4, :]
                dve.wait_ge(s_row, 4 * g + 4)
                dve.wait_ge(s_z, 2 * g + 2)
                add(dve.tensor_tensor(xg, xg, xT[:, g, :].rearrange("p (q d) -> p q d", q=4), ALU.add))
                add(dve.tensor_tensor(xg, xg, bs2[:, :].unsqueeze(1).to_broadcast([P, 4, D]), ALU.add))

            add = Chain(dve, s_c0)
            dve.wait_ge(w_in[2], 16)
            per = NT // (NG - EARLY + 1)
            t = 0
            for g in range(EARLY, NG):
                for _ in range(per):
                    row(t)
                    t += 1
                for i in range(KD):
                    dve.wait_ge(s_si, g * 4 + 2 * i + 2)
                    dve.tensor_tensor(gsh[i], gsh[i], ssh[i], ALU.mult).then_inc(s_gsh, 1)
                for i in range((t - per) // 4, t // 4):
                    add_shared(i)
            for t in range(t, NT):
                row(t)
                if t % 4 == 3:
                    add_shared(t // 4)
            dve.wait_ge(w_in[3], 48)
            dve.wait_ge(w_in[4], 16)

            def biased(h, g, es):
                for u in range(U0):
                    dve.wait_ge(s_hh, first(h, g) + u + 1)
                    dve.tensor_tensor(hb[g][:, u, :], bank[4 * g + u][:, D:2 * D], flat2(b13[:, bass.ds(es[u], 1), :]), ALU.add).then_inc(s_hb, 1)

            def gated(h, g):
                for u in range(U0):
                    dve.wait_ge(s_sg, first(h, g) + u + 1)
                    dve.tensor_tensor(sg[g][:, u, :], sg[g][:, u, :], hb[g][:, u, I0:2 * I0], ALU.mult).then_inc(s_g, 1)

            def results(h, g, es, fresh=False):
                if not fresh:
                    dve.wait_ge(y_out[g], h * 16)
                for u in range(U0):
                    dve.wait_ge(s_yp, first(h, g) + u + 1)
                    dve.tensor_tensor(yo[g][:, u, :], bank[4 * g + u][:, D:2 * D], flat2(b2[:, bass.ds(es[u], 1), :]), ALU.add).then_inc(s_yo, 1)

            def half(h, g, h_before, g_before, es_before=None, fresh=False):
                es = experts(dve, h, g)
                biased(h, g, es)
                gated(h, g)
                results(h_before, g_before, es_before or experts(dve, h_before, g_before), fresh)
                return es

            es = experts(dve, 0, 0)
            biased(0, 0, es)
            gated(0, 0)
            half(0, 1, 0, 0, es, fresh=True)
            es = half(1, 0, 0, 1, fresh=True)
            half(1, 1, 1, 0, es)
            with dve.Fori(2, NH) as h:
                es = half(h, 0, h - 1, 1)
                half(h, 1, h, 0, es)
            results(NH - 1, 1, experts(dve, NH - 1, 1))


def phase_xattn(nc, a, out_tok, k):
    sb, sem = k["sb"], k["sem"]
    pb = k["pb"]
    cst, ident, xres, st6, rows, slots, wk = (k[n] for n in ("cst", "ident", "xres", "st6", "rows", "slots", "wk"))
    ones = cst[:, C_ONE:C_ONE + P]
    TPP = 2 * TPB
    with ExitStack() as ctx:
        ctx_sb = k["ctx_sb"]
        wqv = sb(ctx, "a_wqv", [P, 4, KD, D])
        wsim = sb(ctx, "a_wsim", [P, 3, KD])
        bsim = sb(ctx, "a_bsim", [1, 1])
        bqv = sb(ctx, "a_bqv", [P, D])
        st4 = sb(ctx, "a_st4", [P, TPP, 6])
        ln = sb(ctx, "a_ln", [P, 9, TPP])

        def two(name, shape):
            return [sb(ctx, f"a_{name}{u}", shape) for u in range(2)]

        def four(name, shape):
            return [[sb(ctx, f"a_{name}{g}{u}", shape) for u in range(2)] for g in range(2)]
        cS, cT, qmod, brow = two("cS", [C, D]), two("cT", [P, KD, C]), two("qmod", [P, KD, C]), two("brow", [1, C])
        mx, nmx, ssum = two("mx", [P, TPB]), two("nmx", [P, TPB]), two("ssum", [P, 2 * TPB])
        att, attT = two("att", [P, TPB, C]), two("attT", [C, S])
        gmx, erow, esum, battn, tmp = two("gmx", [1, 1]), two("erow", [1, S]), two("esum", [1, 2]), two("battn", [P, TPB]), two("tmp", [P, TPB, D])
        xn, hcT, hqT, prT, wp = (four(n, s) for n, s in (("xn", [P, TPB, D]), ("hcT", [P, KD, S]), ("hqT", [P, KD, S]),
                                                         ("prT", [P, KD, S]), ("wp", [P, KD, D])))
        A, Ck, Dk, O = ([pb(ctx, f"a_{n}{u}", [P, 512]) for u in range(2)] for n in "ACDO")
        CT = 2 * P

        w_in = [sem(f"a_w_in{i}") for i in range(2)]
        gat = [sem(f"a_gat{u}") for u in range(4)]
        names = ("c0 cb st ln var root xn cS tp ctp hcT qmod cTs r brow sim mx nmx exp rs att attT attE rowm gmx erow es bcol bcs hcb "
                 "wp hq hqE pr out tmp add fst nmr").split()
        q = {n: sem("a_" + n) for n in names}
        block = ctx.enter_context(nc.Block())
        NH = B // 4

        @block.sync
        def _(sp):
            sp.dma_start(wsim[:, :, :], a["wsim"]).then_inc(w_in[0], 16)
            sp.dma_start(bsim[:, :], a["b_sim"]).then_inc(w_in[0], 16)
            sp.dma_start(wqv[:, :, :, :], a["wqv"]).then_inc(w_in[1], 16)
            sp.dma_start(bqv[:, :], a["L1_xattn_b_qv"].partition_broadcast(P)).then_inc(w_in[1], 16)
            for e in range(E1):
                sp.wait_ge(q["cb"], min(e + 1, B // 2) * TPP)
                sp.dma_start(k["l1_w1"][:, :, e, :], a["l1_w1"][:, :, e, :]).then_inc(k["s_w1"], 16)

        @block.gpsimd
        def _(pool):
            for t in range(NT):
                if t >= 4:
                    pool.wait_ge(q["cb"], t - 3)
                for i in range(K0):
                    pool.indirect_dma_start(out=rows[i][:, t % 4, :], out_offset=None, in_=k["ys0"],
                                            in_offset=bass.IndirectOffsetOnAxis(ap=slots[i][:, t:t + 1], axis=0)
                                            ).then_inc(gat[t % 4], 16)

        @block.scalar
        def _(act):
            def root(p):
                act.wait_ge(q["var"], p + 1)
                act.activation(ln[:, 5, :], ln[:, 4, :], ACT.Sqrt).then_inc(q["root"], 1)

            def context(p):
                for u in range(2):
                    act.copy(cS[u][:, :], flat2(ctx_sb[:, bass.ds(p * 2 + u, 1), :])).then_inc(q["cS"], 1)

            def half(p, g, settled, more=True):
                context(p)
                for u in range(2):
                    b = p * 2 + u
                    act.wait_ge(q["ctp"], b + 1)
                    act.copy(cT[u][:, :, :], Dk[u][:, CT:CT + 2 * C].rearrange("p (k c) -> p k c", k=KD)).then_inc(q["cTs"], 1)
                    if settled:
                        act.wait_ge(q["out"], b - 3)
                    act.wait_ge(q["tp"], b + 1)
                    act.copy(hcT[g][u][:, :, :], A[u][:, :].rearrange("p (k n) -> p k n", k=KD)).then_inc(q["hcT"], 1)
                for u in range(2):
                    act.wait_ge(q["nmx"], p * 2 + u + 1)
                    for i in range(TPB):
                        act.activation(att[u][:, i, :], Ck[u][:, i * P:i * P + C], ACT.Exp, bias=nmx[u][:, i:i + 1],
                                       accum_out=ssum[u][:, i:i + 1]).then_inc(q["exp"], 1)
                if more:
                    root(p + 1)
                for u in range(2):
                    act.wait_ge(q["gmx"], p * 2 + u + 1)
                    act.activation(erow[u][:, :], A[u][0:1, 0:S], ACT.Exp, bias=gmx[u][:, :],
                                   accum_out=esum[u][:, 0:1]).then_inc(q["erow"], 1)
                for u in range(2):
                    act.wait_ge(q["attT"], p * 2 + u + 1)
                    act.copy(attT[u][:, :], Dk[u][0:C, 0:S]).then_inc(q["attE"], 1)
                for u in range(2):
                    act.wait_ge(q["hq"], p * 2 + u + 1)
                    act.copy(hqT[g][u][:, :, :], A[u][:, :].rearrange("p (k n) -> p k n", k=KD)).then_inc(q["hqE"], 1)

            root(0)
            half(0, 0, False)
            half(1, 1, False)
            with act.Fori(1, NH - 1) as h:
                half(h * 2, 0, True)
                half(h * 2 + 1, 1, True)
            half(B // 2 - 2, 0, True)
            half(B // 2 - 1, 1, True, more=False)

        @block.tensor
        def _(pe):
            def last(p, g, u, i, used=True):
                b = p * 2 + u
                if i == 0:
                    pe.wait_ge(q["hqE"], b + 1)
                    pe.wait_ge(q["pr"], b + 1)
                    pe.wait_ge(q["wp"], b + 1)
                    if used:
                        pe.wait_ge(q["tmp"], b - 1)
                n = 0
                for part, rhs in ((hqT, lambda kb: wqv[:, 1, kb, :]), (prT, lambda kb: wqv[:, 2, kb, :]), (hcT, lambda kb: wp[g][u][:, kb, :])):
                    for kb in range(KD):
                        ins = pe.matmul(O[u][:, i * D:(i + 1) * D], part[g][u][:, kb, i * P:(i + 1) * P], rhs(kb), start=(n == 0), stop=(n == 5))
                        n += 1
                if i == TPB - 1:
                    ins.then_inc(q["out"], 1)

            def half(p, g, before=None, used=True):
                def piece(u, i):
                    if before is not None:
                        last(before, 1 - g, u, i, used)
                for u in range(2):
                    b = p * 2 + u
                    pe.wait_ge(q["cS"], b + 1)
                    for kb in range(KD):
                        ins = pe.transpose(Dk[u][:, CT + kb * C:CT + (kb + 1) * C], cS[u][:, kb * P:(kb + 1) * P], ident[0:C, 0:C])
                    ins.then_inc(q["ctp"], 1)
                for u in range(2):
                    b = p * 2 + u
                    if before is not None:
                        pe.wait_ge(q["hqE"], b - 1)
                    pe.wait_ge(q["xn"], b + 1)
                    for i in range(TPB):
                        for kb in range(KD):
                            ins = pe.transpose(A[u][:, kb * S + i * P:kb * S + (i + 1) * P], xn[g][u][:, i, kb * P:(kb + 1) * P], ident)
                    ins.then_inc(q["tp"], 1)
                for u in range(2):
                    b = p * 2 + u
                    pe.wait_ge(q["cTs"], b + 1)
                    for kb in range(KD):
                        ins = pe.matmul(Dk[u][0:1, 0:C], wsim[:, 1, kb:kb + 1], cT[u][:, kb, :], start=(kb == 0), stop=(kb == KD - 1))
                    ins.then_inc(q["r"], 1)
                piece(0, 0)
                for u in range(2):
                    b = p * 2 + u
                    pe.wait_ge(q["hcT"], b + 1)
                    pe.wait_ge(q["brow"], b + 1)
                    for i in range(TPB):
                        for kb in range(KD):
                            pe.matmul(Ck[u][:, i * P:i * P + C], hcT[g][u][:, kb, i * P:(i + 1) * P], qmod[u][:, kb, :], start=(kb == 0), stop=False)
                        ins = pe.matmul(Ck[u][:, i * P:i * P + C], ones[0:1, :], brow[u][:, :], start=False, stop=True)
                    ins.then_inc(q["sim"], 1)
                piece(0, 1)
                for u in range(2):
                    pe.wait_ge(q["mx"], p * 2 + u + 1)
                    for i in range(TPB):
                        ins = pe.matmul(A[u][0:1, i * P:(i + 1) * P], mx[u][:, i:i + 1], ident, start=True, stop=True)
                    ins.then_inc(q["rowm"], 1)
                piece(1, 0)
                for u in range(2):
                    pe.wait_ge(q["att"], p * 2 + u + 1)
                    for i in range(TPB):
                        ins = pe.transpose(Dk[u][0:C, i * P:(i + 1) * P], att[u][:, i, :], ident)
                    ins.then_inc(q["attT"], 1)
                for u in range(2):
                    pe.wait_ge(q["es"], p * 2 + u + 1)
                    for i in range(TPB):
                        ins = pe.matmul(Ck[u][:, i:i + 1], erow[u][:, i * P:(i + 1) * P], esum[u][:, 1:2], start=True, stop=True)
                    ins.then_inc(q["bcol"], 1)
                for u in range(2):
                    pe.wait_ge(q["attE"], p * 2 + u + 1)
                    for kb in range(KD):
                        ins = pe.matmul(A[u][:, kb * S:(kb + 1) * S], cS[u][:, kb * P:(kb + 1) * P], attT[u][:, :], start=True, stop=True)
                    ins.then_inc(q["hq"], 1)
                for u in range(2):
                    pe.wait_ge(q["bcs"], p * 2 + u + 1)
                    for kb in range(KD):
                        for i in range(TPB):
                            ins = pe.matmul(Ck[u][:, 8 + kb:9 + kb], xn[g][u][:, i, kb * P:(kb + 1) * P], battn[u][:, i:i + 1],
                                            start=(i == 0), stop=(i == TPB - 1))
                    ins.then_inc(q["hcb"], 1)
                piece(1, 1)

            pe.wait_ge(w_in[0], 32)
            half(0, 0)
            pe.wait_ge(w_in[1], 32)
            half(1, 1, 0, used=False)
            with pe.Fori(1, NH - 1) as h:
                half(h * 2, 0, h * 2 - 1)
                half(h * 2 + 1, 1, h * 2)
            half(B // 2 - 2, 0, B // 2 - 3)
            half(B // 2 - 1, 1, B // 2 - 2)
            for u in range(2):
                for i in range(TPB):
                    last(B // 2 - 1, 1, u, i)

        @block.vector
        def _(dve):
            CHAIN = 10

            def combine(p):
                for u in range(TPP):
                    t = p * TPP + u
                    xt = flat2(xres[:, bass.ds(t, 1), :])
                    dve.wait_ge(gat[u], 16 * K0 * (p + 1))
                    dve.scalar_tensor_tensor(xt, rows[0][:, u, :], wk[:, 0, bass.ds(t, 1)], xt, ALU.mult, ALU.add).then_inc(q["c0"], 1)
                for u in range(TPP):
                    t = p * TPP + u
                    xt = flat2(xres[:, bass.ds(t, 1), :])
                    dve.wait_ge(q["c0"], t + 1)
                    dve.scalar_tensor_tensor(xt, rows[1][:, u, :], wk[:, 1, bass.ds(t, 1)], xt, ALU.mult, ALU.add).then_inc(q["cb"], 1)

            def pair_stats(p):
                for u in range(TPP):
                    dve.bn_stats(st4[:, u, :], flat2(xres[:, bass.ds(p * TPP + u, 1), :])).then_inc(q["st"], 1)

            def variances(p):
                chain = Chain(dve, q["ln"], p * CHAIN)
                even, odd = st4[:, :, 0:3], st4[:, :, 3:6]
                dve.wait_ge(q["st"], p * TPP + TPP)
                chain(dve.tensor_tensor(ln[:, 0, :], even[:, :, 1], odd[:, :, 1], ALU.add))
                chain(dve.tensor_tensor(ln[:, 1, :], even[:, :, 1], odd[:, :, 1], ALU.subtract))
                chain(dve.tensor_tensor(ln[:, 2, :], even[:, :, 2], odd[:, :, 2], ALU.add))
                chain(dve.scalar_tensor_tensor(ln[:, 1, :], ln[:, 1, :], 0.25, ln[:, 1, :], ALU.mult, ALU.mult))
                chain(dve.tensor_scalar(ln[:, 2, :], ln[:, 2, :], 1.0 / D, EPS, ALU.mult, ALU.add))
                dve.tensor_tensor(ln[:, 4, :], ln[:, 1, :], ln[:, 2, :], ALU.add).then_inc(q["var"], 1)

            def normalise(p, g):
                chain = Chain(dve, q["ln"], p * CHAIN + 5)
                dve.wait_ge(q["root"], p + 1)
                chain(dve.reciprocal(ln[:, 6, :], ln[:, 5, :]))
                chain(dve.tensor_tensor(ln[:, 6, :], ln[:, 4, :], ln[:, 6, :], ALU.mult))
                chain(dve.scalar_tensor_tensor(ln[:, 6, :], ln[:, 6, :], 1.0, ln[:, 5, :], ALU.mult, ALU.add))
                chain(dve.tensor_scalar(ln[:, 6, :], ln[:, 6, :], 0.5, None, ALU.mult))
                chain(dve.reciprocal(ln[:, 7, :], ln[:, 6, :]))
                dve.scalar_tensor_tensor(ln[:, 8, :], ln[:, 0, :], -0.5, ln[:, 7, :], ALU.mult, ALU.mult).then_inc(q["nmr"], 1)
                dve.wait_ge(q["nmr"], p + 1)
                for u in range(2):
                    for i in range(TPB):
                        w = u * TPB + i
                        ins = dve.tensor_scalar(xn[g][u][:, i, :], flat2(xres[:, bass.ds(p * TPP + w, 1), :]), ln[:, 7, w:w + 1], ln[:, 8, w:w + 1],
                                                ALU.mult, ALU.add)
                    ins.then_inc(q["xn"], 1)

            def finish(p, u):
                b = p * 2 + u
                dve.wait_ge(q["out"], b + 1)
                dve.tensor_tensor(tmp[u][:, :, :], O[u][:, :].rearrange("p (i d) -> p i d", i=TPB),
                                  bqv[:, :].unsqueeze(1).to_broadcast([P, TPB, D]), ALU.add).then_inc(q["tmp"], 1)
                dve.wait_ge(q["tmp"], b + 1)
                xb = xres[:, bass.ds(b * TPB, TPB), :]
                dve.tensor_tensor(xb, tmp[u][:, :, :], xb, ALU.add).then_inc(q["add"], 1)

            def final_stats(p, u):
                b = p * 2 + u
                for i in range(TPB):
                    dve.bn_stats(flat2(st6[:, bass.ds(b * TPB + i, 1), :]), flat2(xres[:, bass.ds(b * TPB + i, 1), :])).then_inc(q["fst"], 1)

            def half(p, g, before=None, settled=None, more=True):
                for u in range(2):
                    b = p * 2 + u
                    dve.wait_ge(q["cTs"], b + 1)
                    for kb in range(KD):
                        dve.tensor_scalar(qmod[u][:, kb, :], cT[u][:, kb, :], wsim[:, 2, kb:kb + 1], wsim[:, 0, kb:kb + 1],
                                          ALU.mult, ALU.add).then_inc(q["qmod"], 1)
                    dve.wait_ge(q["r"], b + 1)
                    dve.tensor_scalar(brow[u][:, :], Dk[u][0:1, 0:C], bsim[:, :], None, ALU.add).then_inc(q["brow"], 1)
                if settled is not None:
                    finish(settled, 1)
                if more:
                    combine(p + 1)
                for u in range(2):
                    b = p * 2 + u
                    if settled is not None and u == 0:
                        dve.wait_ge(q["add"], settled * 2 + 2)
                    if more and u == 1:
                        dve.wait_ge(q["cb"], (p + 2) * TPP)
                    dve.wait_ge(q["sim"], b + 1)
                    dve.tensor_reduce(mx[u][:, :], Ck[u][:, 0:2 * P].rearrange("p (i c) -> p i c", i=TPB)[:, :, 0:C], AX.X, ALU.max).then_inc(q["mx"], 1)
                    dve.wait_ge(q["mx"], b + 1)
                    dve.tensor_scalar(nmx[u][:, :], mx[u][:, :], -1.0, None, ALU.mult).then_inc(q["nmx"], 1)
                    if settled is not None and u == 0:
                        final_stats(settled, 1)
                    if more and u == 1:
                        pair_stats(p + 1)
                if more:
                    variances(p + 1)
                for u in range(2):
                    dve.wait_ge(q["rowm"], p * 2 + u + 1)
                    dve.tensor_reduce(gmx[u][:, :], A[u][0:1, 0:S], AX.X, ALU.max, negate=True).then_inc(q["gmx"], 1)
                for u in range(2):
                    b = p * 2 + u
                    dve.wait_ge(q["exp"], b * TPB + TPB)
                    dve.reciprocal(ssum[u][:, TPB:2 * TPB], ssum[u][:, 0:TPB]).then_inc(q["rs"], 1)
                    dve.wait_ge(q["rs"], b + 1)
                    for i in range(TPB):
                        ins = dve.tensor_scalar(att[u][:, i, :], att[u][:, i, :], ssum[u][:, TPB + i:TPB + i + 1], None, ALU.mult)
                    ins.then_inc(q["att"], 1)
                for u in range(2):
                    dve.wait_ge(q["erow"], p * 2 + u + 1)
                    dve.reciprocal(esum[u][:, 1:2], esum[u][:, 0:1]).then_inc(q["es"], 1)
                if before is not None:
                    finish(before, 0)
                for u in range(2):
                    dve.wait_ge(q["bcol"], p * 2 + u + 1)
                    dve.tensor_copy(battn[u][:, :], Ck[u][:, 0:TPB]).then_inc(q["bcs"], 1)
                if more:
                    normalise(p + 1, 1 - g)
                if before is not None:
                    dve.wait_ge(q["add"], before * 2 + 1)
                for u in range(2):
                    b = p * 2 + u
                    dve.wait_ge(q["hqE"], b + 1)
                    dve.tensor_tensor(prT[g][u][:, :, :], hcT[g][u][:, :, :], hqT[g][u][:, :, :], ALU.mult).then_inc(q["pr"], 1)
                    dve.wait_ge(q["hcb"], b + 1)
                    for kb in range(KD):
                        ins = dve.scalar_tensor_tensor(wp[g][u][:, kb, :], wqv[:, 3, kb, :], Ck[u][:, 8 + kb:9 + kb], wqv[:, 0, kb, :], ALU.mult, ALU.add)
                    ins.then_inc(q["wp"], 1)
                if before is not None:
                    final_stats(before, 0)

            combine(0)
            dve.wait_ge(q["cb"], TPP)
            pair_stats(0)
            variances(0)
            normalise(0, 0)
            dve.wait_ge(w_in[0], 32)
            dve.wait_ge(w_in[1], 32)
            half(0, 0)
            half(1, 1, 0)
            with dve.Fori(1, NH - 1) as h:
                half(h * 2, 0, h * 2 - 1, h * 2 - 2)
                half(h * 2 + 1, 1, h * 2, h * 2 - 1)
            half(B // 2 - 2, 0, B // 2 - 3, B // 2 - 4)
            half(B // 2 - 1, 1, B // 2 - 2, B // 2 - 3, more=False)
            for p, u in ((B // 2 - 2, 1), (B // 2 - 1, 0), (B // 2 - 1, 1)):
                finish(p, u)
                dve.wait_ge(q["add"], p * 2 + u + 1)
                final_stats(p, u)


def phase_moe1(nc, a, out_tok, k):
    sb, pb, sem = k["sb"], k["pb"], k["sem"]
    cst, ident, xres, rstd, nmr, lnt, st6, mv, w1 = (k[n] for n in ("cst", "ident", "xres", "rstd", "nmr", "lnt", "st6", "mv", "l1_w1"))
    xs, ys = k["xs1"], k["ys1"]
    NE = E1
    with ExitStack() as ctx:
        w2 = sb(ctx, "f_w2", [P, FB, NE, D])
        b1 = sb(ctx, "f_b1", [P, NE, FB])
        b2 = sb(ctx, "f_b2", [P, NE, D])
        lgb = sb(ctx, "f_lgb", [P, NE, 2 * KD])
        cw = sb(ctx, "f_cw", [P, KD, NE])
        xn = [k["rows"][0][:, u, :] for u in range(4)]
        xT = [sb(ctx, f"f_xT{u}", [P, KD, P]) for u in range(4)]
        arena = k["ctx_all"][:, :, :].rearrange("p b d -> p (b d)")
        hs = [arena[:, 1024 * u:1024 * u + 1024] for u in range(U1)]
        hT = [arena[:, 2048 + 1024 * u:3072 + 1024 * u].rearrange("p (f n) -> p f n", f=FB) for u in range(U1)]
        yo = [k["rows"][1][:, u, :] for u in range(U1)]
        big = [arena[:, 256 * i:256 * i + 256].rearrange("p (t e) -> p t e", e=NE) for i in range(5)]
        aff, oh, t3 = big[0], big[1], big[2]
        em = sb(ctx, "f_em", [P, NE])
        sm = sb(ctx, "f_sm", [P, 8, NT])
        top, t1, alpha = sm[:, 0, :], sm[:, 1, :], sm[:, 2, :]
        rs2, nm2 = sb(ctx, "f_rs2", [P, NT]), sb(ctx, "f_nm2", [P, NT])
        slot = sb(ctx, "f_slot", [P, NT], U32)
        etile = sb(ctx, "f_etile", [1, NTL1], I32)
        r = {"totE": big[3].rearrange("p t e -> p (t e)").rearrange("p (e t) -> p e t", e=NE), "t3": t3,
             "cum": big[4].rearrange("p t e -> p (t e)").rearrange("p (e t) -> p e t", e=NE), "sst": sb(ctx, "f_sst", [P, NE + 1])[:, :],
             "ti": sb(ctx, "f_ti", [P, NE], I32)[:, :], "red": sm[:, 3, :],
             "cmp": sb(ctx, "f_cmp", [1, NTL1, NE])[:, :, :], "tsum": sb(ctx, "f_tsum", [1, NTL1])[:, :]}
        for i, n in enumerate(("cnt", "tl", "tend", "delta")):
            r[n] = sm[:, 4 + i, 0:NE]
        bank = [pb(ctx, f"f_bank{u}", [P, 512]) for u in range(8)]

        w_in = [sem(f"f_w_in{i}") for i in range(2)]
        names = ("st var root dve xn tp xT gs gate var2 root2 exp1 exp2 mask rank slot row xt xe hh hs1 hs2 t ht1 ht2 yp yo cb add").split()
        q = {n: sem("f_" + n) for n in names}
        sct = [sem(f"f_sct{u}") for u in range(4)]
        gat = [sem(f"f_gat{u}") for u in range(4)]
        x_in = [sem(f"f_x_in{u}") for u in range(U1)]
        y_out = [sem(f"f_y_out{u}") for u in range(U1)]
        s_res = sem("f_res")
        block = ctx.enter_context(nc.Block())
        xin = xn
        NH = NTL1 // 2

        def expert(eng, n):
            return eng.value_load(etile[0:1, bass.ds(n, 1)], min_val=0, max_val=NE - 1)


        @block.sync
        def _(sp):
            sp.dma_start(cw[:, :, :], a["cw"]).then_inc(w_in[0], 16)
            for dst, name in ((b1[:, :, :], "b1"), (lgb[:, :, :], "lgb")):
                sp.dma_start(dst, a[name]).then_inc(w_in[1], 16)
            sp.dma_start(b2[:, :, :].rearrange("p e n -> p (e n)"), a["L1_ffn_b2"].rearrange("e n -> (e n)").partition_broadcast(P)).then_inc(w_in[1], 16)
            for c in range(4):
                sp.dma_start(w2[:, 2 * c:2 * c + 2, :, :], a["l1_w2"][:, 2 * c:2 * c + 2, :, :]).then_inc(w_in[1], 16)
            for u in range(4):
                sp.wait_ge(sct[u], 16 * NT // 4)

            def load(h, u):
                sp.dma_start(xin[u], xs[bass.ds((h * 2 + u) * P, P), :]).then_inc(x_in[u], 16)

            def reload(h, u):
                sp.wait_ge(q["xt"], h * 2 + u - 1)
                load(h, u)

            def store(h, u):
                sp.wait_ge(q["yo"], h * 2 + u + 1)
                sp.dma_start(ys[bass.ds((h * 2 + u) * P, P), :], yo[u]).then_inc(y_out[u], 16)

            load(0, 0)
            load(0, 1)
            reload(1, 0)
            reload(1, 1)
            store(0, 0)
            with sp.Fori(2, NH) as h:
                reload(h, 0)
                store(h - 2, 1)
                reload(h, 1)
                store(h - 1, 0)
            store(NH - 2, 1)
            store(NH - 1, 0)
            store(NH - 1, 1)
            for t in range(0, NT, 4):
                sp.wait_ge(q["cb"], t + 4)
                sp.dma_start(out_tok[:, t:t + 4, :], xres[:, t:t + 4, :]).then_inc(s_res, 16)
            sp.wait_ge(s_res, 16 * NT // 4)

        @block.gpsimd
        def _(pool):
            pool.wait_ge(q["slot"], 1)
            for t in range(NT):
                pool.wait_ge(q["row"], t + 1)
                pool.indirect_dma_start(out=xs, out_offset=bass.IndirectOffsetOnAxis(ap=slot[:, t:t + 1], axis=0),
                                        in_=xn[t % 4], in_offset=None).then_inc(sct[t % 4], 16)
            for u in range(U1):
                pool.wait_ge(y_out[u], 16 * NH)
            for t in range(NT):
                if t >= 4:
                    pool.wait_ge(q["cb"], t - 3)
                pool.indirect_dma_start(out=xn[t % 4], out_offset=None, in_=ys,
                                        in_offset=bass.IndirectOffsetOnAxis(ap=slot[:, t:t + 1], axis=0)).then_inc(gat[t % 4], 16)

        @block.scalar
        def _(act):
            act.wait_ge(q["var"], 1)
            act.activation(lnt[:, 1, :], lnt[:, 0, :], ACT.Sqrt).then_inc(q["root"], 1)
            act.wait_ge(q["var2"], 1)
            act.activation(lnt[:, 1, :], lnt[:, 0, :], ACT.Sqrt).then_inc(q["root2"], 1)
            act.wait_ge(q["exp1"], 1)
            act.activation(alpha, top, ACT.Exp, scale=-1.0).then_inc(q["exp2"], 1)
            act.wait_ge(w_in[1], 16 * 7)
            act.wait_ge(q["slot"], 1)

            def turned_in(h, u, e):
                act.wait_ge(q["xt"], h * 2 + u + 1)
                for kb in range(KD):
                    act.activation(xT[u][:, kb, :], bank[4 * u + 2][:, kb * P:(kb + 1) * P], ACT.Identity,
                                   scale=flat2(lgb[:, bass.ds(e, 1), kb:kb + 1]), bias=flat2(lgb[:, bass.ds(e, 1), KD + kb:KD + kb + 1])).then_inc(q["xe"], 1)

            def inner(h, u):
                act.wait_ge(q["hh"], h * 2 + u + 1)
                act.copy(hs[u][:, 512:1024], bank[4 * u + 1][:, :]).then_inc(q["hs2"], 1)

            def rectified(h, u, e):
                act.wait_ge(q["t"], (h * 2 + u) * 2 + 2)
                for f in range(FB // 2, FB):
                    act.activation(hT[u][:, f, :], bank[4 * u + 3][:, (f - 4) * P:(f - 3) * P], ACT.Relu,
                                   bias=flat2(b1[:, bass.ds(e, 1), f:f + 1])).then_inc(q["ht2"], 1)

            def half(h, u, h_before, u_before, e_before=None):
                e = expert(act, h * 2 + u)
                turned_in(h, u, e)
                rectified(h_before, u_before, expert(act, h_before * 2 + u_before) if e_before is None else e_before)
                inner(h, u)
                return e

            e = expert(act, 0)
            turned_in(0, 0, e)
            inner(0, 0)
            half(0, 1, 0, 0, e)
            with act.Fori(1, NH) as h:
                e = half(h, 0, h - 1, 1)
                half(h, 1, h, 0, e)
            rectified(NH - 1, 1, expert(act, NTL1 - 1))

        @block.tensor
        def _(pe):
            pe.wait_ge(w_in[0], 16)
            with pe.Fori(0, NT // 4) as h:
                for i in range(4):
                    pe.wait_ge(q["xn"], h * 4 + i + 1)
                    for kb in range(KD):
                        ins = pe.transpose(bank[i][:, kb * P:(kb + 1) * P], xn[i][:, kb * P:(kb + 1) * P], ident)
                    ins.then_inc(q["tp"], 1)
                for i in range(4):
                    pe.wait_ge(q["xT"], h * 4 + i + 1)
                    for kb in range(KD):
                        ins = pe.matmul(bank[4 + i][:, 0:NE], xT[i][:, kb, :], cw[:, kb, :], start=(kb == 0), stop=(kb == KD - 1))
                    ins.then_inc(q["gs"], 1)
            pe.wait_ge(q["mask"], 1)
            pe.matmul(bank[6][:, 0:NT * NE], cst[:, C_TRI:C_TRI + P], oh.rearrange("p t e -> p (t e)"), start=True, stop=True)
            pe.matmul(bank[7][:, 0:NT * NE], cst[:, C_ONE:C_ONE + P], oh.rearrange("p t e -> p (t e)"), start=True, stop=True).then_inc(q["rank"], 1)
            pe.wait_ge(q["slot"], 1)
            pe.wait_ge(k["s_w1"], 16 * E1)
            pe.wait_ge(w_in[1], 16 * 7)

            def turn_in(h, u):
                pe.wait_ge(x_in[u], h * 16 + 16)
                for kb in range(KD):
                    ins = pe.transpose(bank[4 * u + 2][:, kb * P:(kb + 1) * P], xin[u][:, kb * P:(kb + 1) * P], ident)
                ins.then_inc(q["xt"], 1)

            def h1(h, u, e, fresh=False):
                if not fresh:
                    pe.wait_ge(q["yo"], h * 2 + u - 1)
                pe.wait_ge(q["xe"], (h * 2 + u + 1) * KD)
                for c in range(2):
                    for kb in range(KD):
                        ins = pe.matmul(bank[4 * u + c][:, :], xT[u][:, kb, :],
                                        flat2(flat2b(w1[:, kb:kb + 1, bass.ds(e, 1), c * 512:(c + 1) * 512])), start=(kb == 0), stop=(kb == KD - 1))
                ins.then_inc(q["hh"], 1)

            def turn_inner(h, u):
                pe.wait_ge(q["hs1"], h * 2 + u + 1)
                pe.wait_ge(q["hs2"], h * 2 + u + 1)
                for f in range(FB):
                    ins = pe.transpose(bank[4 * u + 2 + f // 4][:, (f % 4) * P:(f % 4 + 1) * P], hs[u][:, f * P:(f + 1) * P], ident)
                    if f % 4 == 3:
                        ins.then_inc(q["t"], 1)

            def out_rows(h, u, e):
                pe.wait_ge(q["ht1"], (h * 2 + u + 1) * (FB // 2))
                pe.wait_ge(q["ht2"], (h * 2 + u + 1) * (FB // 2))
                for f in range(FB):
                    ins = pe.matmul(bank[4 * u][:, 0:D], hT[u][:, f, :], flat2(flat2b(w2[:, f:f + 1, bass.ds(e, 1), :])), start=(f == 0), stop=(f == FB - 1))
                ins.then_inc(q["yp"], 1)

            def half(h, u, h_before, u_before, e_before=None, fresh=False):
                e = expert(pe, h * 2 + u)
                turn_in(h, u)
                turn_inner(h_before, u_before)
                h1(h, u, e, fresh)
                out_rows(h_before, u_before, expert(pe, h_before * 2 + u_before) if e_before is None else e_before)
                return e

            e = expert(pe, 0)
            turn_in(0, 0)
            h1(0, 0, e, fresh=True)
            half(0, 1, 0, 0, e, fresh=True)
            with pe.Fori(1, NH) as h:
                e = half(h, 0, h - 1, 1)
                half(h, 1, h, 0, e)
            turn_inner(NH - 1, 1)
            out_rows(NH - 1, 1, expert(pe, NTL1 - 1))

        @block.vector
        def _(dve):
            chain = Chain(dve, q["dve"])
            k["aggregate"](dve, q["st"])
            k["rstd_steps"](dve, chain, q["var"], q["root"])
            dve.wait_ge(w_in[0], 16)
            with dve.Fori(0, NT // 4) as h:
                for i in range(4):
                    k["norm_tile"](dve, xn[i], h * 4 + i).then_inc(q["xn"], 1)
                for i in range(4):
                    dve.wait_ge(q["xn"], h * 4 + i + 1)
                    dve.bn_stats(flat2(st6[:, bass.ds(h * 4 + i, 1), :]), xn[i]).then_inc(q["st"], 1)
                for i in range(4):
                    dve.wait_ge(q["tp"], h * 4 + i + 1)
                    dve.tensor_copy(xT[i][:, :, :], bank[i][:, 0:D].rearrange("p (k n) -> p k n", k=KD)).then_inc(q["xT"], 1)
                for i in range(4):
                    dve.wait_ge(q["gs"], h * 4 + i + 1)
                    dve.tensor_copy(flat2(aff[:, bass.ds(h * 4 + i, 1), :]), bank[4 + i][:, 0:NE]).then_inc(q["gate"], 1)
            dve.wait_ge(q["gate"], NT)
            dve.wait_ge(q["st"], 2 * NT)
            for t in range(NT):
                dve.bn_aggr(mv[:, t, :], st6[:, t, :]).then_inc(q["st"], 1)
            dve.wait_ge(q["st"], 3 * NT)
            ve, t0, tt = lnt[:, 0, :], lnt[:, 1, :], lnt[:, 2, :]
            dve.tensor_scalar(ve, mv[:, :, 1], EPS, None, ALU.add).then_inc(q["var2"], 1)
            dve.wait_ge(q["root2"], 1)
            chain(dve.reciprocal(tt, t0))
            chain(dve.tensor_tensor(tt, ve, tt, ALU.mult))
            chain(dve.tensor_tensor(tt, tt, t0, ALU.add))
            chain(dve.tensor_scalar(tt, tt, 0.5, None, ALU.mult))
            chain(dve.reciprocal(t0, tt))
            chain(dve.tensor_tensor(rs2[:, :], rstd[:, :], t0, ALU.mult))
            chain(dve.tensor_tensor(tt, nmr[:, :], mv[:, :, 0], ALU.subtract))
            chain(dve.tensor_tensor(nm2[:, :], tt, t0, ALU.mult))
            chain(dve.tensor_scalar(em[:, :], cst[:, C_IOTA:C_IOTA + NE], float(-NE), None, ALU.add))
            pick_first_max(dve, chain, oh, top, aff, em[:, :], t3, t1, NE)
            dve.engine_nop().then_inc(q["exp1"], 1)
            dve.wait_ge(q["exp2"], 1)
            chain(dve.tensor_scalar(alpha, alpha, 1.0, None, ALU.add))
            chain(dve.reciprocal(alpha, alpha))
            assign_slots(dve, chain, r, (oh,), [slot[:, :]], etile[:, :], NE, NTL1,
                         bank[6][:, 0:NT * NE].rearrange("p (t e) -> p t e", e=NE), bank[7][:, 0:NT * NE].rearrange("p (t e) -> p t e", e=NE),
                         cst, q["mask"], q["rank"])
            dve.engine_nop().then_inc(q["slot"], 1)
            for t in range(NT):
                if t >= 4:
                    dve.wait_ge(sct[t % 4], 16 * (t // 4))
                dve.tensor_scalar(xn[t % 4], xres[:, t, :], rs2[:, t:t + 1], nm2[:, t:t + 1], ALU.mult, ALU.add).then_inc(q["row"], 1)
            dve.wait_ge(w_in[1], 16 * 7)

            def inner(h, u):
                dve.wait_ge(q["hh"], h * 2 + u + 1)
                dve.tensor_copy(hs[u][:, 0:512], bank[4 * u][:, :]).then_inc(q["hs1"], 1)

            def rectified(h, u, e):
                dve.wait_ge(q["t"], (h * 2 + u) * 2 + 1)
                for f in range(FB // 2):
                    dve.tensor_scalar(hT[u][:, f, :], bank[4 * u + 2][:, f * P:(f + 1) * P], flat2(b1[:, bass.ds(e, 1), f:f + 1]), 0.0,
                                      ALU.add, ALU.max).then_inc(q["ht1"], 1)

            def results(h, u, e, fresh=False):
                if not fresh:
                    dve.wait_ge(y_out[u], h * 16)
                dve.wait_ge(q["yp"], h * 2 + u + 1)
                dve.tensor_tensor(yo[u], bank[4 * u][:, 0:D], flat2(b2[:, bass.ds(e, 1), :]), ALU.add).then_inc(q["yo"], 1)

            def half(h, u, h_before, u_before, e_before=None, fresh=False):
                e = expert(dve, h * 2 + u)
                e_before = expert(dve, h_before * 2 + u_before) if e_before is None else e_before
                rectified(h_before, u_before, e_before)
                inner(h, u)
                results(h_before, u_before, e_before, fresh)
                return e

            e = expert(dve, 0)
            inner(0, 0)
            half(0, 1, 0, 0, e, fresh=True)
            e = half(1, 0, 0, 1, fresh=True)
            half(1, 1, 1, 0, e)
            with dve.Fori(2, NH) as h:
                e = half(h, 0, h - 1, 1)
                half(h, 1, h, 0, e)
            e = expert(dve, NTL1 - 1)
            rectified(NH - 1, 1, e)
            results(NH - 1, 1, e)
            for u in range(U1):
                dve.wait_ge(y_out[u], 16 * NH)
            add = Chain(dve, q["add"])
            for t in range(NT):
                xt, tmp = xres[:, t, :], yo[t % 2]
                add(dve.tensor_scalar(tmp, xt, rstd[:, t:t + 1], nmr[:, t:t + 1], ALU.mult, ALU.add))
                add(dve.tensor_tensor(xt, xt, tmp, ALU.add))
                dve.wait_ge(gat[t % 4], 16 * (t // 4 + 1))
                dve.scalar_tensor_tensor(xt, xn[t % 4], alpha[:, t:t + 1], xt, ALU.mult, ALU.add).then_inc(q["cb"], 1)


def lay_out(inputs):
    w = {n: np.asarray(v) for n, v in inputs.items()}

    def blocks(m):
        return m.reshape(-1, P, m.shape[-1]).transpose(1, 0, 2)

    we = np.concatenate([w["L0_ffn_We1"], w["L0_ffn_We3"]], axis=2)
    return {
        "gate_w": blocks(w["L0_ffn_gate_w"].T),
        "ws1": blocks(w["L0_ffn_ws1"]), "ws3": blocks(w["L0_ffn_ws3"]), "ws2": blocks(w["L0_ffn_ws2"]),
        "bs13": np.stack([w["L0_ffn_bs1"], w["L0_ffn_bs3"]]).reshape(2, KD, P).transpose(2, 0, 1),
        "w13": we.reshape(E0, KD, P, 2 * I0).transpose(2, 1, 0, 3),
        "w2": w["L0_ffn_We2"].transpose(1, 0, 2),
        "wsim": w["L1_xattn_w_sim"].reshape(3, KD, P).transpose(2, 0, 1),
        "b_sim": w["L1_xattn_b_sim"].reshape(1, 1),
        "wqv": w["L1_xattn_W_qv"].reshape(4, KD, P, D).transpose(2, 0, 1, 3),
        "cw": blocks(w["L1_ffn_centroids"].T),
        "l1_w1": w["L1_ffn_w1"].reshape(E1, F1, KD, P).transpose(3, 2, 0, 1),
        "l1_w2": w["L1_ffn_w2"].reshape(E1, D, FB, P).transpose(3, 2, 0, 1),
        "b1": w["L1_ffn_b1"].reshape(E1, FB, P).transpose(2, 0, 1),
        "lgb": np.concatenate([w["L1_ffn_ln_g"].reshape(E1, KD, P), w["L1_ffn_ln_b"].reshape(E1, KD, P)], axis=1).transpose(2, 0, 1),
        "b13": np.concatenate([w["L0_ffn_be1"], w["L0_ffn_be3"]], axis=1),
    }


_INS = ["x", "ctx_1024", "L0_ffn_gate_b", "L0_ffn_bs2", "L0_ffn_be2", "L1_xattn_b_qv", "L1_ffn_b2"]


def kernel(**inputs):
    import concourse.bacc as bacc
    from concourse.bass_utils import run_bass_kernel_spmd

    nc = bacc.Bacc("TRN2", target_bir_lowering=False, num_devices=1)
    arrays, a = {}, {}

    def give(name, arr):
        arr = np.ascontiguousarray(arr)
        arrays[f"in_{name}"] = arr
        a[name] = nc.dram_tensor(f"in_{name}", arr.shape, mybir.dt.from_np(arr.dtype), kind="ExternalInput").ap()

    for name in _INS:
        give(name, inputs[name])
    for name, arr in lay_out(inputs).items():
        give(name, arr)
    give("cst", constants())
    give("zeros", np.zeros((P, 1), np.float32))
    out = nc.dram_tensor("out_0", (B, S, D), F32, kind="ExternalOutput").ap()
    program(nc, a, out)
    r = run_bass_kernel_spmd(nc, [arrays], core_ids=[0])
    return r.results[0]["out_0"]
```

```python
from contextlib import ExitStack

import numpy as np
import concourse.bass as bass
from concourse import mybir

ALU = mybir.AluOpType
ACT = mybir.ActivationFunctionType
AX = mybir.AxisListType
F32 = mybir.dt.float32
I32 = mybir.dt.int32
U32 = mybir.dt.uint32

P = 128
B, S, D = 16, 256, 256
C = 77
TOK = B * S
NT = TOK // P
TPB = S // P
KD = D // P
EPS = 1e-5
BIG = 1e30

LANES = 8
RPL = C // (LANES - 1)
WCOL = 64
NCOL = S // WCOL
STEPS = NCOL + LANES - 2
PADL = WCOL + 1
SKEW = PADL + STEPS * WCOL
assert RPL * (LANES - 1) == C

C_ID, C_TRI, C_ONE, C_IOTA = 0, 128, 256, 384
C_WIDE = C_IOTA + 256


def constants():
    c = np.zeros((P, C_WIDE), np.float32)
    c[:, C_ID:C_ID + P] = np.eye(P)
    c[:, C_TRI:C_TRI + P] = np.triu(np.ones((P, P)), 1)
    c[:, C_ONE:C_ONE + P] = 1.0
    c[:, C_IOTA:C_IOTA + 256] = np.arange(256)
    return c


def flat2b(ap):
    return ap.rearrange("p a b n -> p (a b) n")


def flat3(ap):
    return ap.rearrange("p a k n -> p (a k) n")


def flat2(ap):
    return ap.rearrange("p a n -> p (a n)")


E0, K0, I0 = 16, 2, 128
GRP = 4
U0 = 4
NTL0 = -(-((TOK * K0 + E0 * (P - 1)) // P) // (2 * U0)) * 2 * U0


E1, F1 = 8, 1024
FB = F1 // P
U1 = 2
NTL1 = -(-((TOK + E1 * (P - 1)) // P) // 4) * 4
IN, BASE, GATE, TOKEN = 0, D, 2 * D, 2 * D + 1
SLOT1 = 2 * D + 4


def pick_first_max(dve, chain, oh, top, v, rev, t3, t1, ne):
    def wide(ap):
        return ap.unsqueeze(2).to_broadcast([P, NT, ne])
    chain(dve.tensor_reduce(top, v, AX.X, ALU.max))
    chain(dve.tensor_tensor(t3, v, wide(top), ALU.is_ge))
    chain(dve.tensor_tensor(t3, t3, rev.unsqueeze(1).to_broadcast([P, NT, ne]), ALU.mult))
    chain(dve.tensor_reduce(t1, t3, AX.X, ALU.min))
    chain(dve.tensor_tensor(oh, rev.unsqueeze(1).to_broadcast([P, NT, ne]), wide(t1), ALU.is_equal))


def assign_slots(dve, chain, r, ohs, slots, ne, rank_ps, tot_ps, s_mask, s_rank):
    totE, cum, sst, cnt, ti, tl, tend, delta, red = (r[n] for n in (
        "totE", "cum", "sst", "cnt", "ti", "tl", "tend", "delta", "red"))
    t3 = r["t3"]
    if len(ohs) == 2:
        chain(dve.tensor_tensor(r["mask"], ohs[0], ohs[1], ALU.add))
    dve.engine_nop().then_inc(s_mask, 1)
    dve.wait_ge(s_rank, 1)
    chain(dve.tensor_copy(totE.rearrange("p e t -> p t e"), tot_ps))
    flat, cumf = totE.rearrange("p e t -> p (e t)"), cum.rearrange("p e t -> p (e t)")
    chain(dve.tensor_tensor_scan(cumf, flat, flat, 0.0, ALU.add, ALU.max))
    chain(dve.memset(sst[:, 0:1], 0.0))
    chain(dve.tensor_copy(sst[:, 1:ne + 1], cum[:, :, NT - 1]))
    chain(dve.tensor_tensor(cnt, sst[:, 1:ne + 1], sst[:, 0:ne], ALU.subtract))
    chain(dve.tensor_scalar(ti, cnt, float(P - 1), None, ALU.add))
    chain(dve.tensor_scalar(ti, ti, 7, None, ALU.arith_shift_right))
    chain(dve.tensor_copy(tl, ti))
    chain(dve.tensor_tensor_scan(tend, tl, tl, 0.0, ALU.add, ALU.max))
    chain(dve.tensor_tensor(delta, tend, tl, ALU.subtract))
    chain(dve.scalar_tensor_tensor(delta, delta, float(P), sst[:, 0:ne], ALU.mult, ALU.subtract))
    chain(dve.tensor_tensor(cumf, cumf, flat, ALU.subtract))
    chain(dve.tensor_tensor(cum, cum, delta.unsqueeze(2).to_broadcast([P, ne, NT]), ALU.add))
    chain(dve.tensor_tensor(t3, rank_ps, cum.rearrange("p e t -> p t e"), ALU.add))
    for oh, slot in zip(ohs, slots):
        chain(dve.tensor_tensor(totE.rearrange("p e t -> p (e t)").rearrange("p (t e) -> p t e", e=ne), oh, t3, ALU.mult))
        chain(dve.tensor_reduce(red, totE.rearrange("p e t -> p (e t)").rearrange("p (t e) -> p t e", e=ne), AX.X, ALU.add))
        chain(dve.tensor_copy(slot, red))


def assign_tiles(dve, chain, r, etile, ne, ntl, cst):
    cmp, tend = r["cmp"], r["tend"]
    chain(dve.tensor_tensor(cmp, tend[0:1, :].unsqueeze(1).to_broadcast([1, ntl, ne]),
                            cst[0:1, C_IOTA:C_IOTA + ntl].unsqueeze(2).to_broadcast([1, ntl, ne]), ALU.is_le))
    chain(dve.tensor_reduce(r["tsum"], cmp, AX.X, ALU.add))
    chain(dve.tensor_scalar(etile, r["tsum"], float(ne - 1), None, ALU.min))


class Chain:

    def __init__(self, eng, sem, base=0):
        self.eng, self.sem, self.base, self.n = eng, sem, base, 0

    def __call__(self, ins):
        self.n += 1
        ins.then_inc(self.sem, 1)
        self.eng.wait_ge(self.sem, self.base + self.n)


def program(nc, a, out):
    with ExitStack() as top:
        build(nc, top, a, out)


def build(nc, top, a, out):
    def sb(ctx, name, shape, dt=F32):
        return ctx.enter_context(nc.sbuf_tensor(name, shape, dt))

    def pb(ctx, name, shape, dt=F32):
        return ctx.enter_context(nc.psum_tensor(name, shape, dt))

    def sem(name):
        return top.enter_context(nc.semaphore(name))

    cst = sb(top, "cst", [P, C_WIDE])
    ident = cst[:, C_ID:C_ID + P]
    xres = sb(top, "xres", [P, NT, D])
    ctx_all = sb(top, "ctx_sb", [P, B, D])
    ctx_sb = ctx_all[0:C, :, :]
    mv = sb(top, "mv", [P, NT, 2])
    rstd = sb(top, "rstd", [P, NT])
    nmr = sb(top, "nmr", [P, NT])
    st6 = sb(top, "st6", [P, NT, 6])
    lnt = sb(top, "lnt", [P, 3, NT])
    rows_mem = [sb(top, f"rows{g}", [P, 4, D + 2]) for g in range(2)]
    rows = [m[:, :, 0:D] for m in rows_mem]
    slots = [sb(top, f"slot{i}", [P, NT], U32) for i in range(K0)]
    wk = sb(top, "wk", [P, K0, NT])
    s_cst = sem("s_cst")

    x_tok = a["x"].rearrange("b s d -> (b s) d").rearrange("(t p) d -> p t d", p=P)

    def load_stats(dve, load_sems, s_st):
        per = NT // len(load_sems)
        for c in range(len(load_sems)):
            dve.wait_ge(load_sems[c], 16)
            for u in range(per):
                dve.bn_stats(st6[:, c * per + u, :], xres[:, c * per + u, :]).then_inc(s_st, 1)
        dve.wait_ge(s_st, NT)

    def moments(chain, dve):
        even, odd = st6[:, :, 0:3], st6[:, :, 3:6]
        mean, var, half, sq = mv[:, :, 0], mv[:, :, 1], lnt[:, 0, :], lnt[:, 1, :]
        chain(dve.tensor_tensor(mean, even[:, :, 1], odd[:, :, 1], ALU.add))
        chain(dve.tensor_tensor(half, even[:, :, 1], odd[:, :, 1], ALU.subtract))
        chain(dve.tensor_tensor(sq, even[:, :, 2], odd[:, :, 2], ALU.add))
        chain(dve.scalar_tensor_tensor(half, half, 0.25, half, ALU.mult, ALU.mult))
        chain(dve.scalar_tensor_tensor(var, sq, 1.0 / D, half, ALU.mult, ALU.add))
        chain(dve.tensor_scalar(mean, mean, 0.5, None, ALU.mult))

    def norm_tile(dve, dst, t):
        return dve.tensor_scalar(dst, flat2(xres[:, bass.ds(t, 1), :]), rstd[:, bass.ds(t, 1)], nmr[:, bass.ds(t, 1)],
                                 ALU.mult, ALU.add)

    def rstd_steps(dve, chain, s_var, s_root):
        ve, t0, t1 = lnt[:, 0, :], lnt[:, 1, :], lnt[:, 2, :]
        dve.tensor_scalar(ve, mv[:, :, 1], EPS, None, ALU.add).then_inc(s_var, 1)
        dve.wait_ge(s_root, 1)
        chain(dve.reciprocal(t1, t0))
        chain(dve.tensor_tensor(t1, ve, t1, ALU.mult))
        chain(dve.tensor_tensor(t1, t1, t0, ALU.add))
        chain(dve.tensor_scalar(t1, t1, 0.5, None, ALU.mult))
        chain(dve.reciprocal(rstd[:, :], t1))
        chain(dve.scalar_tensor_tensor(nmr[:, :], mv[:, :, 0], -1.0, rstd[:, :], ALU.mult, ALU.mult))

    xs0 = nc.dram_tensor("xs0", [NTL0 * P, D], F32).ap()
    ys0 = nc.dram_tensor("ys0", [NTL0 * P, D], F32).ap()
    xs1 = nc.dram_tensor("xs1", [NTL1 * P, SLOT1], F32).ap()
    s_zero = sem("s_zero")
    n_zero = sum(-(-words // 1024) for words in (NTL0 * D, NTL1 * SLOT1))

    def zero_fill(sp, zbuf):
        for slot_rows in (xs0, xs1):
            v = slot_rows.rearrange("(p r) d -> p (r d)", p=P)
            for c in range(0, v.shape[1], 1024):
                w = min(1024, v.shape[1] - c)
                sp.dma_start(v[:, c:c + w], zbuf[:, 0:w]).then_inc(s_zero, 16)

    with ExitStack() as warp_sems:
        old_sems = []

        def warp_sem(name):
            old_sems.append(warp_sems.enter_context(nc.semaphore(name)))
            return old_sems[-1]

        phase_warp(nc, a, locals())
        phase_moe0(nc, a, locals())
    with ExitStack() as late:
        l1_w1 = sb(late, "l1_w1", [P, KD, E1, F1])
        s_w1 = sem("s_w1")
        phase_xattn(nc, a, locals())
        phase_moe1(nc, a, out, locals())


def phase_warp(nc, a, k):
    sb, pb, sem = k["sb"], k["pb"], k["warp_sem"]
    cst, ident, xres, rstd, nmr, lnt, st6 = (k[n] for n in ("cst", "ident", "xres", "rstd", "nmr", "lnt", "st6"))
    x_tok, s_cst = k["x_tok"], k["s_cst"]
    with ExitStack() as ctx:
        ctx_sb = k["ctx_sb"]
        DSK = RPL * STEPS * WCOL
        RSK = (RPL + 1) * SKEW
        CH = (LANES - 1) * RPL * S
        arena = sb(ctx, "w_arena", [P, max(DSK + RSK, CH)])
        dskew = arena[:, 0:DSK].rearrange("p (r w) -> p r w", r=RPL)
        rskew = arena[:, DSK:DSK + RSK].rearrange("p (r w) -> p r w", r=RPL + 1)
        chain_tab = arena[0:B, 0:CH].rearrange("p (r w) -> p r w", w=S)
        rrow = sb(ctx, "w_rrow", [P, RPL + 1, S + 1])
        up = sb(ctx, "w_up", [P, RPL, S])
        gv = sb(ctx, "w_gv", [P, RPL, S])
        jr = sb(ctx, "w_jr", [P, RPL, S])
        junk = sb(ctx, "w_junk", [B, S])
        c2 = sb(ctx, "w_c2", [B, C + 1])
        cs = sb(ctx, "w_cs", [C, 2, B])
        minw = sb(ctx, "w_min", [P, WCOL])
        zbuf = sb(ctx, "w_zbuf", [P, 1024])
        aa = sb(ctx, "w_aa", [C, B])
        iota15 = sb(ctx, "w_iota15", [C, S])
        iota2 = sb(ctx, "w_iota2", [C, S])
        halfneg = sb(ctx, "w_halfneg", [P, C])
        xn = [k["rows"][u][:, 0:TPB, :] for u in range(2)]
        xT = [sb(ctx, f"w_xT{u}", [P, KD, S]) for u in range(2)]
        xsq = [k["rows"][u][:, TPB:TPB + KD, :] for u in range(2)]
        cT = [sb(ctx, f"w_cT{u}", [P, KD, C]) for u in range(2)]
        d2 = [sb(ctx, f"w_d2{u}", [C, S]) for u in range(2)]
        y0 = [sb(ctx, f"w_y0{u}", [C, S]) for u in range(2)]
        ysq = [sb(ctx, f"w_ysq{u}", [C, S]) for u in range(2)]
        ri = [sb(ctx, f"w_ri{u}", [C, S]) for u in range(2)]
        path = [sb(ctx, f"w_path{u}", [C, S]) for u in range(2)]
        pm = [k["rows"][u][0:C, 0, :] for u in range(2)]
        tpx = [pb(ctx, f"w_tpx{u}", [P, KD, S]) for u in range(2)]
        tpc = [pb(ctx, f"w_tpc{u}", [P, KD, S]) for u in range(2)]
        dps = [pb(ctx, f"w_dps{u}", [P, 2 * S]) for u in range(2)]
        xps = tpx
        dscr = nc.dram_tensor("dscr", [B, C, S], F32).ap()

        x_in = [sem(f"w_x_in{c}") for c in range(4)]
        c_in = sem("w_c_in")
        s_st, s_var, s_root, s_dve = sem("w_st"), sem("w_var"), sem("w_root"), sem("w_dve")
        s_init = sem("w_init")
        s_tp, s_xT, s_sq, s_dd, s_d2 = (sem("w_" + n) for n in ("tp", "xT", "sq", "dd", "d2"))
        s_y0, s_ysq, s_res, s_ri, s_cor, s_y = (sem("w_" + n) for n in ("y0", "ysq", "res", "ri", "cor", "y"))
        s_aa, s_cT, s_ctp, s_cTs = sem("w_aa_s"), sem("w_cT_s"), sem("w_ctp"), sem("w_cTs")
        d_out = [sem(f"w_d_out{u}") for u in range(2)]
        d_in, t_in = ([sem(f"w_{n}{lane}") if lane else None for lane in range(LANES)] for n in ("d_in", "t_in"))
        s_dp, r_un, s_c2, s_c2t, s_cs = (sem("w_" + n) for n in ("dp", "r_un", "c2_s", "c2t", "cs_s"))
        s_pm, s_path, s_ex, s_add, s_dmp, s_gch, s_bt = (sem("w_" + n) for n in ("pm_s", "path_s", "ex", "add", "dmp", "gch", "bt"))
        s_corner, s_st2 = k["sem"]("w_corner"), sem("w_st2")
        s_zb = sem("w_zb")

        block = ctx.enter_context(nc.Block())

        @block.sync
        def _(sp):
            sp.dma_start(cst[:, :], a["cst"]).then_inc(s_cst, 16)
            for c in range(4):
                sp.dma_start(xres[:, 8 * c:8 * c + 8, :], x_tok[:, 8 * c:8 * c + 8, :]).then_inc(x_in[c], 16)
            sp.dma_start(ctx_sb[:, :, :], a["ctx_1024"].rearrange("b i d -> i b d")).then_inc(c_in, 16)
            with sp.Fori(0, B // 2) as h:
                for u in range(2):
                    sp.wait_ge(s_y, h * 2 + u + 1)
                    sp.dma_start(dscr[bass.ds(h * 2 + u, 1), :, :].rearrange("a i j -> (a i) j"),
                                 ysq[u][:, :]).then_inc(d_out[u], 16)
            for u in range(2):
                sp.wait_ge(d_out[u], 16 * (B // 2))
            sp.wait_ge(s_init, 2)
            for lane in range(1, LANES):
                sp.dma_start(dskew[lane::LANES, :, WCOL * (lane - 1):WCOL * (lane - 1) + S],
                             dscr[:, RPL * (lane - 1):RPL * lane, :]).then_inc(d_in[lane], 16)
            sp.wait_ge(s_zb, 1)
            k["zero_fill"](sp, zbuf)
            for lane in range(LANES):
                sp.wait_ge(s_dp, (max(lane - 1, 0) + NCOL) * (2 * RPL + 1))
                o = PADL - 1 + WCOL * max(lane - 1, 0)
                sp.dma_start(rrow[lane::LANES, :, :], rskew[lane::LANES, :, o:o + S + 1]).then_inc(r_un, 16)
            sp.wait_ge(s_gch, 8)
            for lane in range(LANES - 1, 0, -1):
                sp.dma_start(chain_tab[:, RPL * (lane - 1):RPL * lane, :], gv[lane::LANES, :, :]).then_inc(t_in[lane], 16)
            sp.wait_ge(k["s_zero"], 16 * k["n_zero"])

        @block.gpsimd
        def _(pool):
            pool.memset(zbuf[:, :], 0.0).then_inc(s_zb, 1)
            pool.memset(dskew, BIG).then_inc(s_init, 1)
            pool.memset(rskew, BIG).then_inc(s_init, 1)
            pool.iota(jr[:, :, :], pattern=[[512, RPL], [1, S]], base=1, channel_multiplier=0,
                      allow_small_or_imprecise_dtypes=True).then_inc(s_dmp, 1)
            pool.wait_ge(s_init, 2)
            pool.dma_start(rskew[1::LANES, 0, PADL - 1:PADL], a["zeros"][0:B, :]).then_inc(s_corner, 16)

            def squares(b, u):
                pool.wait_ge(s_xT, b + 1)
                pool.tensor_tensor(xsq[u], xT[u][:, :, :], xT[u][:, :, :], ALU.mult).then_inc(s_sq, 1)

            def residual(b, u):
                pool.wait_ge(s_ysq, b + 1)
                pool.tensor_tensor(d2[u][:, :], d2[u][:, :], ysq[u][:, :], ALU.subtract).then_inc(s_res, 1)
                pool.wait_ge(s_cor, b + 1)
                pool.tensor_tensor(ysq[u][:, :], y0[u][:, :], d2[u][:, :], ALU.add).then_inc(s_y, 1)

            squares(0, 0)
            squares(1, 1)
            residual(0, 0)
            with pool.Fori(1, B // 2) as h:
                squares(h * 2, 0)
                residual(h * 2 - 1, 1)
                squares(h * 2 + 1, 1)
                residual(h * 2, 0)
            residual(B - 1, 1)

        @block.scalar
        def _(act):
            act.wait_ge(c_in, 16)
            for b in range(B):
                if b == 4:
                    act.wait_ge(s_var, 1)
                    act.activation(lnt[:, 1, :], lnt[:, 0, :], ACT.Sqrt).then_inc(s_root, 1)
                if b >= 2:
                    act.wait_ge(s_aa, b - 1)
                act.activation(ysq[b % 2][:, :], ctx_sb[:, b, :], ACT.Square, accum_out=aa[:, b:b + 1]).then_inc(s_aa, 1)
            act.wait_ge(s_aa, B)

            def root(b, u, fresh=False):
                act.wait_ge(s_dd, b + 1)
                if not fresh:
                    act.wait_ge(s_y, b - 1)
                act.activation(d2[u][:, :], dps[u][0:C, 0:S], ACT.Relu, bias=aa[:, bass.ds(b, 1)], scale=-2.0).then_inc(s_d2, 1)
                act.wait_ge(s_d2, b + 1)
                act.activation(y0[u][:, :], d2[u][:, :], ACT.Sqrt).then_inc(s_y0, 1)
                act.wait_ge(s_y0, b + 1)
                if not fresh:
                    act.wait_ge(d_out[u], (b - u) * 8)
                act.activation(ysq[u][:, :], y0[u][:, :], ACT.Square).then_inc(s_ysq, 1)

            root(0, 0, fresh=True)
            root(1, 1, fresh=True)
            with act.Fori(1, B // 2) as h:
                root(h * 2, 0)
                root(h * 2 + 1, 1)

        @block.tensor
        def _(pe):
            pe.wait_ge(s_cst, 16)
            pe.wait_ge(c_in, 16)

            def turn(b, u, fresh=False):
                if not fresh:
                    pe.wait_ge(s_cTs, b - 1)
                pe.wait_ge(s_ctp, b + 1)
                for i in range(TPB):
                    for kb in range(KD):
                        ins = pe.transpose(tpx[u][:, kb, i * P:(i + 1) * P], xn[u][:, i, kb * P:(kb + 1) * P], ident)
                ins.then_inc(s_tp, 1)
                for kb in range(KD):
                    ins = pe.transpose(tpc[u][:, kb, 0:C], path[u][:, kb * P:(kb + 1) * P], ident[0:C, 0:C])
                ins.then_inc(s_cT, 1)

            def products(b, u, fresh=False):
                if not fresh:
                    pe.wait_ge(s_d2, b - 1)
                pe.wait_ge(s_cTs, b + 1)
                for kb in range(KD):
                    pe.matmul(dps[u][0:C, 0:S], cT[u][:, kb, :], xT[u][:, kb, :], start=(kb == 0), stop=False)
                pe.wait_ge(s_sq, b + 1)
                for kb in range(KD):
                    ins = pe.matmul(dps[u][0:C, 0:S], halfneg[:, :], xsq[u][:, kb, :], start=False, stop=(kb == KD - 1))
                ins.then_inc(s_dd, 1)

            pe.wait_ge(s_bt, 1)
            turn(0, 0, fresh=True)
            turn(1, 1, fresh=True)
            products(0, 0, fresh=True)
            turn(2, 0)
            products(1, 1, fresh=True)
            with pe.Fori(1, B // 2 - 1) as h:
                turn(h * 2 + 1, 1)
                products(h * 2, 0)
                turn(h * 2 + 2, 0)
                products(h * 2 + 1, 1)
            turn(B - 1, 1)
            products(B - 2, 0)
            products(B - 1, 1)
            pe.wait_ge(s_c2, 1)
            pe.transpose(tpx[0][0:C, 0, 0:B], c2[:, 0:C], ident[0:B, 0:B])
            pe.transpose(tpx[0][0:C, 0, B:2 * B], c2[:, 1:C + 1], ident[0:B, 0:B]).then_inc(s_c2t, 1)
            def expand(b, u, fresh=False):
                if not fresh:
                    pe.wait_ge(s_add, b - 1)
                pe.wait_ge(s_path, b + 1)
                for i in range(TPB):
                    ins = pe.matmul(xps[u][:, i, :], path[u][:, i * P:(i + 1) * P],
                                    ctx_sb[:, bass.ds(b, 1), :].rearrange("p a d -> p (a d)"), start=True, stop=True)
                ins.then_inc(s_ex, 1)

            expand(0, 0, fresh=True)
            expand(1, 1, fresh=True)
            with pe.Fori(1, B // 2) as h:
                expand(h * 2, 0)
                expand(h * 2 + 1, 1)

        @block.vector
        def _(dve):
            dve.memset(halfneg[:, :], -0.5).then_inc(s_bt, 1)
            chain = Chain(dve, s_dve)
            dve.wait_ge(s_cst, 16)
            dve.tensor_scalar(iota15[:, :], cst[0:C, C_IOTA:C_IOTA + S], 1.5, None, ALU.add).then_inc(s_bt, 1)
            dve.tensor_scalar(iota2[:, :], cst[0:C, C_IOTA:C_IOTA + S], 2.0, None, ALU.add).then_inc(s_bt, 1)
            k["load_stats"](dve, x_in, s_st)
            k["moments"](chain, dve)
            k["rstd_steps"](dve, chain, s_var, s_root)
            dve.wait_ge(c_in, 16)

            def fetch(b, u):
                for i in range(TPB):
                    k["norm_tile"](dve, xn[u][:, i, :], b * TPB + i)
                dve.tensor_copy(path[u][:, :], flat2(ctx_sb[:, bass.ds(b, 1), :])).then_inc(s_ctp, 1)

            def turned(b, u):
                dve.wait_ge(s_tp, b + 1)
                dve.tensor_copy(xT[u][:, :, :], tpx[u][:, :, :]).then_inc(s_xT, 1)
                dve.wait_ge(s_cT, b + 1)
                dve.tensor_copy(cT[u][:, :, :], tpc[u][:, :, 0:C]).then_inc(s_cTs, 1)

            def correction(b, u):
                dve.wait_ge(s_y0, b + 1)
                dve.tensor_scalar(ri[u][:, :].bitcast(I32), y0[u][:, :].bitcast(I32), -1.0, float(0x7EF311C7),
                                  ALU.mult, ALU.add).then_inc(s_ri, 1)
                dve.wait_ge(s_ri, b + 1)
                dve.wait_ge(s_res, b + 1)
                dve.scalar_tensor_tensor(d2[u][:, :], d2[u][:, :], 0.5, ri[u][:, :], ALU.mult, ALU.mult).then_inc(s_cor, 1)

            fetch(0, 0)
            fetch(1, 1)
            turned(0, 0)
            fetch(2, 0)
            turned(1, 1)
            fetch(3, 1)
            correction(0, 0)
            with dve.Fori(1, B // 2 - 1) as h:
                turned(h * 2, 0)
                fetch(h * 2 + 2, 0)
                correction(h * 2 - 1, 1)
                turned(h * 2 + 1, 1)
                fetch(h * 2 + 3, 1)
                correction(h * 2, 0)
            turned(B - 2, 0)
            correction(B - 3, 1)
            turned(B - 1, 1)
            correction(B - 2, 0)
            correction(B - 1, 1)
            dve.wait_ge(s_corner, 16)
            dp = Chain(dve, s_dp)
            mask = [max(q - 1, 0) for q in range(32)]
            for s in range(STEPS):
                o = s * WCOL + PADL
                if s + 1 < LANES:
                    dve.wait_ge(d_in[s + 1], 16)
                dp(dve.stream_shuffle(rskew[:, 0, o:o + WCOL], rskew[:, RPL, o - WCOL:o], mask))
                for r in range(RPL):
                    dp(dve.tensor_tensor(minw[:, :], rskew[:, r, o:o + WCOL], rskew[:, r, o - 1:o + WCOL - 1], ALU.min))
                    dp(dve.tensor_tensor_scan(rskew[:, r + 1, o:o + WCOL], minw[:, :], dskew[:, r, s * WCOL:(s + 1) * WCOL],
                                              rskew[:, r + 1, o - 1:o], ALU.min, ALU.add))
            g = Chain(dve, s_gch)
            dve.wait_ge(r_un, 16 * LANES)
            dve.wait_ge(s_dmp, 1)
            over, diag, left = rrow[:, 0:RPL, 1:S + 1], rrow[:, 0:RPL, 0:S], rrow[:, 1:RPL + 1, 0:S]
            g(dve.tensor_tensor(up[:, :, :], over, diag, ALU.is_lt))
            g(dve.scalar_tensor_tensor(up[:, :, :], up[:, :, :], 0.75, jr[:, :, :], ALU.mult, ALU.add))
            g(dve.tensor_tensor(gv[:, :, :], over, diag, ALU.min))
            g(dve.tensor_tensor(gv[:, :, :], gv[:, :, :], left, ALU.is_le))
            g(dve.tensor_tensor(up[:, :, :], up[:, :, :], gv[:, :, :], ALU.mult))
            flat = up[:, :, :].rearrange("p r w -> p (r w)")
            runs = rrow[:, :, :].rearrange("p r w -> p (r w)")[:, 0:RPL * S]
            g(dve.tensor_tensor_scan(runs, flat, flat, 0.0, ALU.max, ALU.max))
            run3 = runs.rearrange("p (r w) -> p r w", w=S)
            g(dve.tensor_tensor(gv[:, :, 1:S], run3[:, :, 1:S], run3[:, :, 0:S - 1], ALU.subtract))
            g(dve.scalar_tensor_tensor(gv[:, :, 0:1], run3[:, :, 0:1], 1.0, jr[:, :, 0:1], ALU.add, ALU.subtract))
            dve.memset(c2[:, :], float(S + 1)).then_inc(s_bt, 1)
            for lane in range(LANES - 1, 0, -1):
                dve.wait_ge(t_in[lane], 16)
                for r in range(RPL - 1, -1, -1):
                    i = RPL * (lane - 1) + r
                    dve.wait_ge(s_bt, 4 + C - 1 - i)
                    dve.scalar_tensor_tensor(junk[:, :], iota15[0:B, :], c2[:, i + 1:i + 2], chain_tab[:, i, :],
                                             ALU.is_le, ALU.mult, accum_out=c2[:, i:i + 1]).then_inc(s_bt, 1)
            dve.wait_ge(s_bt, 4 + C)
            dve.engine_nop().then_inc(s_c2, 1)
            dve.wait_ge(s_c2t, 1)
            dve.tensor_copy(cs[:, :, :], tpx[0][0:C, 0, 0:2 * B].rearrange("p (a b) -> p a b", a=2)).then_inc(s_cs, 1)
            dve.wait_ge(s_cs, 1)
            def paths(b, u):
                dve.tensor_scalar(pm[u], iota2[:, :], cs[:, 0, bass.ds(b, 1)], None, ALU.is_gt).then_inc(s_pm, 1)
                dve.wait_ge(s_pm, b + 1)
                dve.scalar_tensor_tensor(path[u][:, :], iota15[:, :], cs[:, 1, bass.ds(b, 1)], pm[u],
                                         ALU.is_le, ALU.mult).then_inc(s_path, 1)

            def add_rows(b, u, first=False):
                if not first:
                    dve.wait_ge(s_add, b)
                dve.wait_ge(s_ex, b + 1)
                xb = xres[:, bass.ds(b * TPB, TPB), :]
                dve.tensor_tensor(xb, xps[u][:, :, :], xb, ALU.add).then_inc(s_add, 1)
                if not first:
                    stats(b - 1)

            def stats(b):
                for i in range(TPB):
                    t = b * TPB + i
                    dve.bn_stats(flat2(st6[:, bass.ds(t, 1), :]), flat2(xres[:, bass.ds(t, 1), :])).then_inc(s_st2, 1)

            paths(0, 0)
            paths(1, 1)
            add_rows(0, 0, first=True)
            paths(2, 0)
            add_rows(1, 1)
            with dve.Fori(1, B // 2 - 1) as h:
                paths(h * 2 + 1, 1)
                add_rows(h * 2, 0)
                paths(h * 2 + 2, 0)
                add_rows(h * 2 + 1, 1)
            paths(B - 1, 1)
            add_rows(B - 2, 0)
            add_rows(B - 1, 1)
            dve.wait_ge(s_add, B)
            stats(B - 1)


def phase_moe0(nc, a, k):
    sb, pb, sem = k["sb"], k["pb"], k["sem"]
    cst, ident, xres, rstd, nmr, lnt = (k[n] for n in ("cst", "ident", "xres", "rstd", "nmr", "lnt"))
    xs, ys, rows, slots, wk = (k[n] for n in ("xs0", "ys0", "rows", "slots", "wk"))
    NE, G4 = E0, E0 // GRP
    NG = TOK // 512
    with ExitStack() as ctx:
        w13 = sb(ctx, "e_w13", [P, KD, NE, 2 * I0])
        w2 = sb(ctx, "e_w2", [P, NE, D])
        b13 = sb(ctx, "e_b13", [P, NE, 2])
        w13_now = [sb(ctx, f"e_w13_now{g}", [P, U0, KD, 2 * I0]) for g in range(2)]
        b2 = sb(ctx, "e_b2", [P, NE, D])
        ws1 = sb(ctx, "e_ws1", [P, KD, 2 * I0])
        ws3 = sb(ctx, "e_ws3", [P, KD, 2 * I0])
        ws2 = sb(ctx, "e_ws2", [P, KD, D])
        bs13 = sb(ctx, "e_bs13", [P, 2, KD])
        bs2 = sb(ctx, "e_bs2", [P, D])
        gw = sb(ctx, "e_gw", [P, KD, NE])
        gb = sb(ctx, "e_gb", [P, NE])
        xT = sb(ctx, "e_xT", [P, NG, KD * 512])
        xT4 = xT[:, :, :].rearrange("p g (k n) -> p g k n", k=KD)
        EARLY = 3
        stage = [rows[u // 4][:, u % 4, :] for u in range(8)]
        arena = sb(ctx, "e_arena", [P, 3072])
        shared_buf = [sb(ctx, f"e_sh{i}", [P, 1024]) for i in range(2)]
        gsh, ssh = ([buf[:, 512 * i:512 * i + 512] for i in range(KD)] for buf in shared_buf)
        gate_xT = [buf[:, :].rearrange("p (c k n) -> p c k n", c=2, k=KD) for buf in shared_buf]
        def expert_buf(o, w):
            flat = xT[:, :, :].rearrange("p g n -> p (g n)")
            return [flat[:, o + w * g:o + w * (g + 1)].rearrange("p (u n) -> p u n", u=U0) for g in range(2)]
        xinT = [v.rearrange("p u (k n) -> p u k n", k=KD) for v in expert_buf(0, 1024)]
        yo, sg, gT = expert_buf(2048, 1024), expert_buf(4096, 512), expert_buf(5120, 512)
        big = [arena[:, 512 * i:512 * i + 512].rearrange("p (t e) -> p t e", e=NE) for i in range(6)]
        sr, scb, oh1, oh2, t3, mask = big[0], big[1], big[2], big[3], big[4], big[5]
        score_T = [arena[0:NE, 512 * (1 + u):512 * (2 + u)] for u in range(2)]
        small = sb(ctx, "e_small", [P, 8, NT * G4])
        em = sb(ctx, "e_em", [P, NE])
        mx, t1 = small[:, 0, 0:NT], small[:, 1, 0:NT]
        etile = sb(ctx, "e_etile", [1, NTL0 // U0], I32)
        E_BITS = NE.bit_length() - 1
        place = sb(ctx, "e_place", [1, U0])
        r = {"totE": mask.rearrange("p t e -> p (t e)").rearrange("p (e t) -> p e t", e=NE), "t3": t3, "mask": mask,
             "cum": scb.rearrange("p t e -> p (t e)").rearrange("p (e t) -> p e t", e=NE), "sst": sb(ctx, "e_sst", [P, NE + 1])[:, :],
             "ti": sb(ctx, "e_ti", [P, NE], I32)[:, :], "red": small[:, 2, 0:NT],
             "cmp": arena[0:1, 0:NTL0 * NE].rearrange("p (t e) -> p t e", e=NE), "tsum": sb(ctx, "e_tsum", [1, NTL0])[:, :],
             "words": sb(ctx, "e_words", [1, NTL0 // U0])[:, :]}
        for i, n in enumerate(("cnt", "tl", "tend", "delta")):
            r[n] = small[:, 3 + i, 0:NE]
        bank = [pb(ctx, f"e_bank{u}", [P, 512]) for u in range(8)]

        w_in = [sem(f"e_w_in{i}") for i in range(5)]
        (s_var, s_root, s_dve, s_xn, s_tp, s_xT, s_xTall, s_gs, s_gate, s_exp, s_max, s_mask, s_rank, s_slot) = (
            sem("e_" + n) for n in ("var", "root", "dve", "xn_s", "tp", "xT_s", "xTall", "gs", "gate", "exp", "max",
                                    "mask", "rank", "slot"))
        s_h1, s_si, s_gsh, s_zp, s_z, s_row = (sem("e_" + n) for n in ("h1", "si", "gsh_s", "zp", "z", "row"))
        sct = [sem(f"e_sct{u}") for u in range(8)]
        x_in = [sem(f"e_x_in{g}") for g in range(2)]
        y_out = [sem(f"e_y_out{g}") for g in range(2)]
        s_xt, s_xe, s_wa, s_wb, s_hh, s_sg, s_g, s_yp, s_yo = (
            sem("e_" + n) for n in ("xt", "xe", "wa", "wb", "hh", "sg_s", "g", "yp", "yo_s"))
        s_c0, s_gpool = sem("e_c0"), sem("e_gpool")
        s_sT, s_back = sem("e_sT"), sem("e_back")

        NH = NTL0 // (2 * U0)

        def first(h, g):
            return h * (2 * U0) + g * U0

        def experts(eng, h, g):
            word = eng.value_load(etile[0:1, bass.ds(h * 2 + g, 1)], min_val=0, max_val=NE ** U0 - 1)
            return [(word >> (E_BITS * u)) & (NE - 1) for u in range(U0)]

        def first_weights(g, u, e, j):
            cols = slice(j * I0, (j + 1) * I0)
            return w13_now[g][:, u, :, cols], flat2b(w13[:, :, bass.ds(e, 1), cols])

        block = ctx.enter_context(nc.Block())

        @block.sync
        def _(sp):
            for old in k["old_sems"]:
                sp.sem_clear(old)
            sp.dma_start(gw[:, :, :], a["gate_w"]).then_inc(w_in[0], 16)
            sp.dma_start(gb[:, :], a["L0_ffn_gate_b"].partition_broadcast(P)).then_inc(w_in[0], 16)
            for dst, name in ((ws1, "ws1"), (ws3, "ws3"), (ws2, "ws2")):
                sp.dma_start(dst[:, :, :], a[name]).then_inc(w_in[1], 16)
            sp.dma_start(bs13[:, :, :], a["bs13"]).then_inc(w_in[1], 16)
            sp.dma_start(bs2[:, :], a["L0_ffn_bs2"].partition_broadcast(P)).then_inc(w_in[2], 16)
            sp.dma_start(w13[:, :, :, :], a["w13"]).then_inc(w_in[3], 16)
            sp.dma_start(w2[:, :, :], a["w2"]).then_inc(w_in[3], 16)
            sp.dma_start(b13[:, :, :], a["b13"]).then_inc(w_in[3], 16)
            sp.dma_start(b2[:, :, :].rearrange("p e n -> p (e n)"),
                         a["L0_ffn_be2"].rearrange("e n -> (e n)").partition_broadcast(P)).then_inc(w_in[4], 16)
            for u in range(8):
                sp.wait_ge(sct[u], 16 * K0 * NT // 8)

            def tiles(dram, h, g):
                return dram[bass.ds(first(h, g) * P, U0 * P), :].rearrange("(u p) d -> p u d", p=P)

            def load(h, g):
                sp.dma_start(rows[g][:, :, :], tiles(xs, h, g)).then_inc(x_in[g], 16)

            def reload(h, g):
                sp.wait_ge(s_xt, first(h - 1, g) + U0)
                load(h, g)

            def store(h, g):
                sp.wait_ge(s_yo, first(h, g) + U0)
                sp.dma_start(tiles(ys, h, g), yo[g]).then_inc(y_out[g], 16)

            load(0, 0)
            load(0, 1)
            reload(1, 0)
            reload(1, 1)
            store(0, 0)
            with sp.Fori(2, NH) as h:
                reload(h, 0)
                store(h - 2, 1)
                reload(h, 1)
                store(h - 1, 0)
            store(NH - 2, 1)
            store(NH - 1, 0)
            store(NH - 1, 1)
            for g in range(2):
                sp.wait_ge(y_out[g], 16 * NH)

        @block.gpsimd
        def _(pool):
            with pool.Fori(0, EARLY) as g:
                for i in range(KD):
                    pool.wait_ge(s_si, g * 4 + 2 * i + 2)
                    pool.tensor_tensor(gsh[i], gsh[i], ssh[i], ALU.mult).then_inc(s_gpool, 1)
            pool.wait_ge(s_slot, 1)
            for t in range(NT):
                pool.wait_ge(s_row, t + 1)
                for i in range(K0):
                    pool.indirect_dma_start(out=xs, out_offset=bass.IndirectOffsetOnAxis(ap=slots[i][:, t:t + 1], axis=0),
                                            in_=stage[t % 8], in_offset=None).then_inc(sct[t % 8], 16)
            pool.wait_ge(w_in[3], 48)
            pool.wait_ge(s_slot, 2)

            def weights(h, g, fresh=False):
                es = experts(pool, h, g)
                for u in range(U0):
                    if not fresh:
                        pool.wait_ge(s_hh, first(h - 1, g) + u + 1)
                    pool.tensor_copy(*first_weights(g, u, es[u], 0)).then_inc(s_wa, 1)

            weights(0, 0, fresh=True)
            weights(0, 1, fresh=True)
            with pool.Fori(1, NH) as h:
                weights(h, 0)
                weights(h, 1)

        @block.scalar
        def _(act):
            act.wait_ge(s_var, 1)
            act.activation(lnt[:, 1, :], lnt[:, 0, :], ACT.Sqrt).then_inc(s_root, 1)

            def turned(g, u):
                for c in range(2):
                    act.wait_ge(s_tp, g * 2 + c + 1)
                    act.copy(flat3(xT4[:, bass.ds(g, 1), :, c * 256:(c + 1) * 256]),
                             bank[2 * u + c][:, :].rearrange("p (k n) -> p k n", k=KD)).then_inc(s_xTall, 1)

            def scores_out(g, u):
                act.wait_ge(s_gs, g + 1)
                act.copy(score_T[u], bank[6 + u][0:NE, :]).then_inc(s_sT, 1)

            turned(0, 0)
            turned(1, 1)
            scores_out(0, 0)
            with act.Fori(1, NG // 2) as h:
                turned(h * 2, 0)
                scores_out(h * 2 - 1, 1)
                turned(h * 2 + 1, 1)
                scores_out(h * 2, 0)
            scores_out(NG - 1, 1)
            act.wait_ge(s_max, 1)
            act.activation(scb, sr, ACT.Exp).then_inc(s_exp, 1)
            act.wait_ge(w_in[1], 64)
            with act.Fori(0, NG) as g:
                for i in range(KD):
                    act.wait_ge(s_h1, g * 4 + 2 * i + 1)
                    act.activation(ssh[i], bank[2 * i][:, :], ACT.Silu, bias=bs13[:, 0, i:i + 1]).then_inc(s_si, 1)
                    act.wait_ge(s_h1, g * 4 + 2 * i + 2)
                    act.activation(gsh[i], bank[2 * i + 1][:, :], ACT.Identity, bias=bs13[:, 1, i:i + 1]).then_inc(s_si, 1)
                for q in range(2):
                    act.wait_ge(s_zp, g * 2 + q + 1)
                    act.copy(flat2(xT[:, bass.ds(g, 1), q * 512:(q + 1) * 512]), bank[4 + q][:, :]).then_inc(s_z, 1)

            def turned_in(h, g):
                for u in range(U0):
                    act.wait_ge(s_xt, first(h, g) + u + 1)
                    act.copy(xinT[g][:, u, :, :], bank[4 * g + u][:, 0:D].rearrange("p (k n) -> p k n", k=KD)).then_inc(s_xe, 1)

            def weights(g, es):
                for u in range(U0):
                    act.copy(*first_weights(g, u, es[u], 1)).then_inc(s_wb, 1)

            def silu(h, g, es):
                for u in range(U0):
                    act.wait_ge(s_hh, first(h, g) + u + 1)
                    act.activation(sg[g][:, u, :], bank[4 * g + u][:, D:D + P], ACT.Silu,
                                   bias=flat2(b13[:, bass.ds(es[u], 1), 0:1])).then_inc(s_sg, 1)

            def half(h, g, h_next, g_next, es):
                turned_in(h, g)
                es_next = experts(act, h_next, g_next)
                weights(g_next, es_next)
                silu(h, g, es)
                return es_next

            act.wait_ge(w_in[3], 48)
            act.wait_ge(s_slot, 2)
            es = experts(act, 0, 0)
            weights(0, es)
            es = half(0, 0, 0, 1, es)
            half(0, 1, 1, 0, es)
            with act.Fori(1, NH - 1) as h:
                es = half(h, 0, h, 1, experts(act, h, 0))
                half(h, 1, h + 1, 0, es)
            es = half(NH - 1, 0, NH - 1, 1, experts(act, NH - 1, 0))
            turned_in(NH - 1, 1)
            silu(NH - 1, 1, es)

        @block.tensor
        def _(pe):
            pe.wait_ge(w_in[0], 32)
            def turn(g, u, fresh=False, turned_later=None, fresh_scores=False):
                for c in range(2):
                    if c == 1 and turned_later is not None:
                        scores_ready(turned_later, fresh_scores)
                    if not fresh:
                        pe.wait_ge(s_xTall, g * 2 + c - 3)
                    pe.wait_ge(s_xn, g * 2 + c + 1)
                    for i in range(2):
                        for kb in range(KD):
                            ins = pe.transpose(bank[2 * u + c][:, kb * 256 + i * P:kb * 256 + (i + 1) * P],
                                               rows[u][:, 2 * c + i, kb * P:(kb + 1) * P], ident)
                    ins.then_inc(s_tp, 1)

            def scores(g, u):
                pe.wait_ge(s_xT, g * 2 + 2)
                for kb in range(KD):
                    ins = pe.matmul(bank[6 + u][0:NE, :].rearrange("p (c n) -> p c n", c=2), gw[:, kb, :], gate_xT[u][:, :, kb, :],
                                    start=(kb == 0), stop=(kb == KD - 1))
                ins.then_inc(s_gs, 1)

            def scores_ready(g, fresh=False):
                if not fresh:
                    pe.wait_ge(s_gate, g - 1)
                pe.wait_ge(s_sT, g + 1)

            def turn_scores(g, u):
                for i in range(4):
                    ins = pe.transpose(bank[4 + u][:, i * NE:(i + 1) * NE], score_T[u][:, i * P:(i + 1) * P], ident[0:NE, 0:NE])
                ins.then_inc(s_back, 1)

            turn(0, 0, fresh=True)
            turn(1, 1, fresh=True)
            scores(0, 0)
            turn(2, 0, turned_later=0, fresh_scores=True)
            turn_scores(0, 0)
            scores(1, 1)
            turn(3, 1, turned_later=1, fresh_scores=True)
            turn_scores(1, 1)
            scores(2, 0)
            with pe.Fori(2, NT // 8) as h:
                turn(h * 2, 0, turned_later=h * 2 - 2)
                turn_scores(h * 2 - 2, 0)
                scores(h * 2 - 1, 1)
                turn(h * 2 + 1, 1, turned_later=h * 2 - 1)
                turn_scores(h * 2 - 1, 1)
                scores(h * 2, 0)
            scores_ready(NT // 4 - 2)
            turn_scores(NT // 4 - 2, 0)
            scores(NT // 4 - 1, 1)
            scores_ready(NT // 4 - 1)
            turn_scores(NT // 4 - 1, 1)
            pe.wait_ge(w_in[1], 64)
            pe.wait_ge(s_xTall, 2 * NG)
            pe.wait_ge(s_gate, NG)

            def shared(g, s_gated, g_gated, fresh=False, between=None):
                for i in range(KD):
                    for j, w in enumerate((ws1, ws3)):
                        for kb in range(KD):
                            ins = pe.matmul(bank[2 * i + j][:, :], w[:, kb, i * P:(i + 1) * P],
                                            flat2(flat2b(xT4[:, bass.ds(g, 1), kb:kb + 1, :])), start=(kb == 0), stop=(kb == KD - 1))
                        ins.then_inc(s_h1, 1)
                if between:
                    between()
                for q in range(4):
                    if q == 0 and not fresh:
                        pe.wait_ge(s_z, g * 2)
                    for i in range(KD):
                        pe.wait_ge(s_gated, (g_gated * 2) + i + 1)
                        ins = pe.matmul(bank[4 + q // 2][:, (q % 2) * D:(q % 2 + 1) * D], gsh[i][:, q * P:(q + 1) * P], ws2[:, i, :],
                                        start=(i == 0), stop=(i == KD - 1))
                    if q % 2 == 1:
                        ins.then_inc(s_zp, 1)

            def counts():
                pe.wait_ge(s_mask, 1)
                pe.matmul(bank[6][:, :], cst[:, C_TRI:C_TRI + P], mask.rearrange("p t e -> p (t e)"), start=True, stop=True)
                pe.matmul(bank[7][:, :], cst[:, C_ONE:C_ONE + P], mask.rearrange("p t e -> p (t e)"), start=True, stop=True).then_inc(s_rank, 1)

            shared(0, s_gpool, 0, fresh=True)
            shared(1, s_gpool, 1, between=counts)
            shared(EARLY - 1, s_gpool, EARLY - 1)
            with pe.Fori(EARLY, NG) as g:
                shared(g, s_gsh, g - EARLY)
            pe.wait_ge(w_in[3], 48)
            pe.wait_ge(s_z, 2 * NG)
            pe.wait_ge(s_slot, 2)
            pe.wait_ge(s_c0, 2 * NG)

            def turn_in(h, g, fresh=False):
                pe.wait_ge(x_in[g], h * 16 + 16)
                for u in range(U0):
                    if not fresh:
                        pe.wait_ge(s_yo, first(h - 1, g) + u + 1)
                    for kb in range(KD):
                        ins = pe.transpose(bank[4 * g + u][:, kb * P:(kb + 1) * P], rows[g][:, u, kb * P:(kb + 1) * P], ident)
                    ins.then_inc(s_xt, 1)

            def h13(h, g):
                for u in range(U0):
                    n = first(h, g) + u + 1
                    pe.wait_ge(s_xe, n)
                    for j, s_w in enumerate((s_wa, s_wb)):
                        pe.wait_ge(s_w, n)
                        for kb in range(KD):
                            ins = pe.matmul(bank[4 * g + u][:, D + j * P:D + (j + 1) * P], w13_now[g][:, u, kb, j * I0:(j + 1) * I0],
                                            xinT[g][:, u, kb, :], start=(kb == 0), stop=(kb == KD - 1))
                    ins.then_inc(s_hh, 1)

            def out_rows(h, g):
                es = experts(pe, h, g)
                for u in range(U0):
                    pe.wait_ge(s_g, first(h, g) + u + 1)
                    pe.matmul(bank[4 * g + u][:, 0:D], gT[g][:, u, :], flat2(w2[:, bass.ds(es[u], 1), :]), start=True, stop=True).then_inc(s_yp, 1)

            turn_in(0, 0, fresh=True)
            h13(0, 0)
            turn_in(0, 1, fresh=True)
            h13(0, 1)
            out_rows(0, 0)
            with pe.Fori(1, NH) as h:
                turn_in(h, 0)
                h13(h, 0)
                out_rows(h - 1, 1)
                turn_in(h, 1)
                h13(h, 1)
                out_rows(h, 0)
            out_rows(NH - 1, 1)

        @block.vector
        def _(dve):
            chain = Chain(dve, s_dve)
            k["moments"](chain, dve)
            k["rstd_steps"](dve, chain, s_var, s_root)
            dve.wait_ge(w_in[0], 32)
            def normal(g, u):
                for i in range(4):
                    ins = k["norm_tile"](dve, rows[u][:, i, :], g * 4 + i)
                    if i % 2 == 1:
                        ins.then_inc(s_xn, 1)

            def turned(g, u):
                for c in range(2):
                    dve.wait_ge(s_xTall, g * 2 + c + 1)
                    dve.tensor_copy(gate_xT[u][:, c, :, :], flat3(xT4[:, bass.ds(g, 1), :, c * 256:(c + 1) * 256])).then_inc(s_xT, 1)

            def scores(g, u):
                dve.wait_ge(s_back, g + 1)
                dve.tensor_copy(sr[:, bass.ds(g * 4, 4), :], bank[4 + u][:, 0:4 * NE].rearrange("p (t e) -> p t e", e=NE)).then_inc(s_gate, 1)

            normal(0, 0)
            normal(1, 1)
            turned(0, 0)
            normal(2, 0)
            turned(1, 1)
            normal(3, 1)
            with dve.Fori(1, NT // 8 - 1) as h:
                turned(h * 2, 0)
                normal(h * 2 + 2, 0)
                scores(h * 2 - 2, 0)
                turned(h * 2 + 1, 1)
                normal(h * 2 + 3, 1)
                scores(h * 2 - 1, 1)
            turned(NT // 4 - 2, 0)
            scores(NT // 4 - 4, 0)
            turned(NT // 4 - 1, 1)
            scores(NT // 4 - 3, 1)
            scores(NT // 4 - 2, 0)
            scores(NT // 4 - 1, 1)
            dve.wait_ge(s_gate, NT // 4)

            def wide(ap, n=NE):
                return ap.unsqueeze(2).to_broadcast([P, NT, n])

            chain(dve.tensor_reduce(mx, sr, AX.X, ALU.max))
            dve.tensor_tensor(sr, sr, wide(mx), ALU.subtract).then_inc(s_max, 1)
            dve.wait_ge(s_exp, 1)
            chain(dve.tensor_reduce(mx, scb, AX.X, ALU.add))
            chain(dve.reciprocal(t1, mx))
            chain(dve.tensor_tensor(sr, scb, wide(t1), ALU.mult))
            chain(dve.tensor_tensor(scb, sr, gb[:, :].unsqueeze(1).to_broadcast([P, NT, NE]), ALU.add))
            v4 = scb.rearrange("p t (g e) -> p (t g) e", e=GRP)
            hi1, lo1, hi2, lo2, gs, gt = (small[:, i, :] for i in range(6))
            chain(dve.tensor_tensor(hi1, v4[:, :, 0], v4[:, :, 1], ALU.max))
            chain(dve.tensor_tensor(lo1, v4[:, :, 0], v4[:, :, 1], ALU.min))
            chain(dve.tensor_tensor(hi2, v4[:, :, 2], v4[:, :, 3], ALU.max))
            chain(dve.tensor_tensor(lo2, v4[:, :, 2], v4[:, :, 3], ALU.min))
            chain(dve.tensor_tensor(gs, hi1, hi2, ALU.max))
            chain(dve.tensor_tensor(gt, hi1, hi2, ALU.min))
            chain(dve.tensor_tensor(lo1, lo1, lo2, ALU.max))
            chain(dve.tensor_tensor(gt, gt, lo1, ALU.max))
            chain(dve.tensor_tensor(gs, gs, gt, ALU.add))
            rk = small[:, 6, :].rearrange("p (t g) -> p t g", g=G4)
            cc = small[:, 7, :].rearrange("p (t g) -> p t g", g=G4)
            g3 = gs.rearrange("p (t g) -> p t g", g=G4)
            chain(dve.tensor_scalar(rk, cst[:, C_IOTA:C_IOTA + G4].unsqueeze(1).to_broadcast([P, NT, G4]),
                                    -1.0, float(G4 - 1), ALU.mult, ALU.add))
            for d in range(1, G4):
                chain(dve.tensor_tensor(cc[:, :, 0:G4 - d], g3[:, :, 0:G4 - d], g3[:, :, d:G4], ALU.is_ge))
                chain(dve.tensor_tensor(rk[:, :, d:G4], rk[:, :, d:G4], cc[:, :, 0:G4 - d], ALU.add))
                chain(dve.tensor_tensor(rk[:, :, 0:G4 - d], rk[:, :, 0:G4 - d], cc[:, :, 0:G4 - d], ALU.subtract))
            chain(dve.tensor_scalar(small[:, 6, :], small[:, 6, :], 1.5, -BIG, ALU.is_gt, ALU.mult))
            chain(dve.tensor_tensor(v4, v4, small[:, 6, :].unsqueeze(2).to_broadcast([P, NT * G4, GRP]), ALU.add))
            chain(dve.tensor_scalar(em[:, :], cst[:, C_IOTA:C_IOTA + NE], float(-NE), None, ALU.add))
            pick_first_max(dve, chain, oh1, mx, scb, em[:, :], t3, t1, NE)
            chain(dve.scalar_tensor_tensor(scb, oh1, -2.0 * BIG, scb, ALU.mult, ALU.add))
            pick_first_max(dve, chain, oh2, mx, scb, em[:, :], t3, t1, NE)
            assign_slots(dve, chain, r, (oh1, oh2), [s[:, :] for s in slots], NE,
                         bank[6][:, :].rearrange("p (t e) -> p t e", e=NE), bank[7][:, :].rearrange("p (t e) -> p t e", e=NE),
                         s_mask, s_rank)
            dve.engine_nop().then_inc(s_slot, 1)
            def row(t):
                if t >= 8:
                    dve.wait_ge(sct[t % 8], 16 * K0 * (t // 8))
                k["norm_tile"](dve, stage[t % 8], t).then_inc(s_row, 1)

            def add_shared(g):
                xg = xres[:, 4 * g:4 * g + 4, :]
                dve.wait_ge(s_row, 4 * g + 4)
                dve.wait_ge(s_z, 2 * g + 2)
                add(dve.tensor_tensor(xg, xg, xT[:, g, :].rearrange("p (q d) -> p q d", q=4), ALU.add))
                add(dve.tensor_tensor(xg, xg, bs2[:, :].unsqueeze(1).to_broadcast([P, 4, D]), ALU.add))

            add = Chain(dve, s_c0)
            dve.wait_ge(w_in[2], 16)
            per = (NT - 8) // (NG - EARLY + 1) + 1
            for t in range(8):
                row(t)
            t, added = 8, 0
            for g in range(EARLY, NG):
                for i in range(KD):
                    dve.wait_ge(s_si, g * 4 + 2 * i + 2)
                    dve.tensor_tensor(gsh[i], gsh[i], ssh[i], ALU.mult).then_inc(s_gsh, 1)
                for t in range(t, min(t + per, NT)):
                    row(t)
                t += 1
                while added < t // 4 - 1:
                    add_shared(added)
                    added += 1
            for i, oh in enumerate((oh1, oh2)):
                chain(dve.tensor_tensor(t3, sr, oh, ALU.mult))
                chain(dve.tensor_reduce(wk[:, i, :], t3, AX.X, ALU.add))
            assign_tiles(dve, chain, r, r["tsum"], NE, NTL0, cst)
            for u in range(U0):
                chain(dve.memset(place[:, u:u + 1], float(NE ** u)))
            packed = r["cmp"].rearrange("p t e -> p (t e)")[:, 0:NTL0].rearrange("p (g u) -> p g u", u=U0)
            chain(dve.tensor_tensor(packed, r["tsum"].rearrange("p (g u) -> p g u", u=U0),
                                    place[:, :].unsqueeze(1).to_broadcast([1, NTL0 // U0, U0]), ALU.mult))
            chain(dve.tensor_reduce(r["words"], packed, AX.X, ALU.add))
            chain(dve.tensor_copy(etile[:, :], r["words"]))
            dve.engine_nop().then_inc(s_slot, 1)
            for g in range(added, NG):
                add_shared(g)
            dve.wait_ge(w_in[3], 48)
            dve.wait_ge(w_in[4], 16)

            def gated(h, g, es):
                for u in range(U0):
                    dve.wait_ge(s_sg, first(h, g) + u + 1)
                    dve.scalar_tensor_tensor(gT[g][:, u, :], bank[4 * g + u][:, D + P:2 * D], flat2(b13[:, bass.ds(es[u], 1), 1:2]),
                                             sg[g][:, u, :], ALU.add, ALU.mult).then_inc(s_g, 1)

            def results(h, g, es, fresh=False):
                if not fresh:
                    dve.wait_ge(y_out[g], h * 16)
                for u in range(U0):
                    dve.wait_ge(s_yp, first(h, g) + u + 1)
                    dve.tensor_tensor(yo[g][:, u, :], bank[4 * g + u][:, 0:D], flat2(b2[:, bass.ds(es[u], 1), :]), ALU.add).then_inc(s_yo, 1)

            def half(h, g, h_before, g_before, es_before=None, fresh=False):
                es = experts(dve, h, g)
                es_before = es_before or experts(dve, h_before, g_before)
                results(h_before, g_before, es_before, fresh)
                gated(h, g, es)
                return es

            es = experts(dve, 0, 0)
            gated(0, 0, es)
            half(0, 1, 0, 0, es, fresh=True)
            es = half(1, 0, 0, 1, fresh=True)
            half(1, 1, 1, 0, es)
            with dve.Fori(2, NH) as h:
                es = half(h, 0, h - 1, 1)
                half(h, 1, h, 0, es)
            results(NH - 1, 1, experts(dve, NH - 1, 1))


def phase_xattn(nc, a, k):
    sb, sem = k["sb"], k["sem"]
    pb = k["pb"]
    cst, ident, xres, st6, rows, slots, wk = (k[n] for n in ("cst", "ident", "xres", "st6", "rows", "slots", "wk"))
    ones = cst[:, C_ONE:C_ONE + P]
    TPP = 2 * TPB
    with ExitStack() as ctx:
        ctx_sb = k["ctx_sb"]
        wqv = sb(ctx, "a_wqv", [P, 4, KD, D])
        wsim = sb(ctx, "a_wsim", [P, 3, KD])
        bsim = sb(ctx, "a_bsim", [1, 1])
        bqv = sb(ctx, "a_bqv", [P, D])
        st4 = sb(ctx, "a_st4", [P, TPP, 6])
        ln = sb(ctx, "a_ln", [P, 9, TPP])

        def two(name, shape):
            return [sb(ctx, f"a_{name}{u}", shape) for u in range(2)]

        def four(name, shape):
            return [[sb(ctx, f"a_{name}{g}{u}", shape) for u in range(2)] for g in range(2)]
        cS, cT, qmod, brow = two("cS", [C, D]), two("cT", [P, KD, C]), two("qmod", [P, KD, C]), two("brow", [1, C])
        mx, nmx, ssum = two("mx", [P, TPB]), two("nmx", [P, TPB]), two("ssum", [P, 2 * TPB])
        att, attT = two("att", [P, TPB, C]), two("attT", [C, S])
        gmx, erow, esum, battn, tmp = two("gmx", [1, 1]), two("erow", [1, S]), two("esum", [1, 2]), two("battn", [P, TPB]), two("tmp", [P, TPB, D])
        xn, hcT, hqT, prT, wp = (four(n, s) for n, s in (("xn", [P, TPB, D]), ("hcT", [P, KD, S]), ("hqT", [P, KD, S]),
                                                         ("prT", [P, KD, S]), ("wp", [P, KD, D])))
        A, Ck, Dk, O = ([pb(ctx, f"a_{n}{u}", [P, 512]) for u in range(2)] for n in "ACDO")
        CT = 2 * P

        w_in = [sem(f"a_w_in{i}") for i in range(2)]
        gat = [sem(f"a_gat{u}") for u in range(4)]
        names = ("c0 cb st ln var root xn cS tp ctp hcT qmod cTs r brow sim mx nmx exp rs att attT attE rowm gmx erow es bcol bcs hcb "
                 "wp hq hqE pr out tmp add fst nmr").split()
        q = {n: sem("a_" + n) for n in names}
        block = ctx.enter_context(nc.Block())
        NH = B // 4

        @block.sync
        def _(sp):
            sp.dma_start(wsim[:, :, :], a["wsim"]).then_inc(w_in[0], 16)
            sp.dma_start(bsim[:, :], a["b_sim"]).then_inc(w_in[0], 16)
            sp.dma_start(wqv[:, :, :, :], a["wqv"]).then_inc(w_in[1], 16)
            sp.dma_start(bqv[:, :], a["L1_xattn_b_qv"].partition_broadcast(P)).then_inc(w_in[1], 16)
            for e in range(E1):
                sp.wait_ge(q["cb"], min(e + 1, B // 2) * TPP)
                sp.dma_start(k["l1_w1"][:, :, e, :], a["l1_w1"][:, :, e, :]).then_inc(k["s_w1"], 16)

        @block.gpsimd
        def _(pool):
            for t in range(NT):
                if t >= 4:
                    pool.wait_ge(q["cb"], t - 3)
                for i in range(K0):
                    pool.indirect_dma_start(out=rows[i][:, t % 4, :], out_offset=None, in_=k["ys0"],
                                            in_offset=bass.IndirectOffsetOnAxis(ap=slots[i][:, t:t + 1], axis=0)
                                            ).then_inc(gat[t % 4], 16)

        @block.scalar
        def _(act):
            def root(p):
                act.wait_ge(q["var"], p + 1)
                act.activation(ln[:, 5, :], ln[:, 4, :], ACT.Sqrt).then_inc(q["root"], 1)

            def context(p):
                for u in range(2):
                    act.copy(cS[u][:, :], flat2(ctx_sb[:, bass.ds(p * 2 + u, 1), :])).then_inc(q["cS"], 1)

            def half(p, g, settled, more=True):
                context(p)
                for u in range(2):
                    b = p * 2 + u
                    act.wait_ge(q["ctp"], b + 1)
                    act.copy(cT[u][:, :, :], Dk[u][:, CT:CT + 2 * C].rearrange("p (k c) -> p k c", k=KD)).then_inc(q["cTs"], 1)
                    if settled:
                        act.wait_ge(q["out"], b - 3)
                    act.wait_ge(q["tp"], b + 1)
                    act.copy(hcT[g][u][:, :, :], A[u][:, :].rearrange("p (k n) -> p k n", k=KD)).then_inc(q["hcT"], 1)
                for u in range(2):
                    act.wait_ge(q["nmx"], p * 2 + u + 1)
                    for i in range(TPB):
                        act.activation(att[u][:, i, :], Ck[u][:, i * P:i * P + C], ACT.Exp, bias=nmx[u][:, i:i + 1],
                                       accum_out=ssum[u][:, i:i + 1]).then_inc(q["exp"], 1)
                if more:
                    root(p + 1)
                for u in range(2):
                    act.wait_ge(q["gmx"], p * 2 + u + 1)
                    act.activation(erow[u][:, :], A[u][0:1, 0:S], ACT.Exp, bias=gmx[u][:, :],
                                   accum_out=esum[u][:, 0:1]).then_inc(q["erow"], 1)
                for u in range(2):
                    act.wait_ge(q["attT"], p * 2 + u + 1)
                    act.copy(attT[u][:, :], Dk[u][0:C, 0:S]).then_inc(q["attE"], 1)
                for u in range(2):
                    act.wait_ge(q["hq"], p * 2 + u + 1)
                    act.copy(hqT[g][u][:, :, :], A[u][:, :].rearrange("p (k n) -> p k n", k=KD)).then_inc(q["hqE"], 1)

            root(0)
            half(0, 0, False)
            half(1, 1, False)
            with act.Fori(1, NH - 1) as h:
                half(h * 2, 0, True)
                half(h * 2 + 1, 1, True)
            half(B // 2 - 2, 0, True)
            half(B // 2 - 1, 1, True, more=False)

        @block.tensor
        def _(pe):
            def last(p, g, u, i, used=True):
                b = p * 2 + u
                if i == 0:
                    pe.wait_ge(q["hqE"], b + 1)
                    pe.wait_ge(q["pr"], b + 1)
                    pe.wait_ge(q["wp"], b + 1)
                    if used:
                        pe.wait_ge(q["tmp"], b - 1)
                n = 0
                for part, rhs in ((hqT, lambda kb: wqv[:, 1, kb, :]), (prT, lambda kb: wqv[:, 2, kb, :]), (hcT, lambda kb: wp[g][u][:, kb, :])):
                    for kb in range(KD):
                        ins = pe.matmul(O[u][:, i * D:(i + 1) * D], part[g][u][:, kb, i * P:(i + 1) * P], rhs(kb), start=(n == 0), stop=(n == 5))
                        n += 1
                if i == TPB - 1:
                    ins.then_inc(q["out"], 1)

            def half(p, g, before=None, used=True):
                def piece(u, i):
                    if before is not None:
                        last(before, 1 - g, u, i, used)
                for u in range(2):
                    b = p * 2 + u
                    pe.wait_ge(q["cS"], b + 1)
                    for kb in range(KD):
                        ins = pe.transpose(Dk[u][:, CT + kb * C:CT + (kb + 1) * C], cS[u][:, kb * P:(kb + 1) * P], ident[0:C, 0:C])
                    ins.then_inc(q["ctp"], 1)
                for u in range(2):
                    b = p * 2 + u
                    if before is not None:
                        pe.wait_ge(q["hqE"], b - 1)
                    pe.wait_ge(q["xn"], b + 1)
                    for i in range(TPB):
                        for kb in range(KD):
                            ins = pe.transpose(A[u][:, kb * S + i * P:kb * S + (i + 1) * P], xn[g][u][:, i, kb * P:(kb + 1) * P], ident)
                    ins.then_inc(q["tp"], 1)
                for u in range(2):
                    b = p * 2 + u
                    pe.wait_ge(q["cTs"], b + 1)
                    for kb in range(KD):
                        ins = pe.matmul(Dk[u][0:1, 0:C], wsim[:, 1, kb:kb + 1], cT[u][:, kb, :], start=(kb == 0), stop=(kb == KD - 1))
                    ins.then_inc(q["r"], 1)
                piece(0, 0)
                for u in range(2):
                    b = p * 2 + u
                    pe.wait_ge(q["hcT"], b + 1)
                    pe.wait_ge(q["brow"], b + 1)
                    for i in range(TPB):
                        for kb in range(KD):
                            pe.matmul(Ck[u][:, i * P:i * P + C], hcT[g][u][:, kb, i * P:(i + 1) * P], qmod[u][:, kb, :], start=(kb == 0), stop=False)
                        ins = pe.matmul(Ck[u][:, i * P:i * P + C], ones[0:1, :], brow[u][:, :], start=False, stop=True)
                    ins.then_inc(q["sim"], 1)
                piece(0, 1)
                for u in range(2):
                    pe.wait_ge(q["mx"], p * 2 + u + 1)
                    for i in range(TPB):
                        ins = pe.transpose(A[u][0:1, i * P:(i + 1) * P], mx[u][:, i:i + 1], ident)
                    ins.then_inc(q["rowm"], 1)
                piece(1, 0)
                for u in range(2):
                    pe.wait_ge(q["att"], p * 2 + u + 1)
                    for i in range(TPB):
                        ins = pe.transpose(Dk[u][0:C, i * P:(i + 1) * P], att[u][:, i, :], ident)
                    ins.then_inc(q["attT"], 1)
                for u in range(2):
                    pe.wait_ge(q["es"], p * 2 + u + 1)
                    for i in range(TPB):
                        ins = pe.matmul(Ck[u][:, i:i + 1], erow[u][:, i * P:(i + 1) * P], esum[u][:, 1:2], start=True, stop=True)
                    ins.then_inc(q["bcol"], 1)
                for u in range(2):
                    pe.wait_ge(q["attE"], p * 2 + u + 1)
                    for kb in range(KD):
                        ins = pe.matmul(A[u][:, kb * S:(kb + 1) * S], cS[u][:, kb * P:(kb + 1) * P], attT[u][:, :], start=True, stop=True)
                    ins.then_inc(q["hq"], 1)
                for u in range(2):
                    pe.wait_ge(q["bcs"], p * 2 + u + 1)
                    for kb in range(KD):
                        for i in range(TPB):
                            ins = pe.matmul(Ck[u][:, 8 + kb:9 + kb], xn[g][u][:, i, kb * P:(kb + 1) * P], battn[u][:, i:i + 1],
                                            start=(i == 0), stop=(i == TPB - 1))
                    ins.then_inc(q["hcb"], 1)
                piece(1, 1)

            pe.wait_ge(w_in[0], 32)
            half(0, 0)
            pe.wait_ge(w_in[1], 32)
            half(1, 1, 0, used=False)
            with pe.Fori(1, NH - 1) as h:
                half(h * 2, 0, h * 2 - 1)
                half(h * 2 + 1, 1, h * 2)
            half(B // 2 - 2, 0, B // 2 - 3)
            half(B // 2 - 1, 1, B // 2 - 2)
            for u in range(2):
                for i in range(TPB):
                    last(B // 2 - 1, 1, u, i)

        @block.vector
        def _(dve):
            CHAIN = 10

            def combine(p):
                for u in range(TPP):
                    t = p * TPP + u
                    xt = flat2(xres[:, bass.ds(t, 1), :])
                    dve.wait_ge(gat[u], 16 * K0 * (p + 1))
                    dve.scalar_tensor_tensor(xt, rows[0][:, u, :], wk[:, 0, bass.ds(t, 1)], xt, ALU.mult, ALU.add).then_inc(q["c0"], 1)
                for u in range(TPP):
                    t = p * TPP + u
                    xt = flat2(xres[:, bass.ds(t, 1), :])
                    dve.wait_ge(q["c0"], t + 1)
                    dve.scalar_tensor_tensor(xt, rows[1][:, u, :], wk[:, 1, bass.ds(t, 1)], xt, ALU.mult, ALU.add).then_inc(q["cb"], 1)

            def pair_stats(p):
                for u in range(TPP):
                    dve.bn_stats(st4[:, u, :], flat2(xres[:, bass.ds(p * TPP + u, 1), :])).then_inc(q["st"], 1)

            def variances(p):
                chain = Chain(dve, q["ln"], p * CHAIN)
                even, odd = st4[:, :, 0:3], st4[:, :, 3:6]
                dve.wait_ge(q["st"], p * TPP + TPP)
                chain(dve.tensor_tensor(ln[:, 0, :], even[:, :, 1], odd[:, :, 1], ALU.add))
                chain(dve.tensor_tensor(ln[:, 1, :], even[:, :, 1], odd[:, :, 1], ALU.subtract))
                chain(dve.tensor_tensor(ln[:, 2, :], even[:, :, 2], odd[:, :, 2], ALU.add))
                chain(dve.scalar_tensor_tensor(ln[:, 1, :], ln[:, 1, :], 0.25, ln[:, 1, :], ALU.mult, ALU.mult))
                chain(dve.tensor_scalar(ln[:, 2, :], ln[:, 2, :], 1.0 / D, EPS, ALU.mult, ALU.add))
                dve.tensor_tensor(ln[:, 4, :], ln[:, 1, :], ln[:, 2, :], ALU.add).then_inc(q["var"], 1)

            def normalise(p, g):
                chain = Chain(dve, q["ln"], p * CHAIN + 5)
                dve.wait_ge(q["root"], p + 1)
                chain(dve.reciprocal(ln[:, 6, :], ln[:, 5, :]))
                chain(dve.tensor_tensor(ln[:, 6, :], ln[:, 4, :], ln[:, 6, :], ALU.mult))
                chain(dve.scalar_tensor_tensor(ln[:, 6, :], ln[:, 6, :], 1.0, ln[:, 5, :], ALU.mult, ALU.add))
                chain(dve.tensor_scalar(ln[:, 6, :], ln[:, 6, :], 0.5, None, ALU.mult))
                chain(dve.reciprocal(ln[:, 7, :], ln[:, 6, :]))
                dve.scalar_tensor_tensor(ln[:, 8, :], ln[:, 0, :], -0.5, ln[:, 7, :], ALU.mult, ALU.mult).then_inc(q["nmr"], 1)
                dve.wait_ge(q["nmr"], p + 1)
                for u in range(2):
                    for i in range(TPB):
                        w = u * TPB + i
                        ins = dve.tensor_scalar(xn[g][u][:, i, :], flat2(xres[:, bass.ds(p * TPP + w, 1), :]), ln[:, 7, w:w + 1], ln[:, 8, w:w + 1],
                                                ALU.mult, ALU.add)
                    ins.then_inc(q["xn"], 1)

            def finish(p, u):
                b = p * 2 + u
                dve.wait_ge(q["out"], b + 1)
                dve.tensor_tensor(tmp[u][:, :, :], O[u][:, :].rearrange("p (i d) -> p i d", i=TPB),
                                  bqv[:, :].unsqueeze(1).to_broadcast([P, TPB, D]), ALU.add).then_inc(q["tmp"], 1)
                dve.wait_ge(q["tmp"], b + 1)
                xb = xres[:, bass.ds(b * TPB, TPB), :]
                dve.tensor_tensor(xb, tmp[u][:, :, :], xb, ALU.add).then_inc(q["add"], 1)

            def final_stats(p, u):
                b = p * 2 + u
                for i in range(TPB):
                    dve.bn_stats(flat2(st6[:, bass.ds(b * TPB + i, 1), :]), flat2(xres[:, bass.ds(b * TPB + i, 1), :])).then_inc(q["fst"], 1)

            def half(p, g, before=None, settled=None, more=True):
                for u in range(2):
                    b = p * 2 + u
                    dve.wait_ge(q["cTs"], b + 1)
                    for kb in range(KD):
                        dve.tensor_scalar(qmod[u][:, kb, :], cT[u][:, kb, :], wsim[:, 2, kb:kb + 1], wsim[:, 0, kb:kb + 1],
                                          ALU.mult, ALU.add).then_inc(q["qmod"], 1)
                    dve.wait_ge(q["r"], b + 1)
                    dve.tensor_scalar(brow[u][:, :], Dk[u][0:1, 0:C], bsim[:, :], None, ALU.add).then_inc(q["brow"], 1)
                if settled is not None:
                    finish(settled, 1)
                if more:
                    combine(p + 1)
                for u in range(2):
                    b = p * 2 + u
                    if settled is not None and u == 0:
                        dve.wait_ge(q["add"], settled * 2 + 2)
                    if more and u == 1:
                        dve.wait_ge(q["cb"], (p + 2) * TPP)
                    dve.wait_ge(q["sim"], b + 1)
                    dve.tensor_reduce(mx[u][:, :], Ck[u][:, 0:2 * P].rearrange("p (i c) -> p i c", i=TPB)[:, :, 0:C], AX.X, ALU.max).then_inc(q["mx"], 1)
                    dve.wait_ge(q["mx"], b + 1)
                    dve.tensor_scalar(nmx[u][:, :], mx[u][:, :], -1.0, None, ALU.mult).then_inc(q["nmx"], 1)
                    if settled is not None and u == 0:
                        final_stats(settled, 1)
                    if more and u == 1:
                        pair_stats(p + 1)
                if more:
                    variances(p + 1)
                for u in range(2):
                    dve.wait_ge(q["rowm"], p * 2 + u + 1)
                    dve.tensor_reduce(gmx[u][:, :], A[u][0:1, 0:S], AX.X, ALU.max, negate=True).then_inc(q["gmx"], 1)
                for u in range(2):
                    b = p * 2 + u
                    dve.wait_ge(q["exp"], b * TPB + TPB)
                    dve.reciprocal(ssum[u][:, TPB:2 * TPB], ssum[u][:, 0:TPB]).then_inc(q["rs"], 1)
                    dve.wait_ge(q["rs"], b + 1)
                    for i in range(TPB):
                        ins = dve.tensor_scalar(att[u][:, i, :], att[u][:, i, :], ssum[u][:, TPB + i:TPB + i + 1], None, ALU.mult)
                    ins.then_inc(q["att"], 1)
                for u in range(2):
                    dve.wait_ge(q["erow"], p * 2 + u + 1)
                    dve.reciprocal(esum[u][:, 1:2], esum[u][:, 0:1]).then_inc(q["es"], 1)
                if before is not None:
                    finish(before, 0)
                for u in range(2):
                    dve.wait_ge(q["bcol"], p * 2 + u + 1)
                    dve.tensor_copy(battn[u][:, :], Ck[u][:, 0:TPB]).then_inc(q["bcs"], 1)
                if more:
                    normalise(p + 1, 1 - g)
                if before is not None:
                    dve.wait_ge(q["add"], before * 2 + 1)
                for u in range(2):
                    b = p * 2 + u
                    dve.wait_ge(q["hqE"], b + 1)
                    dve.tensor_tensor(prT[g][u][:, :, :], hcT[g][u][:, :, :], hqT[g][u][:, :, :], ALU.mult).then_inc(q["pr"], 1)
                    dve.wait_ge(q["hcb"], b + 1)
                    for kb in range(KD):
                        ins = dve.scalar_tensor_tensor(wp[g][u][:, kb, :], wqv[:, 3, kb, :], Ck[u][:, 8 + kb:9 + kb], wqv[:, 0, kb, :], ALU.mult, ALU.add)
                    ins.then_inc(q["wp"], 1)
                if before is not None:
                    final_stats(before, 0)

            combine(0)
            dve.wait_ge(q["cb"], TPP)
            pair_stats(0)
            variances(0)
            normalise(0, 0)
            dve.wait_ge(w_in[0], 32)
            dve.wait_ge(w_in[1], 32)
            half(0, 0)
            half(1, 1, 0)
            with dve.Fori(1, NH - 1) as h:
                half(h * 2, 0, h * 2 - 1, h * 2 - 2)
                half(h * 2 + 1, 1, h * 2, h * 2 - 1)
            half(B // 2 - 2, 0, B // 2 - 3, B // 2 - 4)
            half(B // 2 - 1, 1, B // 2 - 2, B // 2 - 3, more=False)
            for p, u in ((B // 2 - 2, 1), (B // 2 - 1, 0), (B // 2 - 1, 1)):
                finish(p, u)
                dve.wait_ge(q["add"], p * 2 + u + 1)
                final_stats(p, u)


def phase_moe1(nc, a, out, k):
    sb, pb, sem = k["sb"], k["pb"], k["sem"]
    cst, ident, xres, rstd, nmr, lnt, st6, mv, w1 = (k[n] for n in ("cst", "ident", "xres", "rstd", "nmr", "lnt", "st6", "mv", "l1_w1"))
    xs = k["xs1"]
    NE = E1
    with ExitStack() as ctx:
        w2 = sb(ctx, "f_w2", [P, FB, NE, D])
        b1 = sb(ctx, "f_b1", [P, NE, FB])
        b2 = sb(ctx, "f_b2", [P, NE, D])
        lgb = sb(ctx, "f_lgb", [P, NE, 2 * KD])
        cw = sb(ctx, "f_cw", [P, KD, NE])
        slot_row = [k["rows_mem"][v // 2][:, :, :].rearrange("p t d -> p (t d)")[:, (v % 2) * SLOT1:(v % 2 + 1) * SLOT1] for v in range(4)]
        side = sb(ctx, "f_side", [P, NT, SLOT1 - GATE])
        number = sb(ctx, "f_number", [P, NT])
        spare = sb(ctx, "f_spare", [P, NTL1])
        where = sb(ctx, "f_where", [P, 4, 1])
        tick = sb(ctx, "f_tick", [1, 2])
        row_out = sb(ctx, "f_row_out", [P, 4], U32)
        xT = [sb(ctx, f"f_xT{u}", [P, KD, P]) for u in range(U1)]
        arena = k["ctx_all"][:, :, :].rearrange("p b d -> p (b d)")
        w1_now = arena[:, 0:KD * F1].rearrange("p (k n) -> p k n", k=KD)
        hT = [arena[:, KD * F1 + F1 * u:KD * F1 + F1 * (u + 1)].rearrange("p (f n) -> p f n", f=FB) for u in range(U1)]
        big = [arena[:, 256 * i:256 * i + 256].rearrange("p (t e) -> p t e", e=NE) for i in range(5)]
        aff, oh, t3 = big[0], big[1], big[2]
        gate_xT = [arena[:, 2048 + 1024 * u:3072 + 1024 * u].rearrange("p (c k n) -> p c k n", c=2, k=KD) for u in range(2)]
        score_T = [arena[0:NE, 1024 + 512 * u:1536 + 512 * u] for u in range(2)]
        em = sb(ctx, "f_em", [P, NE])
        sm = sb(ctx, "f_sm", [P, 8, NT])
        top, t1, alpha = sm[:, 0, :], sm[:, 1, :], sm[:, 2, :]
        rs2, nm2 = sb(ctx, "f_rs2", [P, NT]), sb(ctx, "f_nm2", [P, NT])
        slot = sb(ctx, "f_slot", [P, NT], U32)
        etile = sb(ctx, "f_etile", [1, NTL1], I32)
        r = {"totE": big[3].rearrange("p t e -> p (t e)").rearrange("p (e t) -> p e t", e=NE), "t3": t3,
             "cum": big[4].rearrange("p t e -> p (t e)").rearrange("p (e t) -> p e t", e=NE), "sst": sb(ctx, "f_sst", [P, NE + 1])[:, :],
             "ti": sb(ctx, "f_ti", [P, NE], I32)[:, :], "red": sm[:, 3, :],
             "cmp": sb(ctx, "f_cmp", [1, NTL1, NE])[:, :, :], "tsum": sb(ctx, "f_tsum", [1, NTL1])[:, :]}
        for i, n in enumerate(("cnt", "tl", "tend", "delta")):
            r[n] = sm[:, 4 + i, 0:NE]
        bank = [pb(ctx, f"f_bank{u}", [P, 512]) for u in range(8)]

        w_in = [sem(f"f_w_in{i}") for i in range(2)]
        names = ("var root dve xn tp xT gs gate var2 root2 exp1 exp2 mask rank slot row xt xe w1a w1b hh ht1 ht2 yp yb yo where iota tick").split()
        q = {n: sem("f_" + n) for n in names}
        sct = [sem(f"f_sct{u}") for u in range(4)]
        x_in = [sem(f"f_x_in{v}") for v in range(4)]
        s_sT, s_back = sem("f_sT"), sem("f_back")
        s_out = [sem(f"f_out{v}") for v in range(4)]
        block = ctx.enter_context(nc.Block())
        ROUNDS = NTL1 // 4

        def before(h, v):
            return (h, v - 1) if v else (h - 1, 3)

        def after(h, v):
            return (h, v + 1) if v < 3 else (h + 1, 0)

        PIECES = 4
        FPP = FB // PIECES
        ROWS, RES = 2, 3

        def expert(eng, n):
            return eng.value_load(etile[0:1, bass.ds(n, 1)], min_val=0, max_val=NE - 1)

        def piece(e, c):
            cols = slice(c * FPP * P, (c + 1) * FPP * P)
            return w1_now[:, :, cols], flat2b(w1[:, :, bass.ds(e, 1), cols])

        @block.sync
        def _(sp):
            sp.dma_start(cw[:, :, :], a["cw"]).then_inc(w_in[0], 16)
            for dst, name in ((b1[:, :, :], "b1"), (lgb[:, :, :], "lgb")):
                sp.dma_start(dst, a[name]).then_inc(w_in[1], 16)
            sp.dma_start(b2[:, :, :].rearrange("p e n -> p (e n)"), a["L1_ffn_b2"].rearrange("e n -> (e n)").partition_broadcast(P)).then_inc(w_in[1], 16)
            for c in range(4):
                sp.dma_start(w2[:, 2 * c:2 * c + 2, :, :], a["l1_w2"][:, 2 * c:2 * c + 2, :, :]).then_inc(w_in[1], 16)
            for u in range(4):
                sp.wait_ge(sct[u], 16 * NT // 4)

            for v in range(4):
                sp.dma_start(slot_row[v], xs[v * P:(v + 1) * P, :]).then_inc(x_in[v], 16)
            with sp.Fori(1, ROUNDS) as h:
                for v in range(4):
                    sp.wait_ge(s_out[v], h * 16)
                    sp.dma_start(slot_row[v], xs[bass.ds((h * 4 + v) * P, P), :]).then_inc(x_in[v], 16)

        @block.gpsimd
        def _(pool):
            pool.memset(tick[:, :], 0.0).then_inc(q["iota"], 1)
            pool.iota(number[:, :], pattern=[[P, NT]], base=1, channel_multiplier=1,
                      allow_small_or_imprecise_dtypes=True).then_inc(q["iota"], 1)
            pool.iota(spare[:, :], pattern=[[P, NTL1]], base=TOK + 1, channel_multiplier=1,
                      allow_small_or_imprecise_dtypes=True).then_inc(q["iota"], 1)
            pool.wait_ge(q["slot"], 1)
            for t in range(NT):
                pool.wait_ge(q["row"], t + 1)
                pool.indirect_dma_start(out=xs, out_offset=bass.IndirectOffsetOnAxis(ap=slot[:, t:t + 1], axis=0),
                                        in_=slot_row[t % 4], in_offset=None).then_inc(sct[t % 4], 16)
            pool.wait_ge(q["slot"], 2)
            pool.wait_ge(k["s_w1"], 16 * E1)

            def first_weights(n, fresh=False):
                e = expert(pool, n)
                for c in range(PIECES // 2):
                    if not fresh:
                        pool.wait_ge(q["hh"], (n - 1) * PIECES + c + 1)
                    pool.tensor_copy(*piece(e, c)).then_inc(q["w1a"], 1)

            def send(h, v, fresh=False):
                n = h * 4 + v
                pool.wait_ge(q["yo"], n + 1)
                if not fresh:
                    pool.wait_ge(q["tick"], n)
                pool.tensor_tensor(tick[:, 1:2], tick[:, 0:1], tick[:, 0:1], ALU.add).then_inc(q["tick"], 1)
                pool.indirect_dma_start(out=out, out_offset=bass.IndirectOffsetOnAxis(ap=row_out[:, v:v + 1], axis=0),
                                        in_=slot_row[v][:, BASE:BASE + D], in_offset=None).then_inc(s_out[v], 16)

            first_weights(0, fresh=True)
            first_weights(1)
            for v in range(2):
                first_weights(v + 2)
                send(0, v, fresh=(v == 0))
            with pool.Fori(1, ROUNDS) as h:
                for v in range(4):
                    first_weights(h * 4 + v)
                    send(*before(*before(h, v)))
            send(ROUNDS - 1, 2)
            send(ROUNDS - 1, 3)
            for v in range(4):
                pool.wait_ge(s_out[v], 16 * ROUNDS)

        @block.scalar
        def _(act):
            act.wait_ge(q["var"], 1)
            act.activation(lnt[:, 1, :], lnt[:, 0, :], ACT.Sqrt).then_inc(q["root"], 1)
            act.wait_ge(q["var2"], 1)
            act.activation(lnt[:, 1, :], lnt[:, 0, :], ACT.Sqrt).then_inc(q["root2"], 1)
            def scores_out(g, u):
                act.wait_ge(q["gs"], g + 1)
                act.copy(score_T[u], bank[6 + u][0:NE, :]).then_inc(s_sT, 1)

            with act.Fori(0, NT // 8) as h:
                scores_out(h * 2, 0)
                scores_out(h * 2 + 1, 1)
            act.wait_ge(q["exp1"], 1)
            act.activation(alpha, top, ACT.Exp, scale=-1.0).then_inc(q["exp2"], 1)
            act.wait_ge(w_in[1], 16 * 7)
            act.wait_ge(q["slot"], 2)
            act.wait_ge(k["s_w1"], 16 * E1)

            def turned_in(h, v, e):
                n, u = h * 4 + v, v % 2
                act.wait_ge(q["xt"], n + 1)
                for kb in range(KD):
                    act.activation(xT[u][:, kb, :], bank[4 * u + ROWS][:, kb * P:(kb + 1) * P], ACT.Identity,
                                   scale=flat2(lgb[:, bass.ds(e, 1), kb:kb + 1]), bias=flat2(lgb[:, bass.ds(e, 1), KD + kb:KD + kb + 1])).then_inc(q["xe"], 1)

            def second_weights(e):
                for c in range(PIECES // 2, PIECES):
                    act.copy(*piece(e, c)).then_inc(q["w1b"], 1)

            def rectified(v, e):
                u = v % 2
                for f in range(FB // 2, FB):
                    act.activation(hT[u][:, f, :], bank[4 * u + 1][:, (f - 4) * P:(f - 3) * P], ACT.Relu,
                                   bias=flat2(b1[:, bass.ds(e, 1), f:f + 1])).then_inc(q["ht2"], 1)

            def tile(h, v, e, last=False):
                if not last:
                    h_next, v_next = after(h, v)
                    e_next = expert(act, h_next * 4 + v_next)
                    turned_in(h_next, v_next, e_next)
                act.wait_ge(q["hh"], (h * 4 + v + 1) * PIECES)
                if not last:
                    second_weights(e_next)
                rectified(v, e)
                return None if last else e_next

            e = expert(act, 0)
            second_weights(e)
            turned_in(0, 0, e)
            for v in range(4):
                e = tile(0, v, e)
            with act.Fori(1, ROUNDS - 1) as h:
                e = expert(act, h * 4)
                for v in range(4):
                    e = tile(h, v, e)
            e = expert(act, NTL1 - 4)
            for v in range(4):
                e = tile(ROUNDS - 1, v, e, last=(v == 3))

        @block.tensor
        def _(pe):
            pe.wait_ge(w_in[0], 16)
            def turn(g, u, fresh=False, turned_later=None, fresh_scores=False):
                for c in range(2):
                    if c == 1 and turned_later is not None:
                        scores_ready(turned_later, fresh_scores)
                    if not fresh:
                        pe.wait_ge(q["xT"], g * 2 + c - 3)
                    pe.wait_ge(q["xn"], g * 2 + c + 1)
                    for i in range(2):
                        for kb in range(KD):
                            ins = pe.transpose(bank[2 * u + c][:, kb * 256 + i * P:kb * 256 + (i + 1) * P],
                                               k["rows"][u][:, 2 * c + i, kb * P:(kb + 1) * P], ident)
                    ins.then_inc(q["tp"], 1)

            def scores(g, u):
                pe.wait_ge(q["xT"], g * 2 + 2)
                for kb in range(KD):
                    ins = pe.matmul(bank[6 + u][0:NE, :].rearrange("p (c n) -> p c n", c=2), cw[:, kb, :], gate_xT[u][:, :, kb, :],
                                    start=(kb == 0), stop=(kb == KD - 1))
                ins.then_inc(q["gs"], 1)

            def scores_ready(g, fresh=False):
                if not fresh:
                    pe.wait_ge(q["gate"], g - 1)
                pe.wait_ge(s_sT, g + 1)

            def turn_scores(g, u):
                for i in range(4):
                    ins = pe.transpose(bank[4 + u][:, i * NE:(i + 1) * NE], score_T[u][:, i * P:(i + 1) * P], ident[0:NE, 0:NE])
                ins.then_inc(s_back, 1)

            turn(0, 0, fresh=True)
            turn(1, 1, fresh=True)
            scores(0, 0)
            turn(2, 0, turned_later=0, fresh_scores=True)
            turn_scores(0, 0)
            scores(1, 1)
            turn(3, 1, turned_later=1, fresh_scores=True)
            turn_scores(1, 1)
            scores(2, 0)
            with pe.Fori(2, NT // 8) as h:
                turn(h * 2, 0, turned_later=h * 2 - 2)
                turn_scores(h * 2 - 2, 0)
                scores(h * 2 - 1, 1)
                turn(h * 2 + 1, 1, turned_later=h * 2 - 1)
                turn_scores(h * 2 - 1, 1)
                scores(h * 2, 0)
            scores_ready(NT // 4 - 2)
            turn_scores(NT // 4 - 2, 0)
            scores(NT // 4 - 1, 1)
            scores_ready(NT // 4 - 1)
            turn_scores(NT // 4 - 1, 1)
            pe.wait_ge(q["mask"], 1)
            pe.matmul(bank[6][:, 0:NT * NE], cst[:, C_TRI:C_TRI + P], oh.rearrange("p t e -> p (t e)"), start=True, stop=True)
            pe.matmul(bank[7][:, 0:NT * NE], cst[:, C_ONE:C_ONE + P], oh.rearrange("p t e -> p (t e)"), start=True, stop=True).then_inc(q["rank"], 1)
            pe.wait_ge(q["slot"], 2)
            pe.wait_ge(k["s_w1"], 16 * E1)
            pe.wait_ge(w_in[1], 16 * 7)

            def turn_in(h, v):
                u = v % 2
                pe.wait_ge(x_in[v], h * 16 + 16)
                for kb in range(KD):
                    ins = pe.transpose(bank[4 * u + ROWS][:, kb * P:(kb + 1) * P], slot_row[v][:, IN + kb * P:IN + (kb + 1) * P], ident)
                ins.then_inc(q["xt"], 1)

            def inner(h, v):
                n, u = h * 4 + v, v % 2
                for f in range(FB):
                    if f % FPP == 0:
                        pe.wait_ge(q["w1a" if f < FB // 2 else "w1b"], n * (PIECES // 2) + f % (FB // 2) // FPP + 1)
                    for kb in range(KD):
                        if f == 0:
                            pe.wait_ge(q["xe"], n * KD + kb + 1)
                        ins = pe.matmul(bank[4 * u + f // 4][:, (f % 4) * P:(f % 4 + 1) * P], w1_now[:, kb, f * P:(f + 1) * P], xT[u][:, kb, :],
                                        start=(kb == 0), stop=(kb == KD - 1))
                    if f % FPP == FPP - 1:
                        ins.then_inc(q["hh"], 1)

            def out_rows(h, v, fresh=False):
                n, u = h * 4 + v, v % 2
                e = expert(pe, n)
                if not fresh:
                    pe.wait_ge(q["yb"], n - 1)
                pe.wait_ge(q["ht1"], (n + 1) * (FB // 2))
                pe.wait_ge(q["ht2"], (n + 1) * (FB // 2))
                for f in range(FB):
                    ins = pe.matmul(bank[4 * u + RES][:, 0:D], hT[u][:, f, :], flat2(flat2b(w2[:, f:f + 1, bass.ds(e, 1), :])), start=(f == 0), stop=(f == FB - 1))
                ins.then_inc(q["yp"], 1)

            turn_in(0, 0)
            inner(0, 0)
            turn_in(0, 1)
            for v in range(1, 4):
                inner(0, v)
                turn_in(*after(0, v))
                out_rows(0, v - 1, fresh=(v <= 2))
            with pe.Fori(1, ROUNDS - 1) as h:
                for v in range(4):
                    inner(h, v)
                    turn_in(*after(h, v))
                    out_rows(*before(h, v))
            for v in range(4):
                inner(ROUNDS - 1, v)
                if v < 3:
                    turn_in(ROUNDS - 1, v + 1)
                out_rows(*before(ROUNDS - 1, v))
            out_rows(ROUNDS - 1, 3)

        @block.vector
        def _(dve):
            chain = Chain(dve, q["dve"])
            k["moments"](chain, dve)
            k["rstd_steps"](dve, chain, q["var"], q["root"])
            dve.wait_ge(w_in[0], 16)
            def normal(g, u):
                for i in range(4):
                    ins = k["norm_tile"](dve, k["rows"][u][:, i, :], g * 4 + i)
                    if i % 2 == 1:
                        ins.then_inc(q["xn"], 1)

            def turned(g, u):
                for c in range(2):
                    dve.wait_ge(q["tp"], g * 2 + c + 1)
                    dve.tensor_copy(gate_xT[u][:, c, :, :], bank[2 * u + c][:, :].rearrange("p (k n) -> p k n", k=KD)).then_inc(q["xT"], 1)

            def scores(g, u):
                dve.wait_ge(s_back, g + 1)
                dve.tensor_copy(aff[:, bass.ds(g * 4, 4), :], bank[4 + u][:, 0:4 * NE].rearrange("p (t e) -> p t e", e=NE)).then_inc(q["gate"], 1)

            normal(0, 0)
            normal(1, 1)
            ve, t0, tt, mean2 = lnt[:, 0, :], lnt[:, 1, :], lnt[:, 2, :], sm[:, 3, :]
            chain(dve.tensor_tensor(ve, mv[:, :, 1], rstd[:, :], ALU.mult))
            chain(dve.tensor_tensor(ve, ve, rstd[:, :], ALU.mult))
            dve.tensor_scalar(ve, ve, EPS, None, ALU.add).then_inc(q["var2"], 1)
            chain(dve.tensor_tensor(mean2, mv[:, :, 0], rstd[:, :], ALU.mult))
            chain(dve.tensor_tensor(mean2, mean2, nmr[:, :], ALU.add))
            dve.wait_ge(q["root2"], 1)
            chain(dve.reciprocal(tt, t0))
            chain(dve.tensor_tensor(tt, ve, tt, ALU.mult))
            chain(dve.tensor_tensor(tt, tt, t0, ALU.add))
            chain(dve.tensor_scalar(tt, tt, 0.5, None, ALU.mult))
            chain(dve.reciprocal(t0, tt))
            chain(dve.tensor_tensor(rs2[:, :], rstd[:, :], t0, ALU.mult))
            chain(dve.tensor_tensor(tt, nmr[:, :], mean2, ALU.subtract))
            chain(dve.tensor_tensor(nm2[:, :], tt, t0, ALU.mult))
            turned(0, 0)
            normal(2, 0)
            turned(1, 1)
            normal(3, 1)
            with dve.Fori(1, NT // 8 - 1) as h:
                turned(h * 2, 0)
                normal(h * 2 + 2, 0)
                scores(h * 2 - 2, 0)
                turned(h * 2 + 1, 1)
                normal(h * 2 + 3, 1)
                scores(h * 2 - 1, 1)
            turned(NT // 4 - 2, 0)
            scores(NT // 4 - 4, 0)
            turned(NT // 4 - 1, 1)
            scores(NT // 4 - 3, 1)
            scores(NT // 4 - 2, 0)
            scores(NT // 4 - 1, 1)
            dve.wait_ge(q["gate"], NT // 4)
            chain(dve.tensor_scalar(rstd[:, :], rstd[:, :], 1.0, None, ALU.add))
            chain(dve.tensor_scalar(em[:, :], cst[:, C_IOTA:C_IOTA + NE], float(-NE), None, ALU.add))
            pick_first_max(dve, chain, oh, top, aff, em[:, :], t3, t1, NE)
            dve.engine_nop().then_inc(q["exp1"], 1)
            assign_slots(dve, chain, r, (oh,), [slot[:, :]], NE,
                         bank[6][:, 0:NT * NE].rearrange("p (t e) -> p t e", e=NE), bank[7][:, 0:NT * NE].rearrange("p (t e) -> p t e", e=NE),
                         q["mask"], q["rank"])
            dve.engine_nop().then_inc(q["slot"], 1)
            dve.wait_ge(q["exp2"], 1)
            chain(dve.tensor_scalar(alpha, alpha, 1.0, None, ALU.add))
            chain(dve.memset(side[:, :, 2:], 0.0))
            chain(dve.reciprocal(side[:, :, 0], alpha))
            dve.wait_ge(q["iota"], 3)
            chain(dve.tensor_copy(side[:, :, 1], number[:, :]))
            for t in range(NT):
                if t >= 4:
                    dve.wait_ge(sct[t % 4], 16 * (t // 4))
                row = slot_row[t % 4]
                dve.tensor_scalar(row[:, IN:IN + D], xres[:, t, :], rs2[:, t:t + 1], nm2[:, t:t + 1], ALU.mult, ALU.add)
                dve.tensor_scalar(row[:, BASE:BASE + D], xres[:, t, :], rstd[:, t:t + 1], nmr[:, t:t + 1], ALU.mult, ALU.add)
                dve.tensor_copy(row[:, GATE:], side[:, t, :]).then_inc(q["row"], 1)
                if t == 4:
                    assign_tiles(dve, chain, r, etile[:, :], NE, NTL1, cst)
                    dve.engine_nop().then_inc(q["slot"], 1)
            dve.wait_ge(w_in[1], 16 * 7)

            def rectified(h, v, e):
                n, u = h * 4 + v, v % 2
                dve.wait_ge(q["hh"], n * PIECES + PIECES // 2)
                for f in range(FB // 2):
                    dve.tensor_scalar(hT[u][:, f, :], bank[4 * u][:, f * P:(f + 1) * P], flat2(b1[:, bass.ds(e, 1), f:f + 1]), 0.0,
                                      ALU.add, ALU.max).then_inc(q["ht1"], 1)

            def results(h, v, e):
                n, u, row = h * 4 + v, v % 2, slot_row[v]
                dve.wait_ge(x_in[v], h * 16 + 16)
                dve.scalar_tensor_tensor(where[:, v, :], row[:, TOKEN:TOKEN + 1], 0.0, spare[:, bass.ds(n, 1)],
                                         ALU.is_equal, ALU.mult).then_inc(q["where"], 1)
                dve.wait_ge(q["yp"], n + 1)
                dve.tensor_tensor(row[:, IN:IN + D], bank[4 * u + RES][:, 0:D], flat2(b2[:, bass.ds(e, 1), :]), ALU.add).then_inc(q["yb"], 1)
                dve.wait_ge(q["where"], 3 * n + 1)
                dve.scalar_tensor_tensor(where[:, v, :], row[:, TOKEN:TOKEN + 1], -1.0, where[:, v, :],
                                         ALU.add, ALU.add).then_inc(q["where"], 1)
                dve.wait_ge(q["where"], 3 * n + 2)
                dve.tensor_copy(row_out[:, v:v + 1], where[:, v, :]).then_inc(q["where"], 1)
                dve.wait_ge(q["yb"], n + 1)
                dve.scalar_tensor_tensor(row[:, BASE:BASE + D], row[:, IN:IN + D], row[:, GATE:GATE + 1], row[:, BASE:BASE + D],
                                         ALU.mult, ALU.add).then_inc(q["yo"], 1)

            def tile(h, v, e_before):
                e = expert(dve, h * 4 + v)
                rectified(h, v, e)
                results(*before(h, v), e_before)
                return e

            e = expert(dve, 0)
            rectified(0, 0, e)
            for v in range(1, 4):
                e = tile(0, v, e)
            with dve.Fori(1, ROUNDS) as h:
                e = expert(dve, h * 4 - 1)
                for v in range(4):
                    e = tile(h, v, e)
            results(ROUNDS - 1, 3, expert(dve, NTL1 - 1))


def lay_out(inputs):
    w = {n: np.asarray(v) for n, v in inputs.items()}

    def blocks(m):
        return m.reshape(-1, P, m.shape[-1]).transpose(1, 0, 2)

    we = np.concatenate([w["L0_ffn_We1"], w["L0_ffn_We3"]], axis=2)
    return {
        "gate_w": blocks(w["L0_ffn_gate_w"].T),
        "ws1": blocks(w["L0_ffn_ws1"]), "ws3": blocks(w["L0_ffn_ws3"]), "ws2": blocks(w["L0_ffn_ws2"]),
        "bs13": np.stack([w["L0_ffn_bs1"], w["L0_ffn_bs3"]]).reshape(2, KD, P).transpose(2, 0, 1),
        "w13": we.reshape(E0, KD, P, 2 * I0).transpose(2, 1, 0, 3),
        "w2": w["L0_ffn_We2"].transpose(1, 0, 2),
        "wsim": w["L1_xattn_w_sim"].reshape(3, KD, P).transpose(2, 0, 1),
        "b_sim": w["L1_xattn_b_sim"].reshape(1, 1),
        "wqv": w["L1_xattn_W_qv"].reshape(4, KD, P, D).transpose(2, 0, 1, 3),
        "cw": blocks(w["L1_ffn_centroids"].T),
        "l1_w1": w["L1_ffn_w1"].reshape(E1, F1, KD, P).transpose(3, 2, 0, 1),
        "l1_w2": w["L1_ffn_w2"].reshape(E1, D, FB, P).transpose(3, 2, 0, 1),
        "b1": w["L1_ffn_b1"].reshape(E1, FB, P).transpose(2, 0, 1),
        "lgb": np.concatenate([w["L1_ffn_ln_g"].reshape(E1, KD, P), w["L1_ffn_ln_b"].reshape(E1, KD, P)], axis=1).transpose(2, 0, 1),
        "b13": np.stack([w["L0_ffn_be1"], w["L0_ffn_be3"]]).transpose(2, 1, 0),
    }


_INS = ["x", "ctx_1024", "L0_ffn_gate_b", "L0_ffn_bs2", "L0_ffn_be2", "L1_xattn_b_qv", "L1_ffn_b2"]


def kernel(**inputs):
    import concourse.bacc as bacc
    from concourse.bass_utils import run_bass_kernel_spmd

    nc = bacc.Bacc("TRN2", target_bir_lowering=False, num_devices=1)
    arrays, a = {}, {}

    def give(name, arr):
        arr = np.ascontiguousarray(arr)
        arrays[f"in_{name}"] = arr
        a[name] = nc.dram_tensor(f"in_{name}", arr.shape, mybir.dt.from_np(arr.dtype), kind="ExternalInput").ap()

    for name in _INS:
        give(name, inputs[name])
    for name, arr in lay_out(inputs).items():
        give(name, arr)
    give("cst", constants())
    give("zeros", np.zeros((P, 1), np.float32))
    out = nc.dram_tensor("out_0", (TOK + NTL1 * P, D), F32, kind="ExternalOutput").ap()
    program(nc, a, out)
    r = run_bass_kernel_spmd(nc, [arrays], core_ids=[0])
    return r.results[0]["out_0"][:TOK].reshape(B, S, D)
```
